# Optimizing a Trainium2 kernel written in Bass

```python
import numpy as np
import jax
import jax.numpy as jnp

def _softmax(x, axis=-1):
    return jax.nn.softmax(x, axis=axis)

def _gelu(x):
    return jax.nn.gelu(x, approximate=True)

def _silu(x):
    return jax.nn.silu(x)

def _sigmoid(x):
    return jax.nn.sigmoid(x)

def _layernorm(x, axis=-1, eps=1e-05):
    m = jnp.mean(x, axis=axis, keepdims=True)
    v = jnp.var(x, axis=axis, keepdims=True)
    return (x - m) / jnp.sqrt(v + eps)

def _scatter_add(tgt, idx, src, axis=0):
    return tgt.at[idx].add(src)

def _segment_sum(src, seg, n):
    return jax.ops.segment_sum(src, seg, n)
kernel_name = 'mk_gnn_ffn_d2_gnn_r8_8859c8'

def setup_inputs(seed: int=0):
    np.random.seed(seed)
    _w = jnp.asarray

    def _rec_inputs():
        import jax
        import jax.numpy as jnp
        _gk = jax.random.key(seed)
        x = -0.0003713 + 1 * jax.random.normal(jax.random.fold_in(_gk, 1), (6250, 256), jnp.float32)
        src = jax.random.randint(jax.random.fold_in(_gk, 2), (100000,), 0, 6250, jnp.int32)
        dst = jax.random.randint(jax.random.fold_in(_gk, 3), (100000,), 0, 6250, jnp.int32)
        _o = jnp.argsort(dst, stable=True)
        src = src[_o]
        dst = dst[_o]
        return (x, src, dst)
    x, src, dst = _rec_inputs()

    def _L0_gnn_setup():
        import jax, jax.numpy as jnp
        import numpy as np
        N_NODES = 6250
        EPS = 1e-12
        key = jax.random.key(seed)
        k1, k2, k3 = jax.random.split(key, 3)
        d_in, d_out, n_edges = (256, 256, 100000)
        input_matrix = jax.random.normal(k1, (N_NODES, d_in), dtype=jnp.float32)
        adjacency_coo_matrix = jax.random.randint(k2, (2, n_edges), 0, N_NODES, dtype=jnp.int64)
        W = jax.random.normal(k3, (2 * d_in, d_out), dtype=jnp.float32) * (1.0 / np.sqrt(2 * d_in))
        b = jnp.zeros((d_out,), dtype=jnp.float32)
        return {'input_matrix': input_matrix, 'adjacency_coo_matrix': adjacency_coo_matrix, 'W': W, 'b': b}
    _L0_gnn_all = _L0_gnn_setup()
    _L0_gnn_in = {k: v for k, v in _L0_gnn_all.items() if k in ('W', 'b')}
    del _L0_gnn_all

    def _L0_ffn_setup():
        import jax, jax.numpy as jnp
        import numpy as np
        B, S, D, H, E, K = (8, 1024, 256, 1024, 8, 2)
        key = jax.random.key(seed)
        ks = jax.random.split(key, 7)
        s_in = 1.0 / np.sqrt(D)
        s_hid = 1.0 / np.sqrt(H)
        return {'x': jax.random.normal(ks[0], (B, S, D), dtype=jnp.float32), 'Wg': jax.random.uniform(ks[1], (E, D), jnp.float32, -s_in, s_in), 'bg': jax.random.uniform(ks[2], (E,), jnp.float32, -s_in, s_in), 'W1': jax.random.uniform(ks[3], (E, H, D), jnp.float32, -s_in, s_in), 'b1': jax.random.uniform(ks[4], (E, H), jnp.float32, -s_in, s_in), 'W2': jax.random.uniform(ks[5], (E, D, H), jnp.float32, -s_hid, s_hid), 'b2': jax.random.uniform(ks[6], (E, D), jnp.float32, -s_hid, s_hid)}
    _L0_ffn_all = _L0_ffn_setup()
    _L0_ffn_in = {k: v for k, v in _L0_ffn_all.items() if k in ('Wg', 'bg', 'W1', 'b1', 'W2', 'b2')}
    del _L0_ffn_all

    def _L1_gnn_setup():
        import jax, jax.numpy as jnp
        import numpy as np
        N = 6250
        E = 100000
        IN_C = 256
        HEADS = 8
        OUT_C = 32
        key = jax.random.key(seed)
        k1, k2, k3, k4, k5 = jax.random.split(key, 5)
        x = jax.random.normal(k1, (N, IN_C), dtype=jnp.float32)
        edge_index = jax.random.randint(k2, (2, E), 0, N, dtype=jnp.int64)
        lim_W = float(np.sqrt(6.0 / (IN_C + HEADS * OUT_C)))
        lim_a = float(np.sqrt(6.0 / (HEADS + OUT_C)))
        W = jax.random.uniform(k3, (IN_C, HEADS * OUT_C), minval=-lim_W, maxval=lim_W, dtype=jnp.float32)
        a_src = jax.random.uniform(k4, (HEADS, OUT_C), minval=-lim_a, maxval=lim_a, dtype=jnp.float32)
        a_dst = jax.random.uniform(k5, (HEADS, OUT_C), minval=-lim_a, maxval=lim_a, dtype=jnp.float32)
        return {'x': x, 'edge_index': edge_index, 'W': W, 'a_src': a_src, 'a_dst': a_dst}
    _L1_gnn_all = _L1_gnn_setup()
    _L1_gnn_in = {k: v for k, v in _L1_gnn_all.items() if k in ('W', 'a_src', 'a_dst')}
    del _L1_gnn_all

    def _L1_ffn_setup():
        import jax, jax.numpy as jnp
        import numpy as np
        B, A = (512, 8)
        IN, OUT = (256, 256)
        SH1, SH2 = (256, 128)
        EH1, EH2 = (128, 64)
        E, TOPK = (4, 2)

        def _shared_mlp(x, W1, b1, W2, b2, W3, b3):
            h = jax.nn.relu(x @ W1 + b1)
            h = jax.nn.relu(h @ W2 + b2)
            return h @ W3 + b3

        def _experts_mlp(x, eW1, eb1, eW2, eb2, eW3, eb3):
            h = jax.nn.relu(jnp.einsum('baf,efh->ebah', x, eW1) + eb1[:, None, None, :])
            h = jax.nn.relu(jnp.einsum('ebah,ehg->ebag', h, eW2) + eb2[:, None, None, :])
            o = jnp.einsum('ebag,ego->ebao', h, eW3) + eb3[:, None, None, :]
            return jnp.moveaxis(o, 0, -1)
        key = jax.random.key(seed)
        ks = jax.random.split(key, 16)
        s = 0.05
        return {'x': jax.random.normal(ks[0], (B, A, IN), jnp.float32), 'sW1': jax.random.normal(ks[1], (IN, SH1), jnp.float32) * s, 'sb1': jnp.zeros((SH1,), jnp.float32), 'sW2': jax.random.normal(ks[2], (SH1, SH2), jnp.float32) * s, 'sb2': jnp.zeros((SH2,), jnp.float32), 'sW3': jax.random.normal(ks[3], (SH2, OUT), jnp.float32) * s, 'sb3': jnp.zeros((OUT,), jnp.float32), 'eW1': jax.random.normal(ks[4], (E, IN, EH1), jnp.float32) * s, 'eb1': jnp.zeros((E, EH1), jnp.float32), 'eW2': jax.random.normal(ks[5], (E, EH1, EH2), jnp.float32) * s, 'eb2': jnp.zeros((E, EH2), jnp.float32), 'eW3': jax.random.normal(ks[6], (E, EH2, OUT), jnp.float32) * s, 'eb3': jnp.zeros((E, OUT), jnp.float32), 'gW': jax.random.normal(ks[7], (IN, E), jnp.float32) * s, 'gb': jnp.zeros((E,), jnp.float32)}
    _L1_ffn_all = _L1_ffn_setup()
    _L1_ffn_in = {k: v for k, v in _L1_ffn_all.items() if k in ('sW1', 'sb1', 'sW2', 'sb2', 'sW3', 'sb3', 'eW1', 'eb1', 'eW2', 'eb2', 'eW3', 'eb3', 'gW', 'gb')}
    del _L1_ffn_all
    return {'x': x, 'src': src, 'dst': dst, 'L0_gnn_W': _L0_gnn_in['W'], 'L0_gnn_b': _L0_gnn_in['b'], 'L0_ffn_Wg': _L0_ffn_in['Wg'], 'L0_ffn_bg': _L0_ffn_in['bg'], 'L0_ffn_W1': _L0_ffn_in['W1'], 'L0_ffn_b1': _L0_ffn_in['b1'], 'L0_ffn_W2': _L0_ffn_in['W2'], 'L0_ffn_b2': _L0_ffn_in['b2'], 'L1_gnn_W': _L1_gnn_in['W'], 'L1_gnn_a_src': _L1_gnn_in['a_src'], 'L1_gnn_a_dst': _L1_gnn_in['a_dst'], 'L1_ffn_sW1': _L1_ffn_in['sW1'], 'L1_ffn_sb1': _L1_ffn_in['sb1'], 'L1_ffn_sW2': _L1_ffn_in['sW2'], 'L1_ffn_sb2': _L1_ffn_in['sb2'], 'L1_ffn_sW3': _L1_ffn_in['sW3'], 'L1_ffn_sb3': _L1_ffn_in['sb3'], 'L1_ffn_eW1': _L1_ffn_in['eW1'], 'L1_ffn_eb1': _L1_ffn_in['eb1'], 'L1_ffn_eW2': _L1_ffn_in['eW2'], 'L1_ffn_eb2': _L1_ffn_in['eb2'], 'L1_ffn_eW3': _L1_ffn_in['eW3'], 'L1_ffn_eb3': _L1_ffn_in['eb3'], 'L1_ffn_gW': _L1_ffn_in['gW'], 'L1_ffn_gb': _L1_ffn_in['gb']}

def reference(x, src, dst, L0_gnn_W, L0_gnn_b, L0_ffn_Wg, L0_ffn_bg, L0_ffn_W1, L0_ffn_b1, L0_ffn_W2, L0_ffn_b2, L1_gnn_W, L1_gnn_a_src, L1_gnn_a_dst, L1_ffn_sW1, L1_ffn_sb1, L1_ffn_sW2, L1_ffn_sb2, L1_ffn_sW3, L1_ffn_sb3, L1_ffn_eW1, L1_ffn_eb1, L1_ffn_eW2, L1_ffn_eb2, L1_ffn_eW3, L1_ffn_eb3, L1_ffn_gW, L1_ffn_gb):
    import jax
    import jax.numpy as jnp

    def _L0_gnn_ref(input_matrix, adjacency_coo_matrix, W, b):
        import jax, jax.numpy as jnp
        import numpy as np
        N_NODES = 6250
        EPS = 1e-12
        src = adjacency_coo_matrix[0]
        dst = adjacency_coo_matrix[1]
        neigh_sum = jax.ops.segment_sum(input_matrix[src], dst, num_segments=N_NODES)
        deg = jax.ops.segment_sum(jnp.ones_like(dst, dtype=input_matrix.dtype), dst, num_segments=N_NODES)
        neigh_mean = neigh_sum / jnp.maximum(deg, 1.0)[:, None]
        h = jnp.concatenate([input_matrix, neigh_mean], axis=-1)
        out = jax.nn.relu(h @ W + b)
        norm = jnp.maximum(jnp.linalg.norm(out, axis=-1, keepdims=True), EPS)
        return out / norm

    def _L0_ffn_ref(x, Wg, bg, W1, b1, W2, b2):
        import jax, jax.numpy as jnp
        import numpy as np
        B, S, D, H, E, K = (8, 1024, 256, 1024, 8, 2)
        gate_scores = jnp.einsum('bsd,ed->bse', x, Wg) + bg
        topk_scores, topk_idx = jax.lax.top_k(gate_scores, K)
        topk_probs = jax.nn.softmax(topk_scores, axis=-1)
        combine = jnp.sum(topk_probs[..., None] * jax.nn.one_hot(topk_idx, E, dtype=x.dtype), axis=-2)
        out = jnp.zeros_like(x)
        for e in range(E):
            h = jax.nn.relu(jnp.einsum('bsd,hd->bsh', x, W1[e]) + b1[e])
            y = jnp.einsum('bsh,dh->bsd', h, W2[e]) + b2[e]
            out = out + combine[..., e:e + 1] * y
        return out

    def _L1_gnn_ref(x, edge_index, W, a_src, a_dst):
        import jax, jax.numpy as jnp
        import numpy as np
        N = 6250
        E = 100000
        IN_C = 256
        HEADS = 8
        OUT_C = 32
        n = x.shape[0]
        H, D = a_src.shape
        x_proj = (x @ W).reshape(n, H, D)
        alpha_src = jnp.einsum('nhd,hd->nh', x_proj, a_src)
        alpha_dst = jnp.einsum('nhd,hd->nh', x_proj, a_dst)
        row, col = (edge_index[0], edge_index[1])
        e = alpha_src[row] + alpha_dst[col]
        m = jax.ops.segment_max(e, col, num_segments=n)
        m = jnp.where(jnp.isfinite(m), m, 0.0)
        e_exp = jnp.exp(e - m[col])
        s = jax.ops.segment_sum(e_exp, col, num_segments=n)
        att = e_exp / (s[col] + 1e-16)
        out = jax.ops.segment_sum(att[:, :, None] * x_proj[row], col, num_segments=n)
        return out.reshape(n, H * D)

    def _L1_ffn_ref(x, sW1, sb1, sW2, sb2, sW3, sb3, eW1, eb1, eW2, eb2, eW3, eb3, gW, gb):
        import jax, jax.numpy as jnp
        import numpy as np
        B, A = (512, 8)
        IN, OUT = (256, 256)
        SH1, SH2 = (256, 128)
        EH1, EH2 = (128, 64)
        E, TOPK = (4, 2)

        def _shared_mlp(x, W1, b1, W2, b2, W3, b3):
            h = jax.nn.relu(x @ W1 + b1)
            h = jax.nn.relu(h @ W2 + b2)
            return h @ W3 + b3

        def _experts_mlp(x, eW1, eb1, eW2, eb2, eW3, eb3):
            h = jax.nn.relu(jnp.einsum('baf,efh->ebah', x, eW1) + eb1[:, None, None, :])
            h = jax.nn.relu(jnp.einsum('ebah,ehg->ebag', h, eW2) + eb2[:, None, None, :])
            o = jnp.einsum('ebag,ego->ebao', h, eW3) + eb3[:, None, None, :]
            return jnp.moveaxis(o, 0, -1)
        all_out = _experts_mlp(x, eW1, eb1, eW2, eb2, eW3, eb3)
        shared = _shared_mlp(x, sW1, sb1, sW2, sb2, sW3, sb3)
        gates = jax.nn.softmax(x @ gW + gb, axis=-1)
        topv, topi = jax.lax.top_k(gates, TOPK)
        topw = jax.nn.softmax(topv, axis=-1)
        sel = jnp.take_along_axis(all_out, topi[:, :, None, :], axis=-1)
        gated = jnp.sum(sel * topw[:, :, None, :], axis=-1)
        return shared + gated
    edge_index = jnp.stack([src, dst])
    x = x + _L0_gnn_ref(_layernorm(x, axis=-1), edge_index, L0_gnn_W, L0_gnn_b)
    x = x + _L0_ffn_ref(_layernorm(x, axis=-1)[None], L0_ffn_Wg, L0_ffn_bg, L0_ffn_W1, L0_ffn_b1, L0_ffn_W2, L0_ffn_b2)[0]
    x = x + _L1_gnn_ref(_layernorm(x, axis=-1), edge_index, L1_gnn_W, L1_gnn_a_src, L1_gnn_a_dst)
    x = x + _L1_ffn_ref(_layernorm(x, axis=-1)[None], L1_ffn_sW1, L1_ffn_sb1, L1_ffn_sW2, L1_ffn_sb2, L1_ffn_sW3, L1_ffn_sb3, L1_ffn_eW1, L1_ffn_eb1, L1_ffn_eW2, L1_ffn_eb2, L1_ffn_eW3, L1_ffn_eb3, L1_ffn_gW, L1_ffn_gb)[0]
    return x

_drawn_inputs = setup_inputs


def setup_inputs(seed=0):
    import zlib

    import numpy as np

    out = dict(_drawn_inputs(seed))
    spreads = {'L0_gnn_b': (0.0, 0.443),
     'L1_ffn_sb1': (0.0, 0.423),
     'L1_ffn_sb2': (0.0, 0.1),
     'L1_ffn_sb3': (0.0, 0.1),
     'L1_ffn_eb1': (0.0, 0.8),
     'L1_ffn_eb2': (0.0, 0.496),
     'L1_ffn_eb3': (0.0, 0.1),
     'L1_ffn_gb': (0.0, 0.428)}
    factors = {'L0_ffn_b1': 4.714, 'L0_ffn_b2': 3.712, 'L1_gnn_a_dst': 8.0}
    for name, (base, spread) in spreads.items():
        noise = np.random.default_rng([zlib.crc32(name.encode()), seed]).standard_normal(out[name].shape)
        drawn = base * np.exp(spread * noise) if base else spread * noise
        out[name] = jnp.asarray(drawn.astype(out[name].dtype))
    for name, factor in factors.items():
        out[name] = (out[name] * factor).astype(out[name].dtype)
    return out
```

```python
from contextlib import ExitStack

import concourse.bass as bass
from concourse import mybir

P = 128
ALU = mybir.AluOpType
ACT = mybir.ActivationFunctionType
AX_X = mybir.AxisListType.X
F32 = mybir.dt.float32
I32 = mybir.dt.int32

LN_EPS = 1e-5
NORM_EPS = 1e-12
BIG = 1e30
STOP = 99


class Sizes:

    def __init__(self, n_nodes, d, n_edges, n_exp, hid, heads):
        self.N, self.D, self.E = n_nodes, d, n_edges
        self.NT = -(-n_nodes // P)
        self.NPAD = self.NT * P
        self.KD = d // P
        self.Q = 4
        self.SE = self.Q * P
        self.NS = -(-n_edges // self.SE)
        self.RG = -(-self.NS * self.Q // P)
        self.EPAD = (self.RG * P + 1) * P
        self.R = 8
        self.ITEMS = self.NS + self.NT - 1
        self.TABW = self.ITEMS + 4
        self.BS = 4
        self.NB = self.NS // self.BS
        self.NE, self.HID = n_exp, hid
        self.KH = hid // P
        self.HEADS = heads
        self.TOK = 256
        self.ET = (2 * self.NPAD + n_exp * (self.TOK - 1)) // self.TOK
        self.NEVER = 8191
        assert self.ITEMS % 2 == 0 and self.NS % self.BS == 0 and self.R == 2 * self.BS and self.NEVER >= self.NPAD


class Local:

    def __init__(self, eng, sem):
        self.eng, self.sem, self.n = eng, sem, 0

    def tick(self, ins):
        ins.then_inc(self.sem, 1)
        self.n += 1

    def settle(self):
        self.eng.wait_ge(self.sem, self.n)

    def link(self, ins):
        self.tick(ins)
        self.settle()

    def restart(self):
        if self.n:
            self.settle()
            self.eng.sem_clear(self.sem)
            self.n = 0


def build(nc, stop, z, a, out):
    N, D, NT, KD, Q, NS, R = z.N, z.D, z.NT, z.KD, z.Q, z.NS, z.R
    FULL = N // P
    REST = N - FULL * P
    HEADS, HC = z.HEADS, z.D // z.HEADS
    GW = D + 2 * HEADS + 2

    def scratch(name, shape, dt):
        return nc.dram_tensor(name, shape, dt).ap()

    src_sorted = scratch("src_sorted", (z.EPAD,), I32)
    dst_sorted = scratch("dst_sorted", (z.EPAD,), I32)
    h0_rows = scratch("h0_rows", (z.NPAD, D), F32)
    xd_rows = scratch("xd_rows", (z.ET * z.TOK, D), F32)
    yd_rows = scratch("yd_rows", (z.ET * z.TOK, D), F32)
    g_rows = scratch("g_rows", (z.NPAD, D + HEADS), F32)

    spent = []

    def clear_spent():
        assert sorted(spent) == list(range(min(spent), max(spent) + 1))
        with nc.Block() as block:
            @block.sync
            def _(sp):
                sp.sem_clear(range(min(spent), max(spent) + 1))
        spent.clear()

    top = ExitStack()

    def make(ctx):
        def sb(name, shape, dt=F32):
            return ctx.enter_context(nc.sbuf_tensor(name, shape, dt))

        def ps(name, shape, dt=F32):
            return ctx.enter_context(nc.psum_tensor(name, shape, dt))

        def sem(name):
            one = ctx.enter_context(nc.semaphore(name))
            spent.append(one.num)
            return one

        return sb, ps, sem

    with top:
        sb, _, sem = make(top)
        s_gath_l0 = [sem(f"s_gath_l0_{k}") for k in range(R)]
        s_gath_l1 = [sem(f"s_gath_l1_{k}") for k in range(R)]
        s_sent = [sem(f"s_sent{k}") for k in range(7)]
        s_got = [sem(f"s_got{k}") for k in range(7)]
        spent.clear()
        X = sb("X", [P, NT, D])
        ACC = sb("ACC", [P, NT, GW])
        ident = sb("ident", [P, P])
        ones = sb("ones", [P, P])
        iota_n = sb("iota_n", [P, P])
        srcT = sb("srcT", [P, z.RG * P], I32)
        dstT = sb("dstT", [P, z.RG * P])
        lastT = sb("lastT", [P, z.RG * P])
        tab = sb("tab", [1, z.TABW, 2], I32)
        free_at = sb("free_at", [1, NS], I32)
        tile_base = sb("tile_base", [P, z.TABW])
        pair_end = sb("pair_end", [1, z.NB + 1], I32)

        stats = sb("stats", [P, NT, 6])
        mean = sb("mean", [P, NT])
        rstd = sb("rstd", [P, NT])
        lnt = sb("lnt", [P, 3, NT])

        def ln_moments(loc, s_var):
            me, vo = stats[:, :, 1], stats[:, :, 5]
            mo, ve = stats[:, :, 4], stats[:, :, 2]
            loc.tick(nc.vector.tensor_tensor(lnt[:, 0], me, mo, ALU.add))
            loc.tick(nc.vector.tensor_tensor(lnt[:, 1], me, mo, ALU.subtract))
            loc.link(nc.vector.tensor_tensor(lnt[:, 2], ve, vo, ALU.add))
            loc.tick(nc.vector.tensor_scalar(mean[:], lnt[:, 0], 0.5, None, ALU.mult))
            loc.link(nc.vector.scalar_tensor_tensor(out=lnt[:, 1], in0=lnt[:, 1], scalar=0.25, in1=lnt[:, 1],
                                                    op0=ALU.mult, op1=ALU.mult))
            loc.link(nc.vector.scalar_tensor_tensor(out=lnt[:, 1], in0=lnt[:, 2], scalar=1.0 / D, in1=lnt[:, 1],
                                                    op0=ALU.mult, op1=ALU.add))
            loc.tick(nc.vector.tensor_scalar(lnt[:, 0], lnt[:, 1], LN_EPS, None, ALU.add))
            loc.settle()
            nc.vector.sem_inc(s_var, 1)

        def ln_root(act, s_var, s_root):
            act.wait_ge(s_var, 1)
            nc.scalar.activation(lnt[:, 2], lnt[:, 0], ACT.Sqrt).then_inc(s_root, 1)

        def ln_rstd(loc, s_root):
            loc.eng.wait_ge(s_root, 1)
            loc.link(nc.vector.reciprocal(rstd[:], lnt[:, 2]))

        def ln_apply(out_ap, in_ap, t):
            return nc.vector.tensor_scalar(out_ap, in_ap, mean[:, t], rstd[:, t], ALU.subtract, ALU.mult)

        with ExitStack() as ctx:
            sb, ps, sem = make(ctx)
            pads = sb("pads", [16, 2, (z.EPAD - z.E) // 16], I32)
            rows_i = sb("rows_i", [P, 3, z.RG, P], I32)
            rows_f = sb("rows_f", [P, 3, z.RG, P])
            q_last_i = sb("q_last_i", [P, 1], I32)
            q_last = sb("q_last", [P, 1])
            thr = sb("thr", [P, 1])
            wi = sb("wi", [P, z.TABW])
            cmp1 = sb("cmp1", [P, NS])
            cmpw = sb("cmpw", [P, z.TABW])
            cmps = sb("cmps", [P, NS])
            cmpb = sb("cmpb", [P, z.NB + 1])
            e_end = sb("e_end", [P, 1])
            w_start = sb("w_start", [P, 1])
            tmp1 = sb("tmp1", [P, z.TABW])
            pT = [ps(f"pT{i}", [P, 4 * P]) for i in range(2)]
            pD = ps("pD", [P, 512])
            pJ = ps("pJ", [P, 512])
            pF = ps("pF", [P, 512])
            pB = ps("pB", [P, 512])
            s_x = sem("s_x")
            s_pads = sem("s_pads")
            s_lists = sem("s_lists")
            s_rows = sem("s_rows")
            s_const = sem("s_const")
            s_rowsf = sem("s_rowsf")
            s_turned = sem("s_turned")
            s_copied = sem("s_copied")
            s_d1 = sem("s_d1")
            s_cmp = sem("s_cmp")
            s_tabs = sem("s_tabs")
            s_h0 = sem("s_h0")
            s_h0st = sem("s_h0st")
            s_stat = sem("s_stat")
            s_var = sem("s_var")
            s_root = sem("s_root")
            s_dve = sem("s_dve")
            s_pool = sem("s_pool")
            NTURN = 3 * z.RG
            with nc.Block() as block:
                @block.sync
                def _(sp):
                    sp.dma_start(src_sorted[0:z.E].rearrange("(a b) -> a b", a=16),
                                 a["src"].rearrange("(a b) -> a b", a=16)).then_inc(s_lists, 16)
                    sp.dma_start(dst_sorted[0:z.E].rearrange("(a b) -> a b", a=16),
                                 a["dst"].rearrange("(a b) -> a b", a=16)).then_inc(s_lists, 16)
                    sp.dma_start(X[:, 0:FULL, :], a["x"][0:FULL * P, :].rearrange("(t p) d -> p t d", p=P))\
                        .then_inc(s_x, 16)
                    sp.wait_ge(s_const, 1)
                    sp.dma_start(X[0:REST, FULL, :], a["x"][FULL * P:N, :]).then_inc(s_x, 16)
                    sp.wait_ge(s_pads, 2)
                    sp.dma_start(src_sorted[z.E:z.EPAD].rearrange("(a b) -> a b", a=16), pads[:, 0, :])\
                        .then_inc(s_lists, 16)
                    sp.dma_start(dst_sorted[z.E:z.EPAD].rearrange("(a b) -> a b", a=16), pads[:, 1, :])\
                        .then_inc(s_lists, 16)
                    sp.wait_ge(s_lists, 64)
                    L = z.RG * P * P
                    for n, (lst, off) in enumerate(((src_sorted, 0), (dst_sorted, 0), (dst_sorted, 1))):
                        sp.dma_start(rows_i[:, n, :, :],
                                     lst[off:off + L].rearrange("(g p e) -> p g e", p=P, e=P))\
                            .then_inc(s_rows, 16)
                    sp.wait_ge(s_h0, NT)
                    sp.dma_start(h0_rows.rearrange("(t p) d -> p t d", p=P), ACC[:, :, 0:D])\
                        .then_inc(s_h0st, 16)
                    sp.wait_ge(s_h0st, 16)

                @block.gpsimd
                def _(pool):
                    loc = Local(pool, s_pool)
                    nc.gpsimd.memset(X[:, FULL, :], 0.0).then_inc(s_const, 1)
                    nc.gpsimd.memset(pads[:, 0, :], 0).then_inc(s_pads, 1)
                    nc.gpsimd.memset(pads[:, 1, :], z.NEVER).then_inc(s_pads, 1)
                    loc.link(nc.gpsimd.memset(ident[:], 0.0))
                    nc.gpsimd.affine_select(out=ident[:], in_=ident[:], compare_op=ALU.not_equal, fill=1.0,
                                            base=0, pattern=[[-1, P]], channel_multiplier=1)\
                        .then_inc(s_const, 1)
                    nc.gpsimd.memset(ones[:], 1.0).then_inc(s_const, 1)
                    nc.gpsimd.iota(iota_n[:], pattern=[[1, P]], base=0, channel_multiplier=0,
                                   allow_small_or_imprecise_dtypes=True).then_inc(s_const, 1)
                    nc.gpsimd.iota(wi[:], pattern=[[1, z.TABW]], base=0, channel_multiplier=0,
                                   allow_small_or_imprecise_dtypes=True).then_inc(s_const, 1)
                    nc.gpsimd.iota(thr[:], pattern=[[1, 1]], base=P, channel_multiplier=P,
                                   allow_small_or_imprecise_dtypes=True).then_inc(s_const, 1)
                    nc.gpsimd.iota(q_last_i[:], pattern=[[1, 1]], base=0, channel_multiplier=1)\
                        .then_inc(s_const, 1)

                @block.scalar
                def _(act):
                    ln_root(act, s_var, s_root)

                @block.vector
                def _(dve):
                    loc = Local(dve, s_dve)
                    dve.wait_ge(s_const, 7)
                    loc.link(nc.vector.tensor_single_scalar(q_last_i[:], q_last_i[:], Q - 1, op=ALU.bitwise_and))
                    loc.tick(nc.vector.tensor_single_scalar(q_last[:], q_last_i[:], Q - 1, op=ALU.is_equal))
                    dve.wait_ge(s_rows, 48)
                    loc.link(nc.vector.tensor_copy(rows_f[:], rows_i[:]))
                    loc.link(nc.vector.tensor_tensor(rows_f[:, 2], rows_f[:, 1], rows_f[:, 2], ALU.not_equal))
                    nc.vector.tensor_scalar(rows_f[:, 2, :, P - 1:P], rows_f[:, 2, :, P - 1:P], q_last[:, 0:1],
                                            None, ALU.max).then_inc(s_rowsf, 1)
                    for t in range(NTURN):
                        n, g = divmod(t, z.RG)
                        dve.wait_ge(s_turned, t + 1)
                        dst = (srcT, dstT, lastT)[n]
                        nc.vector.tensor_copy(dst[:, g * P:(g + 1) * P], pT[t % 2][:, 0:P]).then_inc(s_copied, 1)
                    dve.wait_ge(s_d1, 1)
                    J = NT - 1
                    loc.link(nc.vector.tensor_scalar(cmp1[0:J, 0:NS - 1], pD[0:J, 0:NS - 1], thr[0:J, 0:1], None,
                                                     ALU.is_lt))
                    loc.link(nc.vector.tensor_reduce(e_end[0:J], cmp1[0:J, 0:NS - 1], AX_X, ALU.add))
                    loc.link(nc.vector.scalar_tensor_tensor(out=w_start[0:J], in0=thr[0:J], scalar=1.0 / P,
                                                            in1=e_end[0:J], op0=ALU.mult, op1=ALU.add))
                    nc.vector.tensor_scalar(cmpw[0:J], wi[0:J], w_start[0:J, 0:1], None, ALU.is_ge)\
                        .then_inc(s_cmp, 1)
                    nc.vector.tensor_scalar(cmps[0:J], wi[0:J, 0:NS], float(1 - R), e_end[0:J, 0:1], ALU.add,
                                            ALU.is_gt).then_inc(s_cmp, 1)
                    nc.vector.tensor_scalar(cmpb[0:J], wi[0:J, 0:z.NB + 1], float(z.BS), e_end[0:J, 0:1], ALU.mult,
                                            ALU.is_gt).then_inc(s_cmp, 1)
                    dve.wait_ge(s_tabs, 1)
                    loc.tick(nc.vector.tensor_tensor(tab[0:1, :, 0], wi[0:1], pJ[0:1, 0:z.TABW], ALU.subtract))
                    loc.tick(nc.vector.tensor_copy(tab[0:1, :, 1], pJ[0:1, 0:z.TABW]))
                    loc.tick(nc.vector.tensor_scalar(tile_base[:], pJ[:, 0:z.TABW], float(P), None, ALU.mult))
                    loc.link(nc.vector.tensor_scalar(tmp1[0:1, 0:NS], wi[0:1, 0:NS], float(1 - R), 0.0, ALU.add,
                                                     ALU.max))
                    loc.link(nc.vector.scalar_tensor_tensor(out=free_at[:], in0=tmp1[0:1, 0:NS], scalar=2.0,
                                                            in1=pF[0:1, 0:NS], op0=ALU.add, op1=ALU.add))
                    loc.link(nc.vector.scalar_tensor_tensor(out=pair_end[:], in0=wi[0:1, 0:z.NB + 1], scalar=float(z.BS),
                                                            in1=pB[0:1, 0:z.NB + 1], op0=ALU.mult, op1=ALU.add))
                    loc.link(nc.vector.tensor_single_scalar(pair_end[:], pair_end[:], 1, op=ALU.arith_shift_right))
                    dve.wait_ge(s_x, 32)
                    loc.restart()
                    with dve.Fori(0, NT) as t:
                        nc.vector.bn_stats(stats[:, bass.ds(t, 1), :], X[:, bass.ds(t, 1), :]).then_inc(s_stat, 1)
                    dve.wait_ge(s_stat, NT)
                    ln_moments(loc, s_var)
                    ln_rstd(loc, s_root)
                    with dve.Fori(0, NT) as t:
                        ln_apply(ACC[:, bass.ds(t, 1), 0:D], X[:, bass.ds(t, 1), :], bass.ds(t, 1)).then_inc(s_h0, 1)

                @block.tensor
                def _(pe):
                    pe.wait_ge(s_const, 3)
                    pe.wait_ge(s_rowsf, 1)
                    for t in range(NTURN):
                        n, g = divmod(t, z.RG)
                        if t >= 2:
                            pe.wait_ge(s_copied, t - 1)
                        nc.tensor.transpose(pT[t % 2][:, 0:P], rows_f[:, n, g, :], ident[:]).then_inc(s_turned, 1)
                    pe.wait_ge(s_copied, NTURN)
                    J = NT - 1
                    nc.tensor.matmul(pD[0:J, 0:NS - 1], ones[0:1, 0:J], dstT[0:1, Q:Q * NS:Q], start=True, stop=True)\
                        .then_inc(s_d1, 1)
                    pe.wait_ge(s_cmp, 3)
                    nc.tensor.matmul(pJ[:, 0:z.TABW], ones[0:J, :], cmpw[0:J, :], start=True, stop=True)
                    nc.tensor.matmul(pB[:, 0:z.NB + 1], ones[0:J, :], cmpb[0:J, :], start=True, stop=True)
                    nc.tensor.matmul(pF[:, 0:NS], ones[0:J, :], cmps[0:J, :], start=True, stop=True)\
                        .then_inc(s_tabs, 1)

        def gather_supers(pool, rows, G, width, slot_idx, s_gath, s_item, s_pool_idx, s_seen):
            def one(s, k, n):
                need = pool.value_load(free_at[0:1, bass.ds(s, 1)], min_val=2, max_val=z.ITEMS + 2)
                pool.wait_ge(s_item, need)
                pool.sem_inc(s_seen, 1)
                nc.gpsimd.tensor_copy(slot_idx[:, k * Q:(k + 1) * Q], srcT[:, bass.ds(s * Q, Q)])\
                    .then_inc(s_pool_idx[k], 1)
                pool.wait_ge(s_pool_idx[k], 1)
                pool.sem_clear(s_pool_idx[k])
                for q in range(Q):
                    pool.indirect_dma_start(
                        out=G[:, k * Q + q, 0:width], out_offset=None, in_=rows,
                        in_offset=bass.IndirectOffsetOnAxis(ap=slot_idx[:, k * Q + q:k * Q + q + 1], axis=0),
                    ).then_inc(s_gath[k], 16)
            rounds = NS // R
            with pool.Fori(0, rounds) as i:
                for k in range(R):
                    one(i * R + k, k, i)
            for s in range(rounds * R, NS):
                one(s, s % R, rounds)

        def load_item(eng, w, what):
            hi = (NS + 3, NT - 1)[what]
            return eng.value_load(tab[0:1, bass.ds(w, 1), what], min_val=0, max_val=hi)

        def one_hots(dve, O, w, k):
            s = load_item(dve, w, 0)
            base = tile_base[:, bass.ds(w, 1)]
            return nc.vector.scalar_tensor_tensor(
                out=O[:, k], in0=iota_n[:].unsqueeze(1).to_broadcast([P, Q, P]), scalar=base,
                in1=dstT[:, bass.ds(s * Q, Q)].unsqueeze(2).to_broadcast([P, Q, P]), op0=ALU.add, op1=ALU.is_equal)

        with ExitStack() as ctx:
            sb, ps, sem = make(ctx)
            G = sb("G0", [P, R * Q, D + 1])
            O = sb("O0", [P, 2, Q, P])
            slot_idx = sb("slot_idx0", [P, R * Q], I32)
            pS = [ps(f"pS{i}", [P, 512]) for i in range(2)]
            s_gath = s_gath_l0
            s_pool_idx = [sem(f"s_pidx{k}") for k in range(R)]
            s_landed = sem("s_landed")
            s_item = sem("s_item")
            s_oh = sem("s_oh")
            s_merged = sem("s_merged")
            s_ready = sem("s_ready")
            s_seen = sem("s_seen")
            s_dve = sem("s_dve0")
            W = D + 1
            with nc.Block() as block:
                @block.gpsimd
                def _(pool):
                    pool.wait_ge(s_ready, 1)
                    gather_supers(pool, h0_rows, G, D, slot_idx, s_gath, s_item, s_pool_idx, s_seen)

                @block.sync
                def _(sp):
                    rounds = NS // R
                    with sp.Fori(0, rounds) as i:
                        for k in range(R):
                            sp.wait_ge(s_gath[k], i * (16 * Q) + 16 * Q)
                            sp.sem_inc(s_landed, 1)
                    for s in range(rounds * R, NS):
                        sp.wait_ge(s_gath[s % R], 16 * Q * (rounds + 1))
                        sp.sem_inc(s_landed, 1)

                @block.tensor
                def _(pe):
                    with pe.Fori(0, z.ITEMS // 2) as i:
                        for k in range(2):
                            w = i * 2 + k
                            s = load_item(pe, w, 0)
                            pe.wait_ge(s_landed, s + 1)
                            pe.wait_ge(s_merged, w + 1)
                            pe.wait_ge(s_oh, w + 1)
                            for q in range(Q):
                                mm = nc.tensor.matmul(pS[k][:, 0:W], O[:, k, q, :],
                                                      G[:, bass.ds((s % R) * Q + q, 1), :].rearrange("p a d -> p (a d)"),
                                                      start=(q == 0), stop=(q == Q - 1))
                            mm.then_inc(s_item, 1)

                @block.vector
                def _(dve):
                    loc = Local(dve, s_dve)
                    loc.tick(nc.vector.memset(ACC[:], 0.0))
                    loc.link(nc.vector.memset(G[:, :, D:D + 1], 1.0))
                    dve.sem_inc(s_ready, 1)
                    dve.sem_inc(s_item, 2)
                    dve.sem_inc(s_merged, 2)
                    one_hots(dve, O, 0, 0).then_inc(s_oh, 1)
                    loc.restart()
                    with dve.Fori(0, z.ITEMS // 2) as i:
                        for k in range(2):
                            w = i * 2 + k
                            dve.wait_ge(s_item, w + 2)
                            one_hots(dve, O, w + 1, 1 - k).then_inc(s_oh, 1)
                            j = load_item(dve, w, 1)
                            dve.wait_ge(s_item, w + 3)
                            dve.wait_ge(s_merged, w + 2)
                            nc.vector.tensor_tensor(ACC[:, bass.ds(j, 1), 0:W], ACC[:, bass.ds(j, 1), 0:W],
                                                    pS[k][:, 0:W].unsqueeze(1), ALU.add).then_inc(s_merged, 1)
        def dump(view):
            with ExitStack() as ctx:
                sb, ps, sem = make(ctx)
                s_out = sem("s_outdbg")
                with nc.Block() as block:
                    @block.sync
                    def _(sp):
                        sp.dma_start(out[0:FULL * P, :].rearrange("(t p) d -> p t d", p=P), view[:, 0:FULL, 0:D]).then_inc(s_out, 16)
                        sp.dma_start(out[FULL * P:N, :], view[0:REST, FULL, 0:D]).then_inc(s_out, 16)
                        sp.wait_ge(s_out, 32)

        if stop == 2:
            return dump(ACC)

        def top_two(loc, scores, rest, mx, eq, km, sel, prio, n):
            cur = scores
            for c in range(2):
                wide = lambda v: v.unsqueeze(2).to_broadcast([P, NT, n])
                loc.link(nc.vector.tensor_reduce(mx[:, c], cur[:], AX_X, ALU.max))
                loc.link(nc.vector.tensor_tensor(eq[:], cur[:], wide(mx[:, c]), ALU.is_equal))
                loc.link(nc.vector.tensor_tensor(eq[:], eq[:], prio[:].unsqueeze(1).to_broadcast([P, NT, n]), ALU.mult))
                loc.link(nc.vector.tensor_reduce(km[:], eq[:], AX_X, ALU.max))
                loc.link(nc.vector.tensor_tensor(sel[:, c], eq[:], wide(km[:]), ALU.is_equal))
                if c == 0:
                    loc.link(nc.vector.scalar_tensor_tensor(out=rest[:], in0=sel[:, 0], scalar=-BIG, in1=scores[:],
                                                            op0=ALU.mult, op1=ALU.add))
                    cur = rest

        def each_tile(eng, body):
            with eng.Fori(0, NT // 2) as i:
                for k in range(2):
                    body(i * 2 + k, k)
            if NT % 2:
                body(NT - 1, 0)

        clear_spent()
        NE, KH = z.NE, z.KH
        route = ExitStack()
        with route:
            sb, ps, sem = make(route)
            probs = sb("probs", [P, 2, NT])
            pos_f = sb("pos_f", [P, NT, 2])
            pos = sb("pos", [P, NT, 2], I32)
            eid = sb("eid", [1, z.ET], I32)
            with ExitStack() as ctx:
                sb, ps, sem = make(ctx)
                W0 = sb("W0", [P, 2 * KD, D])
                b0 = sb("b0", [1, D])
                Wg = sb("Wg", [P, KD, NE])
                bg = sb("bg", [1, NE])
                IN = sb("IN", [P, 2, 2 * D])
                HT = sb("HT", [P, 2, 2 * D])
                rdeg = sb("rdeg", [P, NT])
                ssq = sb("ssq", [P, NT])
                rnorm = sb("rnorm", [P, NT])
                sq = sb("sq", [P, 2, D])
                SC = sb("SC", [P, NT, NE])
                pT = [ps(f"pT3{i}", [P, 512]) for i in range(2)]
                pO = [ps(f"pO3{i}", [P, 512]) for i in range(2)]
                pG = [ps(f"pG3{i}", [P, 512]) for i in range(2)]
                s_w = sem("s_w3")
                s_in = sem("s_in3")
                s_mean = sem("s_mean3")
                s_turned = sem("s_turned3")
                s_ht = sem("s_ht3")
                s_out3 = sem("s_out3")
                s_relu = sem("s_relu3")
                s_held = sem("s_held3")
                s_rdeg = sem("s_rdeg3")
                s_root0 = sem("s_root03")
                s_x1 = sem("s_x13")
                s_stat = sem("s_stat3")
                s_var = sem("s_var3")
                s_root = sem("s_root3")
                s_in1 = sem("s_in13")
                s_turned1 = sem("s_turned13")
                s_ht1 = sem("s_ht13")
                s_sc = sem("s_sc3")
                s_sccp = sem("s_sccp3")
                s_kept = sem("s_kept3")
                s_dve = sem("s_dve3")
                s_act = sem("s_act3")
                with nc.Block() as block:
                    @block.sync
                    def _(sp):
                        sp.dma_start(W0[:], a["W0"].rearrange("(k p) n -> p k n", p=P)).then_inc(s_w, 16)
                        sp.dma_start(b0[:], a["b0"].unsqueeze(0)).then_inc(s_w, 16)
                        sp.dma_start(Wg[:], a["WgT"].rearrange("(k p) n -> p k n", p=P)).then_inc(s_w, 16)
                        sp.dma_start(bg[:], a["bg"].unsqueeze(0)).then_inc(s_w, 16)

                    @block.vector
                    def _(dve):
                        loc = Local(dve, s_dve)
                        loc.link(nc.vector.tensor_scalar(rdeg[:], ACC[:, :, D], 1.0, None, ALU.max))
                        loc.link(nc.vector.reciprocal(rdeg[:], rdeg[:]))
                        dve.sem_inc(s_rdeg, 1)
                        dve.sem_inc(s_turned, 2)
                        loc.restart()

                        def tile_in(t, k):
                            dve.wait_ge(s_turned, t + 1)
                            ln_apply(IN[:, k, 0:D].unsqueeze(1), X[:, bass.ds(t, 1), :], bass.ds(t, 1))\
                                .then_inc(s_in, 1)
                        each_tile(dve, tile_in)
                        dve.wait_ge(s_root0, 1)
                        loc.link(nc.vector.tensor_scalar(rnorm[:], rnorm[:], NORM_EPS, None, ALU.max))
                        loc.link(nc.vector.reciprocal(rnorm[:], rnorm[:]))
                        loc.restart()
                        with dve.Fori(0, NT) as t:
                            one = bass.ds(t, 1)
                            nc.vector.scalar_tensor_tensor(
                                out=X[:, one, :], in0=ACC[:, one, 0:D], scalar=rnorm[:, one], in1=X[:, one, :],
                                op0=ALU.mult, op1=ALU.add).then_inc(s_x1, 1)
                        dve.wait_ge(s_x1, NT)
                        with dve.Fori(0, NT) as t:
                            nc.vector.bn_stats(stats[:, bass.ds(t, 1), :], X[:, bass.ds(t, 1), :]).then_inc(s_stat, 1)
                        dve.wait_ge(s_stat, NT)
                        ln_moments(loc, s_var)
                        ln_rstd(loc, s_root)
                        dve.sem_inc(s_turned1, 2)
                        dve.sem_inc(s_kept, 2)

                        def tile_h1(t, k):
                            dve.wait_ge(s_turned1, t + 1)
                            dve.wait_ge(s_kept, t + 1)
                            ln_apply(IN[:, k, 0:D].unsqueeze(1), X[:, bass.ds(t, 1), :], bass.ds(t, 1))\
                                .then_inc(s_in1, 1)
                        each_tile(dve, tile_h1)

                    @block.scalar
                    def _(act):
                        loc = Local(act, s_act)
                        act.wait_ge(s_rdeg, 1)
                        act.sem_inc(s_ht, 2)
                        act.sem_inc(s_relu, 2)
                        act.sem_inc(s_mean, 2)

                        def mean_in(t, k):
                            act.wait_ge(s_turned, t + 1)
                            act.sem_inc(s_held, 1)
                            nc.scalar.activation(IN[:, k, D:2 * D].unsqueeze(1), ACC[:, bass.ds(t, 1), 0:D], ACT.Copy,
                                                 scale=rdeg[:, bass.ds(t, 1)]).then_inc(s_mean, 1)

                        def relu_out(t, k):
                            act.wait_ge(s_turned, t + 3)
                            act.wait_ge(s_out3, t + 1)
                            nc.scalar.activation(HT[:, k, :], pT[k][:], ACT.Copy).then_inc(s_ht, 1)
                            act.wait_ge(s_out3, t + 3)
                            act.sem_inc(s_held, 1)
                            nc.scalar.activation(ACC[:, bass.ds(t, 1), 0:D], pO[k][:, 0:D].unsqueeze(1), ACT.Relu)\
                                .then_inc(s_relu, 1)
                            act.wait_ge(s_relu, t + 3)
                            act.sem_inc(s_held, 1)
                            loc.link(nc.scalar.activation(sq[:, k].unsqueeze(1), ACC[:, bass.ds(t, 1), 0:D],
                                                          ACT.Square, accum_out=ssq[:, bass.ds(t, 1)]))
                            loc.restart()

                        act.sem_inc(s_out3, 2)
                        loc.restart()

                        def both(t, k):
                            mean_in(t, k)
                            relu_out(t, k)
                        each_tile(act, both)
                        nc.scalar.activation(rnorm[:], ssq[:], ACT.Sqrt).then_inc(s_root0, 1)
                        ln_root(act, s_var, s_root)
                        act.sem_inc(s_sc, 2)

                        def scores(t, k):
                            act.wait_ge(s_turned1, t + 3)
                            act.wait_ge(s_sc, t + 1)
                            nc.scalar.activation(HT[:, k, 0:D], pT[k][:, 0:D], ACT.Copy).then_inc(s_ht1, 1)
                            act.sem_inc(s_held, 1)
                            nc.scalar.activation(ACC[:, bass.ds(t, 1), 0:D], IN[:, k, 0:D].unsqueeze(1), ACT.Copy)\
                                .then_inc(s_kept, 1)
                            act.wait_ge(s_sc, t + 3)
                            act.sem_inc(s_held, 1)
                            nc.scalar.activation(SC[:, bass.ds(t, 1), :], pG[k][:, 0:NE].unsqueeze(1), ACT.Copy)\
                                .then_inc(s_sccp, 1)
                        each_tile(act, scores)

                    @block.tensor
                    def _(pe):
                        pe.wait_ge(s_w, 64)
                        pe.wait_ge(s_rdeg, 1)

                        def dense(t, k):
                            pe.wait_ge(s_in, t + 1)
                            pe.wait_ge(s_mean, t + 3)
                            for m in range(2 * KD):
                                tr = nc.tensor.transpose(pT[k][:, m * P:(m + 1) * P], IN[:, k, m * P:(m + 1) * P], ident[:])
                            tr.then_inc(s_turned, 1)
                            pe.wait_ge(s_ht, t + 3)
                            pe.wait_ge(s_relu, t + 1)
                            for m in range(2 * KD):
                                nc.tensor.matmul(pO[k][:, 0:D], HT[:, k, m * P:(m + 1) * P], W0[:, m, :],
                                                 start=(m == 0), stop=False)
                            nc.tensor.matmul(pO[k][:, 0:D], ones[0:1, :], b0[:], start=False, stop=True)\
                                .then_inc(s_out3, 1)
                        each_tile(pe, dense)
                        pe.sem_inc(s_ht1, 2)
                        pe.sem_inc(s_sccp, 2)

                        def gate(t, k):
                            pe.wait_ge(s_in1, t + 1)
                            pe.wait_ge(s_ht1, t + 1)
                            for m in range(KD):
                                tr = nc.tensor.transpose(pT[k][:, m * P:(m + 1) * P], IN[:, k, m * P:(m + 1) * P], ident[:])
                            tr.then_inc(s_turned1, 1)
                            pe.wait_ge(s_ht1, t + 3)
                            pe.wait_ge(s_sccp, t + 1)
                            for m in range(KD):
                                nc.tensor.matmul(pG[k][:, 0:NE], HT[:, k, m * P:(m + 1) * P], Wg[:, m, :],
                                                 start=(m == 0), stop=False)
                            nc.tensor.matmul(pG[k][:, 0:NE], ones[0:1, :], bg[:], start=False, stop=True)\
                                .then_inc(s_sc, 1)
                        each_tile(pe, gate)

                with ExitStack() as ctx4:
                    sb, ps, sem = make(ctx4)
                    prio = sb("prio", [P, NE])
                    mx = sb("mx", [P, 2, NT])
                    eq = sb("eq", [P, NT, NE])
                    km = sb("km", [P, NT])
                    sel = sb("sel", [P, 2, NT, NE])
                    SC2 = sb("SC2", [P, NT, NE])
                    both = sb("both", [P, NT, NE])
                    below = sb("below", [P, P])
                    tot = sb("tot", [P, NE, NT])
                    inc = sb("inc", [P, NE, NT])
                    cnt = sb("cnt", [P, NE])
                    cnt_i = sb("cnt_i", [P, NE], I32)
                    tiles = sb("tiles", [P, NE])
                    tend = sb("tend", [P, NE])
                    tbeg = sb("tbeg", [P, NE])
                    row = sb("row", [P, NT, NE])
                    ui = sb("ui", [1, z.ET])
                    ucmp = sb("ucmp", [1, z.ET, NE])
                    dm = sb("dm", [P, NT])
                    zero_rows = sb("zero_rows", [P, 2048])
                    pA = ps("pA4", [P, 512])
                    pB = ps("pB4", [P, 512])
                    s_const = sem("s_const4")
                    s_zero = sem("s_zero4")
                    s_zst = sem("s_zst4")
                    s_both = sem("s_both4")
                    s_cum = sem("s_cum4")
                    s_dm = sem("s_dm4")
                    s_ex = sem("s_ex4")
                    s_dve = sem("s_dve4")
                    s_pool = sem("s_pool4")
                    with nc.Block() as block:
                        @block.gpsimd
                        def _(pool):
                            loc = Local(pool, s_pool)
                            nc.gpsimd.memset(zero_rows[:], 0.0).then_inc(s_zero, 1)
                            nc.gpsimd.iota(prio[:], pattern=[[-1, NE]], base=NE, channel_multiplier=0,
                                           allow_small_or_imprecise_dtypes=True).then_inc(s_const, 1)
                            nc.gpsimd.iota(ui[:], pattern=[[1, z.ET]], base=0, channel_multiplier=0,
                                           allow_small_or_imprecise_dtypes=True).then_inc(s_const, 1)
                            nc.gpsimd.affine_select(out=below[:], in_=ones[:], compare_op=ALU.is_ge, fill=0.0,
                                                    base=-1, pattern=[[1, P]], channel_multiplier=-1)\
                                .then_inc(s_const, 1)

                        @block.sync
                        def _(sp):
                            sp.wait_ge(s_zero, 1)
                            flat = xd_rows.rearrange("(c p r) d -> c p (r d)", p=P, r=2048 // D)
                            chunks = z.ET * z.TOK * D // (P * 2048)
                            for c in range(chunks):
                                sp.dma_start(flat[c], zero_rows[:]).then_inc(s_zst, 16)
                            sp.wait_ge(s_zst, 16 * chunks)

                        @block.scalar
                        def _(act):
                            act.wait_ge(s_dm, 1)
                            nc.scalar.activation(dm[:], dm[:], ACT.Exp).then_inc(s_ex, 1)

                        @block.tensor
                        def _(pe):
                            pe.wait_ge(s_const, 3)
                            pe.wait_ge(s_both, 1)
                            flat = both[:].rearrange("p t e -> p (t e)")
                            nc.tensor.matmul(pA[:, 0:NT * NE], below[:], flat, start=True, stop=True)
                            nc.tensor.matmul(pB[:, 0:NT * NE], ones[:], flat, start=True, stop=True).then_inc(s_cum, 1)

                        @block.vector
                        def _(dve):
                            loc = Local(dve, s_dve)
                            over_t = lambda v: v.unsqueeze(1).to_broadcast([P, NT, NE])
                            dve.wait_ge(s_const, 3)
                            top_two(loc, SC, SC2, mx, eq, km, sel, prio, NE)
                            loc.tick(nc.vector.tensor_tensor(both[:], sel[:, 0], sel[:, 1], ALU.add))
                            loc.link(nc.vector.tensor_tensor(dm[:], mx[:, 1], mx[:, 0], ALU.subtract))
                            dve.sem_inc(s_both, 1)
                            dve.sem_inc(s_dm, 1)
                            dve.wait_ge(s_ex, 1)
                            loc.link(nc.vector.tensor_scalar(probs[:, 0], dm[:], 1.0, None, ALU.add))
                            loc.link(nc.vector.reciprocal(probs[:, 0], probs[:, 0]))
                            loc.tick(nc.vector.tensor_tensor(probs[:, 1], dm[:], probs[:, 0], ALU.mult))
                            dve.wait_ge(s_cum, 1)
                            loc.link(nc.vector.tensor_copy(tot[:], pB[:, 0:NT * NE].rearrange("p (t e) -> p e t", e=NE)))
                            for e in range(NE):
                                loc.tick(nc.vector.tensor_tensor_scan(inc[:, e], ones[:, 0:NT], tot[:, e], 0.0,
                                                                      ALU.mult, ALU.add))
                            loc.settle()
                            loc.link(nc.vector.tensor_scalar(cnt[:], inc[:, :, NT - 1], float(z.TOK - 1), None, ALU.add))
                            loc.link(nc.vector.tensor_copy(cnt_i[:], cnt[:]))
                            loc.link(nc.vector.tensor_single_scalar(cnt_i[:], cnt_i[:], z.TOK.bit_length() - 1,
                                                                    op=ALU.arith_shift_right))
                            loc.link(nc.vector.tensor_copy(tiles[:], cnt_i[:]))
                            loc.link(nc.vector.tensor_tensor_scan(tend[:], ones[:, 0:NE], tiles[:], 0.0,
                                                                  ALU.mult, ALU.add))
                            loc.link(nc.vector.tensor_tensor(tbeg[:], tend[:], tiles[:], ALU.subtract))
                            loc.tick(nc.vector.tensor_tensor(ucmp[:], tbeg[0:1].unsqueeze(1).to_broadcast([1, z.ET, NE]),
                                                             ui[:].unsqueeze(2).to_broadcast([1, z.ET, NE]), ALU.is_le))
                            loc.link(nc.vector.tensor_tensor(inc[:], inc[:], tot[:], ALU.subtract))
                            loc.link(nc.vector.tensor_tensor(
                                row[:], inc[:].rearrange("p e t -> p t e"),
                                pA[:, 0:NT * NE].rearrange("p (t e) -> p t e", e=NE), ALU.add))
                            loc.link(nc.vector.scalar_tensor_tensor(out=row[:], in0=over_t(tbeg[:]), scalar=float(z.TOK),
                                                                    in1=row[:], op0=ALU.mult, op1=ALU.add))
                            loc.link(nc.vector.tensor_reduce(ui[:], ucmp[:], AX_X, ALU.add))
                            loc.tick(nc.vector.tensor_scalar(eid[:], ui[:], -1.0, None, ALU.add))
                            for c in range(2):
                                loc.link(nc.vector.tensor_tensor(eq[:], sel[:, c], row[:], ALU.mult))
                                loc.link(nc.vector.tensor_reduce(pos_f[:, :, c], eq[:], AX_X, ALU.add))
                            loc.link(nc.vector.tensor_copy(pos[:], pos_f[:]))

            SLOTS = 7
            assert NT % SLOTS == 0
            with ExitStack() as ctx:
                sb, ps, sem = make(ctx)
                stage = sb("stage", [P, SLOTS, D])
                sidx = sb("sidx", [P, SLOTS, 2], I32)
                s_staged = [sem(f"s_staged{k}") for k in range(SLOTS)]
                s_seen = sem("s_seen5")
                s_held = sem("s_held5")
                with nc.Block() as block:
                    @block.scalar
                    def _(act):
                        def one_round(i, first):
                            for k in range(SLOTS):
                                t = bass.ds(i * SLOTS + k, 1)
                                if not first:
                                    act.wait_ge(s_sent[k], i * 32)
                                    act.sem_inc(s_held, 1)
                                nc.scalar.activation(stage[:, k].unsqueeze(1), ACC[:, t, 0:D], ACT.Copy)\
                                    .then_inc(s_staged[k], 1)
                                nc.scalar.activation(sidx[:, k].unsqueeze(1), pos_f[:, t, :], ACT.Copy)\
                                    .then_inc(s_staged[k], 1)

                        one_round(0, True)
                        with act.Fori(1, NT // SLOTS) as i:
                            one_round(i, False)

                    @block.gpsimd
                    def _(pool):
                        with pool.Fori(0, NT // SLOTS) as i:
                            for k in range(SLOTS):
                                pool.wait_ge(s_staged[k], i * 2 + 2)
                                pool.sem_inc(s_seen, 1)
                                for c in range(2):
                                    pool.indirect_dma_start(
                                        out=xd_rows, in_=stage[:, k, :], in_offset=None,
                                        out_offset=bass.IndirectOffsetOnAxis(ap=sidx[:, k, c:c + 1], axis=0),
                                    ).then_inc(s_sent[k], 16)
                        for k in range(SLOTS):
                            pool.wait_ge(s_sent[k], 32 * (NT // SLOTS))

            clear_spent()
            HALVES = z.TOK // P
            with ExitStack() as ctx:
                sb, ps, sem = make(ctx)
                w1s = sb("w1s", [P, 2, KD, z.HID])
                w2s = sb("w2s", [P, 2, KH, D])
                b1s = sb("b1s", [P, 2, KH])
                b2s = sb("b2s", [1, 2, D])
                XE = sb("XE", [P, 2, HALVES, D])
                XT = sb("XT", [P, 2, KD, z.TOK])
                HE = sb("HE", [P, KH, z.TOK])
                YE = sb("YE", [P, 2, HALVES, D])
                pX = ps("pX6", [P, KD, z.TOK])
                pH = [ps(f"pH6{i}", [P, 512]) for i in range(3)]
                pY = [ps(f"pY6{i}", [P, 512]) for i in range(2)]
                s_load = [sem(f"s_load6{k}") for k in range(2)]
                s_tile = sem("s_tile6")
                s_turned = sem("s_turned6")
                s_xt = sem("s_xt6")
                s_hmm = sem("s_hmm6")
                s_relu = sem("s_relu6")
                s_ymm = sem("s_ymm6")
                s_ycp = sem("s_ycp6")
                s_store = [sem(f"s_store6{k}") for k in range(2)]
                U = z.ET
                assert U % 2 == 0
                with nc.Block() as block:
                    @block.sync
                    def _(sp):
                        with sp.Fori(0, U // 2) as i:
                            for k in range(2):
                                u = i * 2 + k
                                e = sp.value_load(eid[0:1, bass.ds(u, 1)], min_val=0, max_val=NE - 1)
                                sp.wait_ge(s_ymm, u + 1)
                                sp.dma_start(XE[:, k], xd_rows[bass.ds(u * z.TOK, z.TOK), :]
                                             .rearrange("(a p) d -> p a d", p=P)).then_inc(s_load[k], 16)
                                sp.dma_start(w1s[:, k], a["W1"][bass.ds(e, 1)].rearrange("a p (k h) -> p (a k) h", k=KD))\
                                    .then_inc(s_load[k], 16)
                                sp.dma_start(w2s[:, k], a["W2"][bass.ds(e, 1)].rearrange("a p (k d) -> p (a k) d", k=KH))\
                                    .then_inc(s_load[k], 16)
                                sp.dma_start(b1s[:, k], a["b1"][bass.ds(e, 1)].rearrange("a p k -> p (a k)"))\
                                    .then_inc(s_load[k], 16)
                                sp.dma_start(b2s[:, k], a["b2"][bass.ds(e, 1)]).then_inc(s_load[k], 16)

                    @block.tensor
                    def _(pe):
                        pe.sem_inc(s_ymm, 2)
                        pe.sem_inc(s_xt, 1)
                        pe.sem_inc(s_relu, 3)
                        with pe.Fori(0, U // 2) as i:
                            for k in range(2):
                                u = i * 2 + k
                                pe.wait_ge(s_load[k], i * 80 + 80)
                                pe.wait_ge(s_xt, u + 1)
                                for h in range(HALVES):
                                    for m in range(KD):
                                        tr = nc.tensor.transpose(pX[:, m, h * P:(h + 1) * P],
                                                                 XE[:, k, h, m * P:(m + 1) * P], ident[:])
                                tr.then_inc(s_turned, 1)
                                pe.wait_ge(s_xt, u + 2)
                                for b in range(KH):
                                    pe.wait_ge(s_relu, u * KH + b + 1)
                                    for m in range(KD):
                                        mm = nc.tensor.matmul(pH[b % 3][:, 0:z.TOK],
                                                              w1s[:, k, m, b * P:(b + 1) * P], XT[:, k, m, :],
                                                              start=(m == 0), stop=(m == KD - 1))
                                    mm.then_inc(s_hmm, 1)
                                pe.wait_ge(s_ycp, 2 * u + 1)
                                for h in range(HALVES):
                                    for b in range(KH):
                                        if h == 0:
                                            pe.wait_ge(s_relu, u * KH + b + 4)
                                        nc.tensor.matmul(pY[h][:, 0:D], HE[:, b, h * P:(h + 1) * P], w2s[:, k, b, :],
                                                         start=(b == 0), stop=False)
                                    mm = nc.tensor.matmul(pY[h][:, 0:D], ones[0:1, :], b2s[:, k], start=False, stop=True)
                                mm.then_inc(s_ymm, 1)

                    @block.scalar
                    def _(act):
                        act.sem_inc(s_ycp, 2)
                        with act.Fori(0, U // 2) as i:
                            for k in range(2):
                                u = i * 2 + k
                                for b in range(KH):
                                    act.wait_ge(s_hmm, u * KH + b + 1)
                                    if b == 0:
                                        act.wait_ge(s_ymm, u + 2)
                                    nc.scalar.activation(HE[:, b, :], pH[b % 3][:, 0:z.TOK], ACT.Relu,
                                                         bias=b1s[:, k, b:b + 1]).then_inc(s_relu, 1)
                                act.wait_ge(s_ycp, 2 * u + 4)
                                act.dma_start(yd_rows[bass.ds(u * z.TOK, z.TOK), :].rearrange("(a p) d -> p a d", p=P),
                                              YE[:, k]).then_inc(s_store[k], 16)
                        for k in range(2):
                            act.wait_ge(s_store[k], 16 * (U // 2))

                    @block.vector
                    def _(dve):
                        def turn(i, first):
                            for k in range(2):
                                u = i * 2 + k
                                dve.wait_ge(s_turned, u + 1)
                                nc.vector.tensor_copy(XT[:, k], pX[:]).then_inc(s_xt, 1)
                                if not first:
                                    dve.wait_ge(s_store[k], i * 16)
                                dve.wait_ge(s_ymm, u + 3)
                                for h in range(HALVES):
                                    nc.vector.tensor_copy(YE[:, k, h, :], pY[h][:, 0:D]).then_inc(s_ycp, 1)
                        turn(0, True)
                        with dve.Fori(1, U // 2) as i:
                            turn(i, False)

            with ExitStack() as ctx:
                sb, ps, sem = make(ctx)
                Y = sb("Y7", [P, SLOTS, 2, D])
                gidx = sb("gidx", [P, SLOTS, 2], I32)
                s_idx = [sem(f"s_idx7{k}") for k in range(SLOTS)]
                s_added = sem("s_added7")
                s_seen = sem("s_seen7")
                with nc.Block() as block:
                    @block.scalar
                    def _(act):
                        act.sem_inc(s_added, 2 * SLOTS)
                        with act.Fori(0, NT // SLOTS) as i:
                            for k in range(SLOTS):
                                t = bass.ds(i * SLOTS + k, 1)
                                act.wait_ge(s_added, (i * SLOTS + k) * 2 + 2)
                                act.sem_inc(s_seen, 1)
                                nc.scalar.activation(gidx[:, k].unsqueeze(1), pos_f[:, t, :], ACT.Copy)\
                                    .then_inc(s_idx[k], 1)

                    @block.gpsimd
                    def _(pool):
                        with pool.Fori(0, NT // SLOTS) as i:
                            for k in range(SLOTS):
                                pool.wait_ge(s_idx[k], i + 1)
                                pool.sem_inc(s_seen, 1)
                                for c in range(2):
                                    pool.indirect_dma_start(
                                        out=Y[:, k, c, :], out_offset=None, in_=yd_rows,
                                        in_offset=bass.IndirectOffsetOnAxis(ap=gidx[:, k, c:c + 1], axis=0),
                                    ).then_inc(s_got[k], 16)

                    @block.vector
                    def _(dve):
                        with dve.Fori(0, NT // SLOTS) as i:
                            for k in range(SLOTS):
                                t = bass.ds(i * SLOTS + k, 1)
                                dve.wait_ge(s_got[k], i * 32 + 32)
                                for c in range(2):
                                    if c:
                                        dve.wait_ge(s_added, (i * SLOTS + k) * 2 + 2 * SLOTS + 1)
                                    nc.vector.scalar_tensor_tensor(
                                        out=X[:, t, :], in0=Y[:, k, c].unsqueeze(1), scalar=probs[:, c, t],
                                        in1=X[:, t, :], op0=ALU.mult, op1=ALU.add).then_inc(s_added, 1)
        if stop == 7:
            return dump(X)

        clear_spent()
        HW = HC + 1
        GR = HEADS * HW
        late = ExitStack()
        with late:
            sb, ps, sem = make(late)
            ADST = sb("ADST", [P, NT, HEADS])
            with ExitStack() as ctx:
                sb, ps, sem = make(ctx)
                Wrow = sb("Wrow", [P, KD, GR])
                Wd = sb("Wd", [P, KD, HEADS])
                WpT = sb("WpT", [P, KD, D])
                att = sb("att", [P, KD, 2])
                head_of = sb("head_of", [P, KD], I32)
                head_f = sb("head_f", [P, KD])
                hh = sb("hh", [P, HEADS])
                A = sb("A8", [P, KD, 2, HEADS])
                IN = sb("IN8", [P, 2, D])
                HT = sb("HT8", [P, 2, D])
                OUT = sb("OUT8", [P, 2, GR])
                pT = [ps(f"pT8{i}", [P, 512]) for i in range(2)]
                pO = [ps(f"pO8{i}", [P, 512]) for i in range(2)]
                pW = ps("pW8", [P, 512])
                s_w = sem("s_w8")
                s_iota = sem("s_iota8")
                s_A = sem("s_A8")
                s_wmm = sem("s_wmm8")
                s_wcp = sem("s_wcp8")
                s_stat = sem("s_stat8")
                s_var = sem("s_var8")
                s_root = sem("s_root8")
                s_in = sem("s_in8")
                s_turned = sem("s_turned8")
                s_ht = sem("s_ht8")
                s_mm = sem("s_mm8")
                s_cp = sem("s_cp8")
                s_held = sem("s_held8")
                s_store = [sem(f"s_store8{k}") for k in range(2)]
                s_dve = sem("s_dve8")
                with nc.Block() as block:
                    @block.sync
                    def _(sp):
                        sp.dma_start(WpT[:], a["WpT"].rearrange("(k p) n -> p k n", p=P)).then_inc(s_w, 16)
                        sp.dma_start(att[:], a["att"].rearrange("(k p) n -> p k n", p=P)).then_inc(s_w, 16)
                        for m in range(KD):
                            sp.dma_start(Wrow[:, m, :].rearrange("p (h c) -> p h c", c=HW)[:, :, 0:HC],
                                         a["Wp"][m * P:(m + 1) * P, :].rearrange("p (h c) -> p h c", c=HC))\
                                .then_inc(s_w, 16)

                        def store(t, k):
                            sp.wait_ge(s_cp, 2 * t + 6)
                            sp.dma_start(g_rows[bass.ds(t * P, P), :], OUT[:, k]).then_inc(s_store[k], 16)
                        each_tile(sp, store)
                        sp.wait_ge(s_store[0], 16 * ((NT + 1) // 2))
                        sp.wait_ge(s_store[1], 16 * (NT // 2))

                    @block.gpsimd
                    def _(pool):
                        nc.gpsimd.iota(head_of[:], pattern=[[P, KD]], base=0, channel_multiplier=1).then_inc(s_iota, 1)
                        nc.gpsimd.iota(hh[:], pattern=[[1, HEADS]], base=0, channel_multiplier=0,
                                       allow_small_or_imprecise_dtypes=True).then_inc(s_iota, 1)

                    @block.vector
                    def _(dve):
                        loc = Local(dve, s_dve)
                        with dve.Fori(0, NT) as t:
                            nc.vector.bn_stats(stats[:, bass.ds(t, 1), :], X[:, bass.ds(t, 1), :]).then_inc(s_stat, 1)
                        dve.wait_ge(s_iota, 2)
                        loc.link(nc.vector.tensor_single_scalar(head_of[:], head_of[:], HC.bit_length() - 1,
                                                                op=ALU.arith_shift_right))
                        loc.link(nc.vector.tensor_copy(head_f[:], head_of[:]))
                        dve.wait_ge(s_w, 16 * (2 + KD))
                        for m in range(KD):
                            for c in range(2):
                                loc.tick(nc.vector.tensor_scalar(A[:, m, c], hh[:], head_f[:, m:m + 1],
                                                                 att[:, m, c:c + 1], ALU.is_equal, ALU.mult))
                        loc.settle()
                        dve.sem_inc(s_A, 1)
                        dve.wait_ge(s_wmm, 1)
                        pw = pW[:, 0:KD * 2 * HEADS].rearrange("p (k c h) -> p k c h", k=KD, c=2)
                        wr = Wrow[:].rearrange("p k (h c) -> p k h c", c=HW)
                        nc.vector.tensor_copy(wr[:, :, :, HC], pw[:, :, 0, :]).then_inc(s_wcp, 1)
                        nc.vector.tensor_copy(Wd[:], pw[:, :, 1, :]).then_inc(s_wcp, 1)
                        dve.wait_ge(s_stat, NT)
                        ln_moments(loc, s_var)
                        ln_rstd(loc, s_root)
                        dve.sem_inc(s_turned, 2)
                        loc.restart()

                        def tile_in(t, k):
                            dve.wait_ge(s_turned, t + 1)
                            ln_apply(IN[:, k].unsqueeze(1), X[:, bass.ds(t, 1), :], bass.ds(t, 1)).then_inc(s_in, 1)
                        each_tile(dve, tile_in)

                    @block.scalar
                    def _(act):
                        ln_root(act, s_var, s_root)
                        act.sem_inc(s_ht, 2)
                        act.sem_inc(s_cp, 4)
                        act.sem_inc(s_mm, 2)

                        def tile_out(t, k, first=False):
                            act.wait_ge(s_turned, t + 3)
                            act.wait_ge(s_mm, t + 1)
                            nc.scalar.activation(HT[:, k], pT[k][:, 0:D], ACT.Copy).then_inc(s_ht, 1)
                            act.wait_ge(s_mm, t + 3)
                            if not first:
                                act.wait_ge(s_store[k], (t - k) * 8)
                            nc.scalar.activation(OUT[:, k], pO[k][:, 0:GR], ACT.Copy).then_inc(s_cp, 1)
                            act.sem_inc(s_held, 1)
                            nc.scalar.activation(ADST[:, bass.ds(t, 1), :], pO[k][:, GR:GR + HEADS].unsqueeze(1),
                                                 ACT.Copy).then_inc(s_cp, 1)
                        for k in range(2):
                            tile_out(k, k, True)
                        with act.Fori(1, NT // 2) as i:
                            for k in range(2):
                                tile_out(i * 2 + k, k)
                        if NT % 2:
                            tile_out(NT - 1, 0)

                    @block.tensor
                    def _(pe):
                        pe.wait_ge(s_A, 1)
                        for m in range(KD):
                            for j in range(KD):
                                mm = nc.tensor.matmul(pW[:, m * 2 * HEADS:(m + 1) * 2 * HEADS],
                                                      WpT[:, j, m * P:(m + 1) * P],
                                                      A[:, j].rearrange("p c h -> p (c h)"), start=(j == 0), stop=(j == KD - 1))
                        mm.then_inc(s_wmm, 1)
                        pe.wait_ge(s_wcp, 2)

                        def proj(t, k):
                            pe.wait_ge(s_in, t + 1)
                            for m in range(KD):
                                tr = nc.tensor.transpose(pT[k][:, m * P:(m + 1) * P], IN[:, k, m * P:(m + 1) * P], ident[:])
                            tr.then_inc(s_turned, 1)
                            pe.wait_ge(s_ht, t + 3)
                            pe.wait_ge(s_cp, 2 * t + 2)
                            for m in range(KD):
                                nc.tensor.matmul(pO[k][:, 0:GR], HT[:, k, m * P:(m + 1) * P], Wrow[:, m, :],
                                                 start=(m == 0), stop=(m == KD - 1))
                            for m in range(KD):
                                mm = nc.tensor.matmul(pO[k][:, GR:GR + HEADS], HT[:, k, m * P:(m + 1) * P], Wd[:, m, :],
                                                      start=(m == 0), stop=(m == KD - 1))
                            mm.then_inc(s_mm, 1)
                        each_tile(pe, proj)

            BC = z.BS * Q
            BR = z.BS * HEADS
            FAR = 1e28
            with ExitStack() as ctx:
                sb, ps, sem = make(ctx)
                G = sb("G1", [P, R * Q, GW])
                O = sb("O1", [P, 2, Q, P])
                slot_idx = sb("slot_idx1", [P, R * Q], I32)
                MR = sb("MR", [P, NT, HEADS])
                DR = sb("DR", [BR, 2, z.SE], I32)
                DB = sb("DB", [BR, 2, z.SE])
                FL = sb("FL", [BR, z.SE + 1])
                M1 = sb("M1", [BR, z.SE])
                M2 = sb("M2", [BR, z.SE])
                SCO = sb("SCO", [P, Q, z.BS, HEADS])
                EX = sb("EX", [P, Q, z.BS, HEADS])
                gone = sb("gone", [P, 1])
                mi = sb("mi", [P, HEADS])
                mn = sb("mn", [P, HEADS])
                df = sb("df", [P, 2, HEADS])
                fac = sb("fac", [P, 2, HEADS])
                TM = sb("TM", [P, GR])
                pS = [ps(f"pS9{i}", [P, 512]) for i in range(2)]
                pA = ps("pA9", [P, 512])
                pM = ps("pM9", [P, 512])
                s_gath = s_gath_l1
                s_pool_idx = [sem(f"s_pidx9{k}") for k in range(R)]
                s_item = sem("s_item9")
                s_oh = sem("s_oh9")
                s_merged = sem("s_merged9")
                s_seen = sem("s_seen9")
                s_dr = [sem(f"s_dr9{k}") for k in range(2)]
                s_db = sem("s_db9")
                s_fl = sem("s_fl9")
                s_at = sem("s_at9")
                s_sco = sem("s_sco9")
                s_max = sem("s_max9")
                s_mt = sem("s_mt9")
                s_sub = sem("s_sub9")
                s_exp = sem("s_exp9")
                s_prep = sem("s_prep9")
                s_diff = sem("s_diff9")
                s_fac = sem("s_fac9")
                s_dve = sem("s_dve9")
                NR = GR + HEADS + 1

                def batches(eng, body):
                    with eng.Fori(0, z.NB // 2) as i:
                        for k in range(2):
                            body(i * 2 + k, k, i)
                    if z.NB % 2:
                        body(z.NB - 1, 0, z.NB // 2)

                def pairs(eng, b, item):
                    lo = eng.value_load(pair_end[0:1, bass.ds(b, 1)], min_val=0, max_val=z.ITEMS // 2)
                    hi = eng.value_load(pair_end[0:1, bass.ds(b + 1, 1)], min_val=1, max_val=z.ITEMS // 2)
                    with eng.Fori(lo, hi) as i:
                        for k in range(2):
                            item(i * 2 + k, k)

                with nc.Block() as block:
                    @block.gpsimd
                    def _(pool):
                        gather_supers(pool, g_rows, G, GR, slot_idx, s_gath, s_item, s_pool_idx, s_seen)

                    @block.sync
                    def _(sp):
                        def load(b, k, i):
                            if not isinstance(b, int) or b:
                                sp.wait_ge(s_db, b + 1)
                            v = dst_sorted[bass.ds(b * (BC * P), BC * P)].rearrange("(s e) -> s e", s=z.BS)
                            sp.dma_start(DR[:, k], v.unsqueeze(1).to_broadcast([z.BS, HEADS, z.SE]))\
                                .then_inc(s_dr[k], 16)
                        batches(sp, load)

                    @block.tensor
                    def _(pe):
                        def item(w, k):
                            s = load_item(pe, w, 0)
                            pe.wait_ge(s_merged, w + 1)
                            pe.wait_ge(s_oh, w + 1)
                            for q in range(Q):
                                mm = nc.tensor.matmul(pS[k][:, 0:NR], O[:, k, q, :],
                                                      G[:, bass.ds((s % R) * Q + q, 1), 0:NR].rearrange("p a d -> p (a d)"),
                                                      start=(q == 0), stop=(q == Q - 1))
                            mm.then_inc(s_item, 1)

                        def batch(b, k, i):
                            pe.wait_ge(s_sco, b + 1)
                            for q in range(Q):
                                tr = nc.tensor.transpose(pA[0:BR, q * P:(q + 1) * P],
                                                         SCO[:, q].rearrange("p s h -> p (s h)"), ident[:])
                            tr.then_inc(s_at, 1)
                            pe.wait_ge(s_max, b + 1)
                            pe.sem_inc(s_seen, 1)
                            for q in range(Q):
                                tr = nc.tensor.transpose(pM[:, q * BR:(q + 1) * BR], M2[:, q * P:(q + 1) * P],
                                                         ident[0:BR, 0:BR])
                            tr.then_inc(s_mt, 1)
                            pe.wait_ge(s_prep, b + 1)
                            pe.sem_inc(s_seen, 1)
                            pairs(pe, b, item)
                        batches(pe, batch)

                    @block.scalar
                    def _(act):
                        act.sem_inc(s_db, 2)

                        def item(w, k):
                            act.wait_ge(s_diff, w + 1)
                            nc.scalar.activation(fac[:], df[:], ACT.Exp).then_inc(s_fac, 1)

                        def batch(b, k, i):
                            gate = G[:, k * BC:(k + 1) * BC, 0:GR].rearrange("p (s q) (h c) -> p q s h c", q=Q, c=HW)
                            for s in range(z.BS):
                                act.wait_ge(s_gath[k * z.BS + s], i * (16 * Q) + 16 * Q)
                            nc.scalar.activation(SCO[:], gate[:, :, :, :, HC], ACT.Copy).then_inc(s_sco, 1)
                            act.wait_ge(s_dr[k], i * 16 + 16)
                            act.wait_ge(s_fl, b + 1)
                            nc.scalar.activation(DB[:, k], DR[:, k], ACT.Copy, scale=FAR).then_inc(s_db, 1)
                            act.wait_ge(s_sub, b + 1)
                            nc.scalar.activation(gate[:, :, :, :, HC], EX[:], ACT.Exp).then_inc(s_exp, 1)
                            pairs(act, b, item)
                        batches(act, batch)

                    @block.vector
                    def _(dve):
                        loc = Local(dve, s_dve)
                        loc.tick(nc.vector.memset(ACC[:], 0.0))
                        loc.tick(nc.vector.memset(MR[:], -BIG))
                        loc.tick(nc.vector.memset(FL[:, 0:1], -FAR))
                        loc.link(nc.vector.memset(FL[:, z.SE:z.SE + 1], -FAR))
                        dve.sem_inc(s_fl, 1)
                        dve.sem_inc(s_item, 2)
                        dve.sem_inc(s_merged, 2)
                        one_hots(dve, O, 0, 0).then_inc(s_oh, 1)
                        loc.restart()

                        def item(w, k):
                            dve.wait_ge(s_item, w + 2)
                            one_hots(dve, O, w + 1, 1 - k).then_inc(s_oh, 1)
                            j = load_item(dve, w, 1)
                            J = bass.ds(j, 1)
                            S = pS[k]
                            dve.wait_ge(s_item, w + 3)
                            loc.link(nc.vector.tensor_scalar(gone[:], S[:, GR + HEADS:NR], BIG, -BIG, ALU.mult, ALU.add))
                            loc.link(nc.vector.scalar_tensor_tensor(
                                out=mi[:].unsqueeze(1), in0=S[:, GR:GR + HEADS].unsqueeze(1), scalar=gone[:, 0:1],
                                in1=ADST[:, J, :], op0=ALU.add, op1=ALU.add))
                            loc.link(nc.vector.tensor_tensor(mn[:].unsqueeze(1), mi[:].unsqueeze(1), MR[:, J, :], ALU.max))
                            loc.tick(nc.vector.tensor_tensor(df[:, 0:1], MR[:, J, :], mn[:].unsqueeze(1), ALU.subtract))
                            loc.link(nc.vector.tensor_tensor(df[:, 1], mi[:], mn[:], ALU.subtract))
                            dve.sem_inc(s_diff, 1)
                            loc.tick(nc.vector.tensor_scalar(MR[:, J, :], mn[:].unsqueeze(1), 0.0, None, ALU.add))
                            dve.wait_ge(s_fac, w + 1)
                            by = lambda f: fac[:, f].unsqueeze(2).to_broadcast([P, HEADS, HW])
                            acc = ACC[:, J, 0:GR].rearrange("p a (h c) -> p (a h) c", c=HW)
                            loc.tick(nc.vector.tensor_tensor(TM[:].rearrange("p (h c) -> p h c", c=HW),
                                                             S[:, 0:GR].rearrange("p (h c) -> p h c", c=HW), by(1), ALU.mult))
                            loc.link(nc.vector.tensor_tensor(acc, acc, by(0), ALU.mult))
                            loc.link(nc.vector.tensor_tensor(ACC[:, J, 0:GR], ACC[:, J, 0:GR], TM[:].unsqueeze(1), ALU.add))
                            dve.sem_inc(s_merged, 1)
                            loc.restart()

                        def batch(b, k, i):
                            dve.wait_ge(s_db, b + 3)
                            loc.link(nc.vector.tensor_tensor(FL[:, 1:z.SE], DB[:, k, 0:z.SE - 1], DB[:, k, 1:z.SE],
                                                             ALU.subtract))
                            dve.sem_inc(s_fl, 1)
                            dve.wait_ge(s_at, b + 1)
                            loc.link(nc.vector.tensor_tensor_scan(M1[:], FL[:, 0:z.SE], pA[0:BR, :], -BIG, ALU.add, ALU.max))
                            loc.link(nc.vector.tensor_tensor_scan(M2[:, ::-1], FL[:, 1:z.SE + 1][:, ::-1], M1[:, ::-1], -BIG,
                                                                  ALU.add, ALU.max))
                            dve.sem_inc(s_max, 1)
                            dve.wait_ge(s_mt, b + 1)
                            rows = G[:, k * BC:(k + 1) * BC, :]
                            top = rows[:, :, GR:GR + HEADS].rearrange("p (s q) h -> p q s h", q=Q)
                            pm = pM[:, 0:Q * BR].rearrange("p (q s h) -> p q s h", q=Q, h=HEADS)
                            last = lastT[:, bass.ds(b * BC, BC)]
                            loc.link(nc.vector.tensor_tensor(EX[:], SCO[:], pm, ALU.subtract))
                            dve.sem_inc(s_sub, 1)
                            for q in range(Q):
                                lq = last.rearrange("p (s q) -> p q s", q=Q)[:, q]
                                loc.tick(nc.vector.tensor_tensor(top[:, q], pm[:, q],
                                                                 lq.unsqueeze(2).to_broadcast([P, z.BS, HEADS]), ALU.mult))
                            loc.tick(nc.vector.tensor_scalar(rows[:, :, GR + HEADS], last, 0.0, None, ALU.add))
                            dve.wait_ge(s_exp, b + 1)
                            for s in range(z.BS):
                                for q in range(Q):
                                    c = rows[:, s * Q + q, 0:GR].rearrange("p (h c) -> p h c", c=HW)
                                    loc.tick(nc.vector.tensor_tensor(
                                        c[:, :, 0:HC], c[:, :, 0:HC], c[:, :, HC:HW].to_broadcast([P, HEADS, HC]), ALU.mult))
                            loc.settle()
                            dve.sem_inc(s_prep, 1)
                            loc.restart()
                            pairs(dve, b, item)
                        batches(dve, batch)

            FE = a["eb3"].shape[0]
            H1, H2, HS = a["eb1"].shape[0], a["eb2"].shape[0], a["sb1"].shape[1]
            G4 = late.enter_context(nc.sbuf_tensor("G4", [P, NT, FE], F32))
            with ExitStack() as ctx:
                sb, ps, sem = make(ctx)
                gW = sb("gW", [P, KD, FE])
                gb = sb("gb", [1, FE])
                RS = sb("RS", [P, NT, HEADS])
                T1 = sb("T1", [P, 2, D])
                IN = sb("IN10", [P, 2, D])
                HT = sb("HT10", [P, 2, D])
                SC = sb("SC10", [P, NT, FE])
                SC2 = sb("SC210", [P, NT, FE])
                eq = sb("eq10", [P, NT, FE])
                km = sb("km10", [P, NT])
                mx = sb("mx10", [P, 2, NT])
                sel = sb("sel10", [P, 2, NT, FE])
                pr = sb("pr10", [P, 2, NT])
                prio = sb("prio10", [P, FE])
                pT = [ps(f"pT10{i}", [P, 512]) for i in range(2)]
                pG = [ps(f"pG10{i}", [P, 512]) for i in range(2)]
                s_w = sem("s_w10")
                s_const = sem("s_const10")
                s_t1 = sem("s_t110")
                s_x3 = sem("s_x310")
                s_stat = sem("s_stat10")
                s_var = sem("s_var10")
                s_root = sem("s_root10")
                s_in = sem("s_in10")
                s_turned = sem("s_turned10")
                s_ht = sem("s_ht10")
                s_kept = sem("s_kept10")
                s_sc = sem("s_sc10")
                s_sccp = sem("s_sccp10")
                s_held = sem("s_held10")
                s_e = sem("s_e10")
                s_ed = sem("s_ed10")
                s_dve = sem("s_dve10")
                with nc.Block() as block:
                    @block.sync
                    def _(sp):
                        sp.dma_start(gW[:], a["gW"].rearrange("(k p) n -> p k n", p=P)).then_inc(s_w, 16)
                        sp.dma_start(gb[:], a["gb"].unsqueeze(0)).then_inc(s_w, 16)

                    @block.gpsimd
                    def _(pool):
                        nc.gpsimd.iota(prio[:], pattern=[[-1, FE]], base=FE, channel_multiplier=0,
                                       allow_small_or_imprecise_dtypes=True).then_inc(s_const, 1)

                    @block.vector
                    def _(dve):
                        loc = Local(dve, s_dve)
                        sums = ACC[:, :, 0:GR].rearrange("p t (h c) -> p t h c", c=HW)
                        loc.link(nc.vector.tensor_scalar(RS[:], sums[:, :, :, HC], 1e-16, None, ALU.add))
                        loc.link(nc.vector.reciprocal(RS[:], RS[:]))
                        dve.sem_inc(s_x3, 2)
                        loc.restart()

                        def add_tile(t, k):
                            one = bass.ds(t, 1)
                            dve.wait_ge(s_x3, t + 1)
                            acc = ACC[:, one, 0:GR].rearrange("p a (h c) -> p (a h) c", c=HW)[:, :, 0:HC]
                            nc.vector.tensor_tensor(T1[:, k].rearrange("p (h c) -> p h c", c=HC), acc,
                                                    RS[:, one, :].rearrange("p a h -> p (a h)").unsqueeze(2)
                                                    .to_broadcast([P, HEADS, HC]), ALU.mult).then_inc(s_t1, 1)
                            dve.wait_ge(s_t1, t + 1)
                            nc.vector.tensor_tensor(X[:, one, :], X[:, one, :], T1[:, k].unsqueeze(1), ALU.add)\
                                .then_inc(s_x3, 1)
                        each_tile(dve, add_tile)
                        dve.wait_ge(s_x3, NT + 2)
                        with dve.Fori(0, NT) as t:
                            nc.vector.bn_stats(stats[:, bass.ds(t, 1), :], X[:, bass.ds(t, 1), :]).then_inc(s_stat, 1)
                        dve.wait_ge(s_stat, NT)
                        ln_moments(loc, s_var)
                        ln_rstd(loc, s_root)
                        dve.sem_inc(s_turned, 2)
                        loc.restart()

                        def tile_in(t, k):
                            dve.wait_ge(s_turned, t + 1)
                            ln_apply(IN[:, k].unsqueeze(1), X[:, bass.ds(t, 1), :], bass.ds(t, 1)).then_inc(s_in, 1)
                        each_tile(dve, tile_in)
                        wide = lambda v: v.unsqueeze(2).to_broadcast([P, NT, FE])
                        dve.wait_ge(s_sccp, NT + 2)
                        dve.wait_ge(s_const, 1)
                        loc.link(nc.vector.tensor_reduce(km[:], SC[:], AX_X, ALU.max))
                        loc.link(nc.vector.tensor_tensor(SC[:], SC[:], wide(km[:]), ALU.subtract))
                        dve.sem_inc(s_e, 1)
                        dve.wait_ge(s_ed, 1)
                        loc.link(nc.vector.tensor_reduce(km[:], SC[:], AX_X, ALU.add))
                        loc.link(nc.vector.reciprocal(km[:], km[:]))
                        loc.link(nc.vector.tensor_tensor(SC[:], SC[:], wide(km[:]), ALU.mult))
                        top_two(loc, SC, SC2, mx, eq, km, sel, prio, FE)
                        loc.link(nc.vector.tensor_tensor(pr[:, 1], mx[:, 1], mx[:, 0], ALU.subtract))
                        dve.sem_inc(s_e, 1)
                        dve.wait_ge(s_ed, 2)
                        loc.link(nc.vector.tensor_scalar(pr[:, 0], pr[:, 1], 1.0, None, ALU.add))
                        loc.link(nc.vector.reciprocal(pr[:, 0], pr[:, 0]))
                        loc.link(nc.vector.tensor_tensor(pr[:, 1], pr[:, 1], pr[:, 0], ALU.mult))
                        loc.tick(nc.vector.tensor_tensor(G4[:], sel[:, 0], wide(pr[:, 0]), ALU.mult))
                        loc.link(nc.vector.tensor_tensor(eq[:], sel[:, 1], wide(pr[:, 1]), ALU.mult))
                        loc.link(nc.vector.tensor_tensor(G4[:], G4[:], eq[:], ALU.add))

                    @block.scalar
                    def _(act):
                        ln_root(act, s_var, s_root)
                        act.sem_inc(s_ht, 2)
                        act.sem_inc(s_kept, 2)
                        act.sem_inc(s_sc, 2)
                        act.sem_inc(s_sccp, 2)

                        def tile_out(t, k):
                            act.wait_ge(s_turned, t + 3)
                            act.wait_ge(s_sc, t + 1)
                            nc.scalar.activation(HT[:, k], pT[k][:, 0:D], ACT.Copy).then_inc(s_ht, 1)
                            act.sem_inc(s_held, 1)
                            nc.scalar.activation(ACC[:, bass.ds(t, 1), 0:D], pT[k][:, 0:D].unsqueeze(1), ACT.Copy)\
                                .then_inc(s_kept, 1)
                            act.wait_ge(s_sc, t + 3)
                            act.sem_inc(s_held, 1)
                            nc.scalar.activation(SC[:, bass.ds(t, 1), :], pG[k][:, 0:FE].unsqueeze(1), ACT.Copy)\
                                .then_inc(s_sccp, 1)
                        each_tile(act, tile_out)
                        act.wait_ge(s_e, 1)
                        nc.scalar.activation(SC[:], SC[:], ACT.Exp).then_inc(s_ed, 1)
                        act.wait_ge(s_e, 2)
                        nc.scalar.activation(pr[:, 1], pr[:, 1], ACT.Exp).then_inc(s_ed, 1)

                    @block.tensor
                    def _(pe):
                        pe.wait_ge(s_w, 32)
                        pe.wait_ge(s_in, 1)

                        def gate(t, k):
                            pe.wait_ge(s_in, t + 1)
                            pe.wait_ge(s_kept, t + 1)
                            for m in range(KD):
                                tr = nc.tensor.transpose(pT[k][:, m * P:(m + 1) * P], IN[:, k, m * P:(m + 1) * P], ident[:])
                            tr.then_inc(s_turned, 1)
                            pe.wait_ge(s_ht, t + 3)
                            pe.wait_ge(s_sccp, t + 1)
                            for m in range(KD):
                                nc.tensor.matmul(pG[k][:, 0:FE], HT[:, k, m * P:(m + 1) * P], gW[:, m, :],
                                                 start=(m == 0), stop=False)
                            nc.tensor.matmul(pG[k][:, 0:FE], ones[0:1, :], gb[:], start=False, stop=True)\
                                .then_inc(s_sc, 1)
                        each_tile(pe, gate)
            if stop == 10:
                return dump(X)

            with ExitStack() as ctx:
                sb, ps, sem = make(ctx)
                NH, NE1 = HS, FE
                sW1 = sb("sW1", [P, KD, HS * P])
                sW2 = sb("sW2", [P, HS, P])
                sW3 = sb("sW3", [P, D])
                eW1 = sb("eW1", [P, KD, FE * H1])
                eW2 = sb("eW2", [P, FE, H2])
                eW3 = sb("eW3", [H2, FE, D])
                sb1 = sb("sb1", [P, HS])
                sb2 = sb("sb2", [P, 1])
                sb3 = sb("sb3", [1, D])
                eb1 = sb("eb1", [P, FE])
                eb2 = sb("eb2", [H2, FE])
                eb3 = sb("eb3", [1, FE, D])
                S1 = sb("S1", [P, HS, P])
                E1 = sb("E1", [P, FE, P])
                S2 = sb("S2", [P, P])
                E2 = sb("E2", [H2, FE, P])
                pS1 = ps("pS111", [P, HS, P])
                pE1 = ps("pE111", [P, FE, P])
                pS2 = ps("pS211", [P, 512])
                pE2 = ps("pE211", [P, FE, P])
                pSo = ps("pSo11", [P, 512])
                pEo = [ps(f"pEo11{i}", [P, 2, D]) for i in range(2)]
                s_w = sem("s_w11")
                s_l1 = sem("s_l111")
                s_r1 = sem("s_r111")
                s_l2 = sem("s_l211")
                s_r2 = sem("s_r211")
                s_l3 = sem("s_l311")
                s_add = sem("s_add11")
                s_store = sem("s_store11")
                assert H1 == P and FE == 4
                with nc.Block() as block:
                    @block.sync
                    def _(sp):
                        loads = [(sW1[:], a["sW1"].rearrange("(k p) n -> p k n", p=P)),
                                 (sW2[:], a["sW2"].rearrange("(k p) n -> p k n", p=P)), (sW3[:], a["sW3"]),
                                 (eW1[:], a["eW1"].rearrange("(k p) n -> p k n", p=P)),
                                 (eW2[:], a["eW2"].rearrange("p (e n) -> p e n", e=FE)),
                                 (eW3[:], a["eW3"].rearrange("p (e n) -> p e n", e=FE)),
                                 (sb1[:], a["sb1"]), (sb2[:], a["sb2"]), (sb3[:], a["sb3"].unsqueeze(0)),
                                 (eb1[:], a["eb1"]), (eb2[:], a["eb2"]), (eb3[:], a["eb3"].unsqueeze(0))]
                        for o_, i_ in loads:
                            sp.dma_start(o_, i_).then_inc(s_w, 16)
                        with sp.Fori(0, FULL) as t:
                            sp.wait_ge(s_add, (t + 1) * (FE + 1) + 1)
                            sp.dma_start(out[bass.ds(t * P, P), :], X[:, bass.ds(t, 1), :].rearrange("p a d -> p (a d)"))\
                                .then_inc(s_store, 16)
                        sp.wait_ge(s_add, NT * (FE + 1) + 1)
                        sp.dma_start(out[FULL * P:N, :], X[0:REST, FULL, :]).then_inc(s_store, 16)
                        sp.wait_ge(s_store, 16 * NT)

                    @block.tensor
                    def _(pe):
                        pe.wait_ge(s_w, 16 * 12)

                        def tile(t):
                            h = lambda m: ACC[:, bass.ds(t, 1), m * P:(m + 1) * P].rearrange("p a d -> p (a d)")
                            pe.wait_ge(s_r1, t * (HS + FE) + 1)
                            for b in range(HS):
                                for m in range(KD):
                                    mm = nc.tensor.matmul(pS1[:, b, :], sW1[:, m, b * P:(b + 1) * P], h(m),
                                                          start=(m == 0), stop=(m == KD - 1))
                                mm.then_inc(s_l1, 1)
                            for e in range(FE):
                                for m in range(KD):
                                    mm = nc.tensor.matmul(pE1[:, e, :], eW1[:, m, e * P:(e + 1) * P], h(m),
                                                          start=(m == 0), stop=(m == KD - 1))
                                mm.then_inc(s_l1, 1)
                            pe.wait_ge(s_r2, t * (1 + FE) + 1)
                            pe.wait_ge(s_r1, t * (HS + FE) + 1 + HS)
                            for b in range(HS):
                                mm = nc.tensor.matmul(pS2[:, 0:P], sW2[:, b, :], S1[:, b, :],
                                                      start=(b == 0), stop=(b == HS - 1))
                            mm.then_inc(s_l2, 1)
                            for e in range(FE):
                                pe.wait_ge(s_r1, t * (HS + FE) + 1 + HS + e + 1)
                                nc.tensor.matmul(pE2[0:H2, e, :], eW2[:, e, :], E1[:, e, :], start=True, stop=True)\
                                    .then_inc(s_l2, 1)
                            pe.wait_ge(s_add, t * (FE + 1) + 1)
                            pe.wait_ge(s_r2, t * (1 + FE) + 2)
                            nc.tensor.matmul(pSo[:, 0:D], S2[:], sW3[:], start=True, stop=False)
                            nc.tensor.matmul(pSo[:, 0:D], ones[0:1, :], sb3[:], start=False, stop=True).then_inc(s_l3, 1)
                            for e in range(FE):
                                pe.wait_ge(s_r2, t * (1 + FE) + 3 + e)
                                nc.tensor.matmul(pEo[e // 2][:, e % 2, :], E2[:, e, :], eW3[:, e, :], start=True, stop=False)
                                nc.tensor.matmul(pEo[e // 2][:, e % 2, :], ones[0:1, :], eb3[:, e, :], start=False, stop=True)\
                                    .then_inc(s_l3, 1)
                        with pe.Fori(0, NT) as t:
                            tile(t)

                    @block.scalar
                    def _(act):
                        act.sem_inc(s_r1, 1)
                        act.sem_inc(s_r2, 1)
                        act.wait_ge(s_w, 16 * 12)
                        with act.Fori(0, NT) as t:
                            for b in range(HS + FE):
                                if b in (0, HS):
                                    act.wait_ge(s_l1, t * (HS + FE) + (HS if b == 0 else HS + FE))
                                o_, i_, bi = ((S1[:, b], pS1[:, b], sb1[:, b:b + 1]) if b < HS else
                                              (E1[:, b - HS], pE1[:, b - HS], eb1[:, b - HS:b - HS + 1]))
                                nc.scalar.activation(o_, i_, ACT.Relu, bias=bi).then_inc(s_r1, 1)
                            for e in range(-1, FE):
                                if e < 1:
                                    act.wait_ge(s_l2, t * (1 + FE) + (1 if e < 0 else 1 + FE))
                                o_, i_, bi = ((S2[:], pS2[:, 0:P], sb2[:, 0:1]) if e < 0 else
                                              (E2[:, e], pE2[0:H2, e], eb2[:, e:e + 1]))
                                nc.scalar.activation(o_, i_, ACT.Relu, bias=bi).then_inc(s_r2, 1)

                    @block.vector
                    def _(dve):
                        dve.sem_inc(s_add, 1)
                        with dve.Fori(0, NT) as t:
                            one = bass.ds(t, 1)
                            dve.wait_ge(s_l3, t * (FE + 1) + 1)
                            nc.vector.tensor_tensor(X[:, one, :], X[:, one, :], pSo[:, 0:D].unsqueeze(1), ALU.add)\
                                .then_inc(s_add, 1)
                            for e in range(FE):
                                if e % 2 == 0:
                                    dve.wait_ge(s_l3, t * (FE + 1) + 3 + e)
                                dve.wait_ge(s_add, t * (FE + 1) + 2 + e)
                                nc.vector.scalar_tensor_tensor(
                                    out=X[:, one, :], in0=pEo[e // 2][:, e % 2, :].unsqueeze(1), scalar=G4[:, one, e],
                                    in1=X[:, one, :], op0=ALU.mult, op1=ALU.add).then_inc(s_add, 1)


def kernel(**inputs):
    import numpy as _np
    import concourse.bacc as _bacc
    from concourse import mybir as _mybir
    from concourse.bass_utils import run_bass_kernel_spmd as _run

    nc = _bacc.Bacc("TRN2", target_bir_lowering=False, num_devices=1)
    a = {k: _np.asarray(v) for k, v in inputs.items()}
    ne, hid, d = a["L0_ffn_W1"].shape
    heads, hc = a["L1_gnn_a_src"].shape
    z = Sizes(a["x"].shape[0], a["x"].shape[1], a["src"].shape[0], ne, hid, heads)
    t_ = lambda v, *axes: _np.transpose(v, axes)
    blocks = lambda v: t_(v.reshape(ne, -1, P, v.shape[-1]), 0, 2, 1, 3).reshape(ne, P, -1)
    laid = {
        "x": a["x"], "src": a["src"], "dst": a["dst"],
        "W0": a["L0_gnn_W"], "b0": a["L0_gnn_b"],
        "WgT": a["L0_ffn_Wg"].T, "bg": a["L0_ffn_bg"],
        "W1": blocks(t_(a["L0_ffn_W1"], 0, 2, 1)),
        "b1": t_(a["L0_ffn_b1"].reshape(ne, hid // P, P), 0, 2, 1),
        "W2": blocks(t_(a["L0_ffn_W2"], 0, 2, 1)),
        "b2": a["L0_ffn_b2"],
        "Wp": a["L1_gnn_W"], "WpT": a["L1_gnn_W"].T,
        "att": _np.stack([a["L1_gnn_a_src"].reshape(-1), a["L1_gnn_a_dst"].reshape(-1)], 1),
        "sW1": a["L1_ffn_sW1"], "sb1": a["L1_ffn_sb1"].reshape(-1, P).T,
        "sW2": a["L1_ffn_sW2"], "sb2": a["L1_ffn_sb2"].reshape(-1, P).T,
        "sW3": a["L1_ffn_sW3"], "sb3": a["L1_ffn_sb3"],
        "eW1": t_(a["L1_ffn_eW1"], 1, 0, 2).reshape(d, -1), "eb1": a["L1_ffn_eb1"].T,
        "eW2": t_(a["L1_ffn_eW2"], 1, 0, 2).reshape(P, -1), "eb2": a["L1_ffn_eb2"].T,
        "eW3": t_(a["L1_ffn_eW3"], 1, 0, 2).reshape(a["L1_ffn_eW3"].shape[1], -1), "eb3": a["L1_ffn_eb3"],
        "gW": a["L1_ffn_gW"], "gb": a["L1_ffn_gb"],
    }
    arrays, aps = {}, {}
    for name, v in laid.items():
        v = _np.ascontiguousarray(v)
        arrays[f"in_{name}_dram"] = v
        aps[name] = nc.dram_tensor(f"in_{name}_dram", v.shape, _mybir.dt.from_np(v.dtype), kind="ExternalInput").ap()
    out = nc.dram_tensor("out_0_dram", a["x"].shape, F32, kind="ExternalOutput").ap()
    build(nc, STOP, z, aps, out)
    r = _run(nc, [arrays], core_ids=[0])
    return r.results[0]["out_0_dram"]
```

```python
from contextlib import ExitStack

import concourse.bass as bass
from concourse import mybir

P = 128
ALU = mybir.AluOpType
ACT = mybir.ActivationFunctionType
AX_X = mybir.AxisListType.X
F32 = mybir.dt.float32
I32 = mybir.dt.int32

LN_EPS = 1e-5
NORM_EPS = 1e-12
BIG = 1e30
STOP = 99


class Sizes:

    def __init__(self, n_nodes, d, n_edges, n_exp, hid, heads):
        self.N, self.D, self.E = n_nodes, d, n_edges
        self.NT = -(-n_nodes // P)
        self.NPAD = self.NT * P
        self.KD = d // P
        self.Q = 8
        self.SE = self.Q * P
        self.NS = -(-n_edges // self.SE)
        self.RG = -(-self.NS * self.Q // P)
        self.EPAD = (self.RG * P + 1) * P
        self.R = 6
        self.ITEMS = self.NS + self.NT - 1
        self.TABW = self.ITEMS + 4
        self.BS = 2
        self.NB = self.NS // self.BS
        self.NE, self.HID = n_exp, hid
        self.KH = hid // P
        self.HEADS = heads
        self.TOK = 256
        self.ET = (2 * self.NPAD + n_exp * (self.TOK - 1)) // self.TOK
        self.NEVER = 8191
        assert self.ITEMS % 2 == 0 and self.NS % self.BS == 0 and self.R == 3 * self.BS and self.NB % 3 == 1 and self.NT % 2 and self.NEVER >= self.NPAD


class Local:

    def __init__(self, eng, sem):
        self.eng, self.sem, self.n = eng, sem, 0

    def tick(self, ins):
        ins.then_inc(self.sem, 1)
        self.n += 1

    def settle(self):
        self.eng.wait_ge(self.sem, self.n)

    def link(self, ins):
        self.tick(ins)
        self.settle()

    def restart(self):
        if self.n:
            self.settle()
            self.eng.sem_clear(self.sem)
            self.n = 0


def build(nc, stop, z, a, out):
    N, D, NT, KD, Q, NS, R = z.N, z.D, z.NT, z.KD, z.Q, z.NS, z.R
    FULL = N // P
    REST = N - FULL * P
    HEADS, HC = z.HEADS, z.D // z.HEADS
    GW = D + 2 * HEADS + 2

    def scratch(name, shape, dt):
        return nc.dram_tensor(name, shape, dt).ap()

    src_sorted = scratch("src_sorted", (z.EPAD,), I32)
    dst_sorted = scratch("dst_sorted", (z.EPAD,), I32)
    node_count = scratch("node_count", (z.NEVER + 1, 1), F32)
    node_start = scratch("node_start", (z.NEVER + 1, 1), F32)
    h0_rows = scratch("h0_rows", (z.NPAD, D), F32)
    xd_rows = scratch("xd_rows", (z.ET * z.TOK, D), F32)
    yd_rows = scratch("yd_rows", (z.ET * z.TOK, D), F32)
    g_rows = scratch("g_rows", (z.NPAD, D + HEADS), F32)

    spent = []

    def clear_spent():
        nums = sorted(set(spent))
        firsts = [n for n in nums if n - 1 not in nums]
        lasts = [n for n in nums if n + 1 not in nums]
        with nc.Block() as block:
            @block.sync
            def _(sp):
                for lo, hi in zip(firsts, lasts):
                    sp.sem_clear(range(lo, hi + 1))
        spent.clear()

    top = ExitStack()

    def make(ctx):
        def sb(name, shape, dt=F32):
            return ctx.enter_context(nc.sbuf_tensor(name, shape, dt))

        def ps(name, shape, dt=F32):
            return ctx.enter_context(nc.psum_tensor(name, shape, dt))

        def sem(name):
            one = ctx.enter_context(nc.semaphore(name))
            spent.append(one.num)
            return one

        return sb, ps, sem

    with top:
        sb, _, sem = make(top)
        s_gath_l0 = [sem(f"s_gath_l0_{k}") for k in range(R)]
        s_gath_l1 = [sem(f"s_gath_l1_{k}") for k in range(R)]
        s_sent = [sem(f"s_sent{k}") for k in range(7)]
        s_got = [sem(f"s_got{k}") for k in range(7)]
        s_sort = [sem(f"s_sort{k}") for k in range(4)]
        spent.clear()
        X = sb("X", [P, NT, D])
        ACC = sb("ACC", [P, NT, GW])
        ident = sb("ident", [P, P])
        ones = sb("ones", [P, P])
        iota_n = sb("iota_n", [P, P])
        srcT = sb("srcT", [P, z.RG * P], I32)
        dstT = sb("dstT", [P, z.RG * P])
        lastT = sb("lastT", [P, z.RG * P])
        tab = sb("tab", [1, z.TABW, 2], I32)
        free_at = sb("free_at", [1, NS], I32)
        tile_base = sb("tile_base", [P, z.TABW])
        pair_end = sb("pair_end", [1, z.NB + 1], I32)

        stats = sb("stats", [P, NT, 6])
        mean = sb("mean", [P, NT])
        rstd = sb("rstd", [P, NT])
        lnt = sb("lnt", [P, 3, NT])

        def ln_moments(loc, s_var):
            me, vo = stats[:, :, 1], stats[:, :, 5]
            mo, ve = stats[:, :, 4], stats[:, :, 2]
            loc.tick(nc.vector.tensor_tensor(lnt[:, 0], me, mo, ALU.add))
            loc.tick(nc.vector.tensor_tensor(lnt[:, 1], me, mo, ALU.subtract))
            loc.link(nc.vector.tensor_tensor(lnt[:, 2], ve, vo, ALU.add))
            loc.tick(nc.vector.tensor_scalar(mean[:], lnt[:, 0], 0.5, None, ALU.mult))
            loc.link(nc.vector.scalar_tensor_tensor(out=lnt[:, 1], in0=lnt[:, 1], scalar=0.25, in1=lnt[:, 1],
                                                    op0=ALU.mult, op1=ALU.mult))
            loc.link(nc.vector.scalar_tensor_tensor(out=lnt[:, 1], in0=lnt[:, 2], scalar=1.0 / D, in1=lnt[:, 1],
                                                    op0=ALU.mult, op1=ALU.add))
            loc.tick(nc.vector.tensor_scalar(lnt[:, 0], lnt[:, 1], LN_EPS, None, ALU.add))
            loc.settle()
            nc.vector.sem_inc(s_var, 1)

        def ln_root(act, s_var, s_root):
            act.wait_ge(s_var, 1)
            nc.scalar.activation(lnt[:, 2], lnt[:, 0], ACT.Sqrt).then_inc(s_root, 1)

        def ln_rstd(loc, s_root):
            loc.eng.wait_ge(s_root, 1)
            loc.link(nc.vector.reciprocal(rstd[:], lnt[:, 2]))

        def ln_apply(out_ap, in_ap, t):
            return nc.vector.tensor_scalar(out_ap, in_ap, mean[:, t], rstd[:, t], ALU.subtract, ALU.mult)

        LISTS = ((src_sorted, 0), (dst_sorted, 0), (dst_sorted, 1))
        LLEN = z.RG * P * P
        NTURN = len(LISTS) * z.RG
        edge = ExitStack()
        with edge:
            sb, ps, sem = make(edge)
            rows_i = sb("rows_i", [P, 3, z.RG, P], I32)
            rows_f = sb("rows_f", [P, 3, z.RG, P])
            q_last = sb("q_last", [P, 1])
            viol = sb("viol", [P, 1])
            unsorted = sb("unsorted", [1, 1], I32)
            pT = [ps(f"pT{i}", [P, 4 * P]) for i in range(2)]

            def load_lists(sp, s_rows):
                for n, (lst, off) in enumerate(LISTS):
                    sp.dma_start(rows_i[:, n, :, :], lst[off:off + LLEN].rearrange("(g p e) -> p g e", p=P, e=P))\
                        .then_inc(s_rows, 16)

            def rows_ready(loc, s_rows, s_rowsf):
                loc.eng.wait_ge(s_rows, 16 * len(LISTS))
                loc.link(nc.vector.tensor_copy(rows_f[:], rows_i[:]))
                loc.link(nc.vector.tensor_tensor(rows_i[:, 0], rows_f[:, 1], rows_f[:, 2], ALU.is_gt))
                loc.link(nc.vector.tensor_reduce(viol[:], rows_i[:, 0].rearrange("p g e -> p (g e)"), AX_X, ALU.max))
                loc.link(nc.vector.tensor_tensor(rows_f[:, 2], rows_f[:, 1], rows_f[:, 2], ALU.not_equal))
                loc.link(nc.vector.tensor_scalar(rows_f[:, 2, :, P - 1:P], rows_f[:, 2, :, P - 1:P], q_last[:, 0:1],
                                                 None, ALU.max))
                loc.eng.sem_inc(s_rowsf, 1)

            def turn_lists(pe, s_rowsf, s_turned, s_copied):
                pe.wait_ge(s_rowsf, 1)
                for t in range(NTURN):
                    n, g = divmod(t, z.RG)
                    if t >= 2:
                        pe.wait_ge(s_copied, t - 1)
                    nc.tensor.transpose(pT[t % 2][:, 0:P], rows_f[:, n, g, :], ident[:]).then_inc(s_turned, 1)

            def copy_lists(dve, s_turned, s_copied):
                for t in range(NTURN):
                    n, g = divmod(t, z.RG)
                    dve.wait_ge(s_turned, t + 1)
                    nc.vector.tensor_copy((srcT, dstT, lastT)[n][:, g * P:(g + 1) * P], pT[t % 2][:, 0:P])\
                        .then_inc(s_copied, 1)
                dve.wait_ge(s_copied, NTURN)

            with ExitStack() as ctx:
                sb, ps, sem = make(ctx)
                pads = sb("pads", [16, 2, (z.EPAD - z.E) // 16], I32)
                q_last_i = sb("q_last_i", [P, 1], I32)
                pV = ps("pV", [P, 512])
                s_x = sem("s_x")
                s_pads = sem("s_pads")
                s_lists = sem("s_lists")
                s_rows = sem("s_rows")
                s_const = sem("s_const")
                s_rowsf = sem("s_rowsf")
                s_turned = sem("s_turned")
                s_copied = sem("s_copied")
                s_viol = sem("s_viol")
                s_stat = sem("s_stat")
                s_var = sem("s_var")
                s_root = sem("s_root")
                s_h0 = sem("s_h0")
                s_h0st = sem("s_h0st")
                s_dve = sem("s_dve")
                s_pool = sem("s_pool")
                with nc.Block() as block:
                    @block.sync
                    def _(sp):
                        for lst, name in ((src_sorted, "src"), (dst_sorted, "dst")):
                            sp.dma_start(lst[0:z.E].rearrange("(a b) -> a b", a=16),
                                         a[name].rearrange("(a b) -> a b", a=16)).then_inc(s_lists, 16)
                        sp.dma_start(X[:, 0:FULL, :], a["x"][0:FULL * P, :].rearrange("(t p) d -> p t d", p=P))\
                            .then_inc(s_x, 16)
                        sp.wait_ge(s_const, 1)
                        sp.dma_start(X[0:REST, FULL, :], a["x"][FULL * P:N, :]).then_inc(s_x, 16)
                        sp.wait_ge(s_pads, 2)
                        for n, lst in enumerate((src_sorted, dst_sorted)):
                            sp.dma_start(lst[z.E:z.EPAD].rearrange("(a b) -> a b", a=16), pads[:, n, :])\
                                .then_inc(s_lists, 16)
                        sp.wait_ge(s_lists, 64)
                        load_lists(sp, s_rows)
                        sp.wait_ge(s_h0, NT)
                        sp.dma_start(h0_rows.rearrange("(t p) d -> p t d", p=P), ACC[:, :, 0:D])\
                            .then_inc(s_h0st, 16)
                        sp.wait_ge(s_h0st, 16)

                    @block.gpsimd
                    def _(pool):
                        loc = Local(pool, s_pool)
                        nc.gpsimd.memset(X[:, FULL, :], 0.0).then_inc(s_const, 1)
                        nc.gpsimd.memset(pads[:, 0, :], 0).then_inc(s_pads, 1)
                        nc.gpsimd.memset(pads[:, 1, :], z.NEVER).then_inc(s_pads, 1)
                        loc.link(nc.gpsimd.memset(ident[:], 0.0))
                        nc.gpsimd.affine_select(out=ident[:], in_=ident[:], compare_op=ALU.not_equal, fill=1.0,
                                                base=0, pattern=[[-1, P]], channel_multiplier=1)\
                            .then_inc(s_const, 1)
                        nc.gpsimd.memset(ones[:], 1.0).then_inc(s_const, 1)
                        nc.gpsimd.iota(iota_n[:], pattern=[[1, P]], base=0, channel_multiplier=0,
                                       allow_small_or_imprecise_dtypes=True).then_inc(s_const, 1)
                        nc.gpsimd.iota(q_last_i[:], pattern=[[1, 1]], base=0, channel_multiplier=1)\
                            .then_inc(s_const, 1)

                    @block.scalar
                    def _(act):
                        ln_root(act, s_var, s_root)

                    @block.vector
                    def _(dve):
                        loc = Local(dve, s_dve)
                        dve.wait_ge(s_const, 5)
                        loc.link(nc.vector.tensor_single_scalar(q_last_i[:], q_last_i[:], Q - 1, op=ALU.bitwise_and))
                        loc.link(nc.vector.tensor_single_scalar(q_last[:], q_last_i[:], Q - 1, op=ALU.is_equal))
                        rows_ready(loc, s_rows, s_rowsf)
                        copy_lists(dve, s_turned, s_copied)
                        dve.wait_ge(s_viol, 1)
                        loc.link(nc.vector.tensor_scalar(unsorted[:], pV[0:1, 0:1], 1.0, None, ALU.min))
                        dve.wait_ge(s_x, 32)
                        with dve.Fori(0, NT) as t:
                            nc.vector.bn_stats(stats[:, bass.ds(t, 1), :], X[:, bass.ds(t, 1), :]).then_inc(s_stat, 1)
                        dve.wait_ge(s_stat, NT)
                        ln_moments(loc, s_var)
                        ln_rstd(loc, s_root)
                        with dve.Fori(0, NT) as t:
                            ln_apply(ACC[:, bass.ds(t, 1), 0:D], X[:, bass.ds(t, 1), :], bass.ds(t, 1)).then_inc(s_h0, 1)

                    @block.tensor
                    def _(pe):
                        pe.wait_ge(s_const, 3)
                        turn_lists(pe, s_rowsf, s_turned, s_copied)
                        nc.tensor.matmul(pV[:, 0:1], ones[:], viol[:], start=True, stop=True).then_inc(s_viol, 1)

            CHUNKS = -(-z.E // P)
            NODES = z.NEVER + 1
            PER = NODES // P
            with ExitStack() as ctx:
                sb, ps, sem = make(ctx)
                rank = sb("rank", [P, CHUNKS])
                lower = sb("lower", [P, P])
                below = sb("below1", [P, P])
                col = sb("col", [P, 1])
                diag = sb("diag", [P, P])
                same = sb("same", [P, P])
                r_in = sb("r_in", [P, 1])
                n_in = sb("n_in", [P, 1])
                got = sb("got", [P, 1])
                put = sb("put", [P, 1])
                cidx = sb("cidx", [P, 1], I32)
                pidx = sb("pidx", [P, 1], I32)
                fidx = sb("fidx", [P, 1])
                pay = sb("pay", [P, 2], I32)
                counts = sb("counts", [P, PER])
                starts = sb("starts", [P, PER])
                off = sb("off", [P, 1])
                pB = ps("pB1", [P, 512])
                pP = ps("pP1", [P, 512])
                s_ones = sem("s_ones1")
                s_cz = sem("s_cz")
                s_set = sem("s_set1")
                s_a = sem("s_a1")
                s_b = sem("s_b1")
                s_cur = s_sort[0]
                s_put = s_sort[1]
                s_start = s_sort[2]
                s_move = s_sort[3]
                s_c = sem("s_c1")
                s_done = sem("s_done1")
                s_seen = sem("s_seen1")
                s_cl = sem("s_cl1")
                s_tot = sem("s_tot1")
                s_off = sem("s_off1")
                s_st = sem("s_st1")
                s_stw = sem("s_stw1")
                s_p = sem("s_p1")
                s_q = sem("s_q1")
                s_moved = sem("s_moved1")
                s_rows = sem("s_rows1")
                s_rowsf = sem("s_rowsf1")
                s_turned = sem("s_turned1")
                s_copied = sem("s_copied1")
                s_dve = sem("s_dve1")
                s_pool = sem("s_pool1")
                flag = lambda eng: eng.value_load(unsorted[0:1, 0:1], min_val=0, max_val=1)
                with nc.Block() as block:
                    @block.sync
                    def _(sp):
                        with sp.If(flag(sp)):
                            sp.wait_ge(s_set, 1)
                            sp.dma_start(node_count.rearrange("(p c) a -> p (c a)", p=P), counts[:]).then_inc(s_cz, 16)
                            sp.wait_ge(s_done, CHUNKS + 1)
                            sp.dma_start(counts[:], node_count.rearrange("(p c) a -> p (c a)", p=P)).then_inc(s_cl, 16)
                            sp.wait_ge(s_st, 1)
                            sp.dma_start(node_start.rearrange("(p c) a -> p (c a)", p=P), starts[:]).then_inc(s_stw, 16)
                            sp.wait_ge(s_stw, 16)
                            sp.wait_ge(s_moved, CHUNKS + 1)
                            load_lists(sp, s_rows)

                    @block.gpsimd
                    def _(pool):
                        with pool.If(flag(pool)):
                            loc = Local(pool, s_pool)
                            nc.gpsimd.affine_select(out=lower[:], in_=ones[:], compare_op=ALU.is_ge, fill=0.0,
                                                    base=-1, pattern=[[-1, P]], channel_multiplier=1).then_inc(s_ones, 1)
                            nc.gpsimd.affine_select(out=below[:], in_=ones[:], compare_op=ALU.is_ge, fill=0.0,
                                                    base=-1, pattern=[[1, P]], channel_multiplier=-1).then_inc(s_ones, 1)
                            pool.wait_ge(s_cz, 16)
                            pool.sem_inc(s_done, 1)
                            with pool.Fori(0, CHUNKS) as c:
                                pool.wait_ge(s_a, c + 1)
                                pool.sem_inc(s_seen, 1)
                                pool.indirect_dma_start(
                                    out=got[:], out_offset=None, in_=node_count,
                                    in_offset=bass.IndirectOffsetOnAxis(ap=cidx[:, 0:1], axis=0)).then_inc(s_cur, 16)
                                pool.wait_ge(s_c, c + 1)
                                pool.sem_inc(s_seen, 1)
                                pool.indirect_dma_start(
                                    out=node_count, in_=put[:], in_offset=None,
                                    out_offset=bass.IndirectOffsetOnAxis(ap=pidx[:, 0:1], axis=0),
                                    bounds_check=NODES - 1, oob_is_err=False).then_inc(s_put, 16)
                                pool.wait_ge(s_put, c * 16 + 16)
                                pool.sem_inc(s_done, 1)
                            pool.wait_ge(s_stw, 16)
                            pool.sem_inc(s_moved, 1)
                            with pool.Fori(0, CHUNKS) as c:
                                pool.wait_ge(s_p, c + 1)
                                pool.sem_inc(s_seen, 1)
                                pool.indirect_dma_start(
                                    out=got[:], out_offset=None, in_=node_start,
                                    in_offset=bass.IndirectOffsetOnAxis(ap=cidx[:, 0:1], axis=0)).then_inc(s_start, 16)
                                pool.wait_ge(s_q, c + 1)
                                pool.sem_inc(s_seen, 1)
                                for n, lst in enumerate((src_sorted, dst_sorted)):
                                    pool.indirect_dma_start(
                                        out=lst.unsqueeze(1), in_=pay[:, n:n + 1], in_offset=None,
                                        out_offset=bass.IndirectOffsetOnAxis(ap=pidx[:, 0:1], axis=0)).then_inc(s_move, 16)
                                pool.wait_ge(s_move, c * 32 + 32)
                                pool.sem_inc(s_moved, 1)

                    @block.tensor
                    def _(pe):
                        with pe.If(flag(pe)):
                            with pe.Fori(0, CHUNKS) as c:
                                pe.wait_ge(s_a, c + 1)
                                nc.tensor.matmul(pB[:, 0:P], ones[:], diag[:], start=True, stop=True).then_inc(s_b, 1)
                            pe.wait_ge(s_ones, 2)
                            pe.wait_ge(s_tot, 1)
                            nc.tensor.matmul(pP[:, 0:1], below[:], off[:], start=True, stop=True).then_inc(s_off, 1)
                            turn_lists(pe, s_rowsf, s_turned, s_copied)

                    @block.vector
                    def _(dve):
                        with dve.If(flag(dve)):
                            loc = Local(dve, s_dve)
                            loc.link(nc.vector.memset(counts[:], 0.0))
                            dve.sem_inc(s_set, 1)
                            dve.wait_ge(s_ones, 2)
                            loc.restart()
                            with dve.Fori(0, CHUNKS) as c:
                                dve.wait_ge(s_done, c + 1)
                                loc.link(nc.vector.tensor_scalar(col[:], dstT[:, bass.ds(c, 1)], 0.0, None, ALU.add))
                                loc.tick(nc.vector.tensor_copy(cidx[:], col[:]))
                                loc.link(nc.vector.tensor_scalar(diag[:], ident[:], col[:, 0:1], None, ALU.mult))
                                dve.sem_inc(s_a, 1)
                                dve.wait_ge(s_b, c + 1)
                                loc.link(nc.vector.tensor_scalar(same[:], pB[:, 0:P], col[:, 0:1], None, ALU.is_equal))
                                loc.tick(nc.vector.tensor_reduce(n_in[:], same[:], AX_X, ALU.add))
                                loc.link(nc.vector.tensor_tensor(diag[:], same[:], lower[:], ALU.mult))
                                loc.link(nc.vector.tensor_reduce(r_in[:], diag[:], AX_X, ALU.add))
                                loc.link(nc.vector.tensor_tensor(fidx[:], n_in[:], r_in[:], ALU.subtract))
                                loc.link(nc.vector.tensor_scalar(fidx[:], fidx[:], -1.0, float(2 * NODES), ALU.add, ALU.mult))
                                loc.link(nc.vector.tensor_tensor(pidx[:], fidx[:], col[:], ALU.add))
                                dve.wait_ge(s_cur, c * 16 + 16)
                                loc.tick(nc.vector.tensor_tensor(rank[:, bass.ds(c, 1)], got[:], r_in[:], ALU.add))
                                loc.link(nc.vector.tensor_tensor(put[:], got[:], n_in[:], ALU.add))
                                dve.sem_inc(s_c, 1)
                                loc.restart()
                            dve.wait_ge(s_cl, 16)
                            loc.link(nc.vector.tensor_tensor_scan(starts[:], ones[:, 0:PER], counts[:], 0.0,
                                                                  ALU.mult, ALU.add))
                            loc.link(nc.vector.tensor_copy(off[:], starts[:, PER - 1:PER]))
                            dve.sem_inc(s_tot, 1)
                            loc.link(nc.vector.tensor_tensor(starts[:], starts[:], counts[:], ALU.subtract))
                            dve.wait_ge(s_off, 1)
                            loc.link(nc.vector.tensor_scalar(starts[:], starts[:], pP[:, 0:1], None, ALU.add))
                            dve.sem_inc(s_st, 1)
                            loc.restart()
                            with dve.Fori(0, CHUNKS) as c:
                                dve.wait_ge(s_moved, c + 1)
                                loc.tick(nc.vector.tensor_scalar(cidx[:], dstT[:, bass.ds(c, 1)], 0.0, None, ALU.add))
                                loc.tick(nc.vector.tensor_scalar(pay[:, 1:2], dstT[:, bass.ds(c, 1)], 0.0, None, ALU.add))
                                loc.link(nc.vector.tensor_scalar(pay[:, 0:1], srcT[:, bass.ds(c, 1)], 0.0, None, ALU.add))
                                dve.sem_inc(s_p, 1)
                                dve.wait_ge(s_start, c * 16 + 16)
                                loc.link(nc.vector.tensor_tensor(pidx[:], got[:], rank[:, bass.ds(c, 1)], ALU.add))
                                dve.sem_inc(s_q, 1)
                                loc.restart()
                            rows_ready(loc, s_rows, s_rowsf)
                            copy_lists(dve, s_turned, s_copied)

        with ExitStack() as ctx:
            sb, ps, sem = make(ctx)
            J = NT - 1
            thr = sb("thr", [P, 1])
            wi = sb("wi", [P, z.TABW])
            cmp1 = sb("cmp1", [P, NS])
            cmpw = sb("cmpw", [P, z.TABW])
            cmps = sb("cmps", [P, NS])
            cmpb = sb("cmpb", [P, z.NB + 1])
            e_end = sb("e_end", [P, 1])
            w_start = sb("w_start", [P, 1])
            tmp1 = sb("tmp1", [P, z.TABW])
            pD = ps("pD", [P, 512])
            pJ = ps("pJ", [P, 512])
            pF = ps("pF", [P, 512])
            pB = ps("pB", [P, 512])
            s_const = sem("s_const1c")
            s_d1 = sem("s_d1")
            s_cmp = sem("s_cmp")
            s_tabs = sem("s_tabs")
            s_dve = sem("s_dve1c")
            with nc.Block() as block:
                @block.gpsimd
                def _(pool):
                    nc.gpsimd.iota(wi[:], pattern=[[1, z.TABW]], base=0, channel_multiplier=0,
                                   allow_small_or_imprecise_dtypes=True).then_inc(s_const, 1)
                    nc.gpsimd.iota(thr[:], pattern=[[1, 1]], base=P, channel_multiplier=P,
                                   allow_small_or_imprecise_dtypes=True).then_inc(s_const, 1)

                @block.tensor
                def _(pe):
                    nc.tensor.matmul(pD[0:J, 0:NS - 1], ones[0:1, 0:J], dstT[0:1, Q:Q * NS:Q], start=True, stop=True)\
                        .then_inc(s_d1, 1)
                    pe.wait_ge(s_cmp, 3)
                    nc.tensor.matmul(pJ[:, 0:z.TABW], ones[0:J, :], cmpw[0:J, :], start=True, stop=True)
                    nc.tensor.matmul(pB[:, 0:z.NB + 1], ones[0:J, :], cmpb[0:J, :], start=True, stop=True)
                    nc.tensor.matmul(pF[:, 0:NS], ones[0:J, :], cmps[0:J, :], start=True, stop=True)\
                        .then_inc(s_tabs, 1)

                @block.vector
                def _(dve):
                    loc = Local(dve, s_dve)
                    dve.wait_ge(s_const, 2)
                    dve.wait_ge(s_d1, 1)
                    loc.link(nc.vector.tensor_scalar(cmp1[0:J, 0:NS - 1], pD[0:J, 0:NS - 1], thr[0:J, 0:1], None,
                                                     ALU.is_lt))
                    loc.link(nc.vector.tensor_reduce(e_end[0:J], cmp1[0:J, 0:NS - 1], AX_X, ALU.add))
                    loc.link(nc.vector.scalar_tensor_tensor(out=w_start[0:J], in0=thr[0:J], scalar=1.0 / P,
                                                            in1=e_end[0:J], op0=ALU.mult, op1=ALU.add))
                    loc.tick(nc.vector.tensor_scalar(cmpw[0:J], wi[0:J], w_start[0:J, 0:1], None, ALU.is_ge))
                    loc.tick(nc.vector.tensor_scalar(cmps[0:J], wi[0:J, 0:NS], float(1 - R), e_end[0:J, 0:1], ALU.add,
                                                     ALU.is_gt))
                    loc.link(nc.vector.tensor_scalar(cmpb[0:J], wi[0:J, 0:z.NB + 1], float(z.BS), e_end[0:J, 0:1],
                                                     ALU.mult, ALU.is_gt))
                    dve.sem_inc(s_cmp, 3)
                    dve.wait_ge(s_tabs, 1)
                    loc.tick(nc.vector.tensor_tensor(tab[0:1, :, 0], wi[0:1], pJ[0:1, 0:z.TABW], ALU.subtract))
                    loc.tick(nc.vector.tensor_copy(tab[0:1, :, 1], pJ[0:1, 0:z.TABW]))
                    loc.tick(nc.vector.tensor_scalar(tile_base[:], pJ[:, 0:z.TABW], float(P), None, ALU.mult))
                    loc.link(nc.vector.tensor_scalar(tmp1[0:1, 0:NS], wi[0:1, 0:NS], float(1 - R), 0.0, ALU.add,
                                                     ALU.max))
                    loc.link(nc.vector.scalar_tensor_tensor(out=free_at[:], in0=tmp1[0:1, 0:NS], scalar=2.0,
                                                            in1=pF[0:1, 0:NS], op0=ALU.add, op1=ALU.add))
                    loc.link(nc.vector.scalar_tensor_tensor(out=pair_end[:], in0=wi[0:1, 0:z.NB + 1], scalar=float(z.BS),
                                                            in1=pB[0:1, 0:z.NB + 1], op0=ALU.mult, op1=ALU.add))
                    loc.link(nc.vector.tensor_single_scalar(pair_end[:], pair_end[:], 1, op=ALU.arith_shift_right))

        def gather_supers(pool, rows, G, width, slot_idx, s_gath, s_item, s_pool_idx, s_seen):
            def one(s, k, n):
                need = pool.value_load(free_at[0:1, bass.ds(s, 1)], min_val=2, max_val=z.ITEMS + 2)
                pool.wait_ge(s_item, need)
                pool.sem_inc(s_seen, 1)
                nc.gpsimd.tensor_copy(slot_idx[:, k * Q:(k + 1) * Q], srcT[:, bass.ds(s * Q, Q)])\
                    .then_inc(s_pool_idx[k], 1)
                pool.wait_ge(s_pool_idx[k], 1)
                pool.sem_clear(s_pool_idx[k])
                for q in range(Q):
                    pool.indirect_dma_start(
                        out=G[:, k * Q + q, 0:width], out_offset=None, in_=rows,
                        in_offset=bass.IndirectOffsetOnAxis(ap=slot_idx[:, k * Q + q:k * Q + q + 1], axis=0),
                    ).then_inc(s_gath[k], 16)
            rounds = NS // R
            with pool.Fori(0, rounds) as i:
                for k in range(R):
                    one(i * R + k, k, i)
            for s in range(rounds * R, NS):
                one(s, s % R, rounds)

        def load_item(eng, w, what):
            hi = (NS + 3, NT - 1)[what]
            return eng.value_load(tab[0:1, bass.ds(w, 1), what], min_val=0, max_val=hi)

        def one_hots(dve, O, w, k):
            s = load_item(dve, w, 0)
            base = tile_base[:, bass.ds(w, 1)]
            return nc.vector.scalar_tensor_tensor(
                out=O[:, k], in0=iota_n[:].unsqueeze(1).to_broadcast([P, Q, P]), scalar=base,
                in1=dstT[:, bass.ds(s * Q, Q)].unsqueeze(2).to_broadcast([P, Q, P]), op0=ALU.add, op1=ALU.is_equal)

        clear_spent()
        with ExitStack() as ctx:
            sb, ps, sem = make(ctx)
            G = sb("G0", [P, R * Q, D + 1])
            O = sb("O0", [P, 2, Q, P])
            slot_idx = sb("slot_idx0", [P, R * Q], I32)
            pS = [ps(f"pS{i}", [P, 512]) for i in range(2)]
            s_gath = s_gath_l0
            s_pool_idx = [sem(f"s_pidx{k}") for k in range(R)]
            s_landed = sem("s_landed")
            s_item = sem("s_item")
            s_oh = sem("s_oh")
            s_merged = sem("s_merged")
            s_ready = sem("s_ready")
            s_seen = sem("s_seen")
            s_dve = sem("s_dve0")
            W = D + 1
            with nc.Block() as block:
                @block.gpsimd
                def _(pool):
                    pool.wait_ge(s_ready, 1)
                    gather_supers(pool, h0_rows, G, D, slot_idx, s_gath, s_item, s_pool_idx, s_seen)

                @block.sync
                def _(sp):
                    rounds = NS // R
                    with sp.Fori(0, rounds) as i:
                        for k in range(R):
                            sp.wait_ge(s_gath[k], i * (16 * Q) + 16 * Q)
                            sp.sem_inc(s_landed, 1)
                    for s in range(rounds * R, NS):
                        sp.wait_ge(s_gath[s % R], 16 * Q * (rounds + 1))
                        sp.sem_inc(s_landed, 1)

                @block.tensor
                def _(pe):
                    with pe.Fori(0, z.ITEMS // 2) as i:
                        for k in range(2):
                            w = i * 2 + k
                            s = load_item(pe, w, 0)
                            pe.wait_ge(s_landed, s + 1)
                            pe.wait_ge(s_merged, w + 1)
                            pe.wait_ge(s_oh, w + 1)
                            for q in range(Q):
                                mm = nc.tensor.matmul(pS[k][:, 0:W], O[:, k, q, :],
                                                      G[:, bass.ds((s % R) * Q + q, 1), :].rearrange("p a d -> p (a d)"),
                                                      start=(q == 0), stop=(q == Q - 1))
                            mm.then_inc(s_item, 1)

                @block.vector
                def _(dve):
                    loc = Local(dve, s_dve)
                    loc.tick(nc.vector.memset(ACC[:], 0.0))
                    loc.link(nc.vector.memset(G[:, :, D:D + 1], 1.0))
                    dve.sem_inc(s_ready, 1)
                    dve.sem_inc(s_item, 2)
                    dve.sem_inc(s_merged, 2)
                    one_hots(dve, O, 0, 0).then_inc(s_oh, 1)
                    loc.restart()
                    with dve.Fori(0, z.ITEMS // 2) as i:
                        for k in range(2):
                            w = i * 2 + k
                            dve.wait_ge(s_item, w + 2)
                            one_hots(dve, O, w + 1, 1 - k).then_inc(s_oh, 1)
                            j = load_item(dve, w, 1)
                            dve.wait_ge(s_item, w + 3)
                            dve.wait_ge(s_merged, w + 2)
                            nc.vector.tensor_tensor(ACC[:, bass.ds(j, 1), 0:W], ACC[:, bass.ds(j, 1), 0:W],
                                                    pS[k][:, 0:W].unsqueeze(1), ALU.add).then_inc(s_merged, 1)
        def dump(view):
            with ExitStack() as ctx:
                sb, ps, sem = make(ctx)
                s_out = sem("s_outdbg")
                with nc.Block() as block:
                    @block.sync
                    def _(sp):
                        sp.dma_start(out[0:FULL * P, :].rearrange("(t p) d -> p t d", p=P), view[:, 0:FULL, 0:D]).then_inc(s_out, 16)
                        sp.dma_start(out[FULL * P:N, :], view[0:REST, FULL, 0:D]).then_inc(s_out, 16)
                        sp.wait_ge(s_out, 32)

        if stop == 2:
            return dump(ACC)

        def top_two(loc, scores, rest, mx, eq, km, sel, prio, n):
            cur = scores
            for c in range(2):
                wide = lambda v: v.unsqueeze(2).to_broadcast([P, NT, n])
                loc.link(nc.vector.tensor_reduce(mx[:, c], cur[:], AX_X, ALU.max))
                loc.link(nc.vector.tensor_tensor(eq[:], cur[:], wide(mx[:, c]), ALU.is_equal))
                loc.link(nc.vector.tensor_tensor(eq[:], eq[:], prio[:].unsqueeze(1).to_broadcast([P, NT, n]), ALU.mult))
                loc.link(nc.vector.tensor_reduce(km[:], eq[:], AX_X, ALU.max))
                loc.link(nc.vector.tensor_tensor(sel[:, c], eq[:], wide(km[:]), ALU.is_equal))
                if c == 0:
                    loc.link(nc.vector.scalar_tensor_tensor(out=rest[:], in0=sel[:, 0], scalar=-BIG, in1=scores[:],
                                                            op0=ALU.mult, op1=ALU.add))
                    cur = rest

        def each_tile(eng, body):
            with eng.Fori(0, NT // 2) as i:
                for k in range(2):
                    body(i * 2 + k, k)
            if NT % 2:
                body(NT - 1, 0)

        clear_spent()
        def skewed(eng, lead, main):
            lead(0, 0)
            with eng.Fori(0, NT // 2) as i:
                for k in range(2):
                    lead(i * 2 + k + 1, 1 - k)
                    main(i * 2 + k, k)
            main(NT - 1, 0)

        NE, KH = z.NE, z.KH
        route = ExitStack()
        with route:
            sb, ps, sem = make(route)
            probs = sb("probs", [P, 2, NT])
            pos_f = sb("pos_f", [P, NT, 2])
            pos = sb("pos", [P, NT, 2], I32)
            eid = sb("eid", [1, z.ET], I32)
            with ExitStack() as ctx:
                sb, ps, sem = make(ctx)
                W0 = sb("W0", [P, 2 * KD, D])
                b0 = sb("b0", [1, D])
                Wg = sb("Wg", [P, KD, NE])
                bg = sb("bg", [1, NE])
                IN = sb("IN", [P, 2, 2 * D])
                HT = sb("HT", [P, 2, 2 * D])
                rdeg = sb("rdeg", [P, NT])
                ssq = sb("ssq", [P, NT])
                rnorm = sb("rnorm", [P, NT])
                sq = sb("sq", [P, 2, D])
                SC = sb("SC", [P, NT, NE])
                pT = [ps(f"pT3{i}", [P, 512]) for i in range(2)]
                pO = [ps(f"pO3{i}", [P, 512]) for i in range(2)]
                pG = [ps(f"pG3{i}", [P, 512]) for i in range(2)]
                s_w = sem("s_w3")
                s_in = sem("s_in3")
                s_turned = sem("s_turned3")
                s_ht = sem("s_ht3")
                s_out3 = sem("s_out3")
                s_relu = sem("s_relu3")
                s_held = sem("s_held3")
                s_rdeg = sem("s_rdeg3")
                s_root0 = sem("s_root03")
                s_x1 = sem("s_x13")
                s_stat = sem("s_stat3")
                s_var = sem("s_var3")
                s_root = sem("s_root3")
                s_in1 = sem("s_in13")
                s_turned1 = sem("s_turned13")
                s_ht1 = sem("s_ht13")
                s_sc = sem("s_sc3")
                s_sccp = sem("s_sccp3")
                s_kept = sem("s_kept3")
                s_dve = sem("s_dve3")
                s_act = sem("s_act3")
                with nc.Block() as block:
                    @block.sync
                    def _(sp):
                        sp.dma_start(W0[:], a["W0"].rearrange("(k p) n -> p k n", p=P)).then_inc(s_w, 16)
                        sp.dma_start(b0[:], a["b0"].unsqueeze(0)).then_inc(s_w, 16)
                        sp.dma_start(Wg[:], a["WgT"].rearrange("(k p) n -> p k n", p=P)).then_inc(s_w, 16)
                        sp.dma_start(bg[:], a["bg"].unsqueeze(0)).then_inc(s_w, 16)

                    @block.vector
                    def _(dve):
                        loc = Local(dve, s_dve)
                        loc.link(nc.vector.tensor_scalar(rdeg[:], ACC[:, :, D], 1.0, None, ALU.max))
                        loc.link(nc.vector.reciprocal(rdeg[:], rdeg[:]))
                        dve.sem_inc(s_rdeg, 1)
                        dve.sem_inc(s_turned, 2)
                        loc.restart()

                        def tile_in(t, k):
                            dve.wait_ge(s_turned, t + 1)
                            ln_apply(IN[:, k, 0:D].unsqueeze(1), X[:, bass.ds(t, 1), :], bass.ds(t, 1))\
                                .then_inc(s_in, 1)
                            nc.vector.tensor_scalar(IN[:, k, D:2 * D].unsqueeze(1), ACC[:, bass.ds(t, 1), 0:D],
                                                    rdeg[:, bass.ds(t, 1)], None, ALU.mult).then_inc(s_in, 1)
                        each_tile(dve, tile_in)
                        dve.wait_ge(s_root0, 1)
                        loc.link(nc.vector.tensor_scalar(rnorm[:], rnorm[:], NORM_EPS, None, ALU.max))
                        loc.link(nc.vector.reciprocal(rnorm[:], rnorm[:]))
                        loc.restart()
                        with dve.Fori(0, NT) as t:
                            one = bass.ds(t, 1)
                            nc.vector.scalar_tensor_tensor(
                                out=X[:, one, :], in0=ACC[:, one, 0:D], scalar=rnorm[:, one], in1=X[:, one, :],
                                op0=ALU.mult, op1=ALU.add).then_inc(s_x1, 1)
                        dve.wait_ge(s_x1, NT)
                        with dve.Fori(0, NT) as t:
                            nc.vector.bn_stats(stats[:, bass.ds(t, 1), :], X[:, bass.ds(t, 1), :]).then_inc(s_stat, 1)
                        dve.wait_ge(s_stat, NT)
                        ln_moments(loc, s_var)
                        ln_rstd(loc, s_root)
                        dve.sem_inc(s_turned1, 2)
                        dve.sem_inc(s_kept, 2)

                        def tile_h1(t, k):
                            dve.wait_ge(s_turned1, t + 1)
                            dve.wait_ge(s_kept, t + 1)
                            ln_apply(IN[:, k, 0:D].unsqueeze(1), X[:, bass.ds(t, 1), :], bass.ds(t, 1))\
                                .then_inc(s_in1, 1)
                        each_tile(dve, tile_h1)

                    @block.scalar
                    def _(act):
                        loc = Local(act, s_act)
                        act.wait_ge(s_rdeg, 1)
                        act.sem_inc(s_ht, 2)
                        act.sem_inc(s_relu, 2)

                        def turned_in(t, k):
                            act.wait_ge(s_turned, t + 3)
                            act.wait_ge(s_out3, t + 1)
                            nc.scalar.activation(HT[:, k, :], pT[k][:], ACT.Copy).then_inc(s_ht, 1)

                        def relu_out(t, k):
                            act.wait_ge(s_out3, t + 3)
                            act.sem_inc(s_held, 1)
                            nc.scalar.activation(ACC[:, bass.ds(t, 1), 0:D], pO[k][:, 0:D].unsqueeze(1), ACT.Relu)\
                                .then_inc(s_relu, 1)
                            act.wait_ge(s_relu, t + 3)
                            act.sem_inc(s_held, 1)
                            loc.link(nc.scalar.activation(sq[:, k].unsqueeze(1), ACC[:, bass.ds(t, 1), 0:D],
                                                          ACT.Square, accum_out=ssq[:, bass.ds(t, 1)]))
                            loc.restart()

                        act.sem_inc(s_out3, 2)
                        loc.restart()

                        skewed(act, turned_in, relu_out)
                        nc.scalar.activation(rnorm[:], ssq[:], ACT.Sqrt).then_inc(s_root0, 1)
                        ln_root(act, s_var, s_root)
                        act.sem_inc(s_sc, 2)

                        def turned_h1(t, k):
                            act.wait_ge(s_turned1, t + 3)
                            act.wait_ge(s_sc, t + 1)
                            nc.scalar.activation(HT[:, k, 0:D], pT[k][:, 0:D], ACT.Copy).then_inc(s_ht1, 1)
                            act.sem_inc(s_held, 1)
                            nc.scalar.activation(ACC[:, bass.ds(t, 1), 0:D], IN[:, k, 0:D].unsqueeze(1), ACT.Copy)\
                                .then_inc(s_kept, 1)

                        def scores(t, k):
                            act.wait_ge(s_sc, t + 3)
                            act.sem_inc(s_held, 1)
                            nc.scalar.activation(SC[:, bass.ds(t, 1), :], pG[k][:, 0:NE].unsqueeze(1), ACT.Copy)\
                                .then_inc(s_sccp, 1)
                        skewed(act, turned_h1, scores)

                    @block.tensor
                    def _(pe):
                        pe.wait_ge(s_w, 64)
                        pe.wait_ge(s_rdeg, 1)

                        def turn(t, k):
                            pe.wait_ge(s_in, 2 * t + 2)
                            pe.wait_ge(s_ht, t + 1)
                            for m in range(2 * KD):
                                tr = nc.tensor.transpose(pT[k][:, m * P:(m + 1) * P], IN[:, k, m * P:(m + 1) * P], ident[:])
                            tr.then_inc(s_turned, 1)

                        def dense(t, k):
                            pe.wait_ge(s_ht, t + 3)
                            pe.wait_ge(s_relu, t + 1)
                            for m in range(2 * KD):
                                nc.tensor.matmul(pO[k][:, 0:D], HT[:, k, m * P:(m + 1) * P], W0[:, m, :],
                                                 start=(m == 0), stop=False)
                            nc.tensor.matmul(pO[k][:, 0:D], ones[0:1, :], b0[:], start=False, stop=True)\
                                .then_inc(s_out3, 1)
                        skewed(pe, turn, dense)
                        pe.sem_inc(s_ht1, 2)
                        pe.sem_inc(s_sccp, 2)

                        def turn_h1(t, k):
                            pe.wait_ge(s_in1, t + 1)
                            pe.wait_ge(s_ht1, t + 1)
                            for m in range(KD):
                                tr = nc.tensor.transpose(pT[k][:, m * P:(m + 1) * P], IN[:, k, m * P:(m + 1) * P], ident[:])
                            tr.then_inc(s_turned1, 1)

                        def gate(t, k):
                            pe.wait_ge(s_ht1, t + 3)
                            pe.wait_ge(s_sccp, t + 1)
                            for m in range(KD):
                                nc.tensor.matmul(pG[k][:, 0:NE], HT[:, k, m * P:(m + 1) * P], Wg[:, m, :],
                                                 start=(m == 0), stop=False)
                            nc.tensor.matmul(pG[k][:, 0:NE], ones[0:1, :], bg[:], start=False, stop=True)\
                                .then_inc(s_sc, 1)
                        skewed(pe, turn_h1, gate)

                with ExitStack() as ctx4:
                    sb, ps, sem = make(ctx4)
                    prio = sb("prio", [P, NE])
                    mx = sb("mx", [P, 2, NT])
                    eq = sb("eq", [P, NT, NE])
                    km = sb("km", [P, NT])
                    sel = sb("sel", [P, 2, NT, NE])
                    SC2 = sb("SC2", [P, NT, NE])
                    both = sb("both", [P, NT, NE])
                    below = sb("below", [P, P])
                    tot = sb("tot", [P, NE, NT])
                    inc = sb("inc", [P, NE, NT])
                    cnt = sb("cnt", [P, NE])
                    cnt_i = sb("cnt_i", [P, NE], I32)
                    tiles = sb("tiles", [P, NE])
                    tend = sb("tend", [P, NE])
                    tbeg = sb("tbeg", [P, NE])
                    row = sb("row", [P, NT, NE])
                    ui = sb("ui", [1, z.ET])
                    ucmp = sb("ucmp", [1, z.ET, NE])
                    dm = sb("dm", [P, NT])
                    zero_rows = sb("zero_rows", [P, 2048])
                    pA = ps("pA4", [P, 512])
                    pB = ps("pB4", [P, 512])
                    s_const = sem("s_const4")
                    s_zero = sem("s_zero4")
                    s_zst = sem("s_zst4")
                    s_both = sem("s_both4")
                    s_cum = sem("s_cum4")
                    s_dm = sem("s_dm4")
                    s_ex = sem("s_ex4")
                    s_dve = sem("s_dve4")
                    s_pool = sem("s_pool4")
                    with nc.Block() as block:
                        @block.gpsimd
                        def _(pool):
                            loc = Local(pool, s_pool)
                            nc.gpsimd.memset(zero_rows[:], 0.0).then_inc(s_zero, 1)
                            nc.gpsimd.iota(prio[:], pattern=[[-1, NE]], base=NE, channel_multiplier=0,
                                           allow_small_or_imprecise_dtypes=True).then_inc(s_const, 1)
                            nc.gpsimd.iota(ui[:], pattern=[[1, z.ET]], base=0, channel_multiplier=0,
                                           allow_small_or_imprecise_dtypes=True).then_inc(s_const, 1)
                            nc.gpsimd.affine_select(out=below[:], in_=ones[:], compare_op=ALU.is_ge, fill=0.0,
                                                    base=-1, pattern=[[1, P]], channel_multiplier=-1)\
                                .then_inc(s_const, 1)

                        @block.sync
                        def _(sp):
                            sp.wait_ge(s_zero, 1)
                            flat = xd_rows.rearrange("(c p r) d -> c p (r d)", p=P, r=2048 // D)
                            chunks = z.ET * z.TOK * D // (P * 2048)
                            for c in range(chunks):
                                sp.dma_start(flat[c], zero_rows[:]).then_inc(s_zst, 16)
                            sp.wait_ge(s_zst, 16 * chunks)

                        @block.scalar
                        def _(act):
                            act.wait_ge(s_dm, 1)
                            nc.scalar.activation(dm[:], dm[:], ACT.Exp).then_inc(s_ex, 1)

                        @block.tensor
                        def _(pe):
                            pe.wait_ge(s_const, 3)
                            pe.wait_ge(s_both, 1)
                            flat = both[:].rearrange("p t e -> p (t e)")
                            nc.tensor.matmul(pA[:, 0:NT * NE], below[:], flat, start=True, stop=True)
                            nc.tensor.matmul(pB[:, 0:NT * NE], ones[:], flat, start=True, stop=True).then_inc(s_cum, 1)

                        @block.vector
                        def _(dve):
                            loc = Local(dve, s_dve)
                            over_t = lambda v: v.unsqueeze(1).to_broadcast([P, NT, NE])
                            dve.wait_ge(s_const, 3)
                            top_two(loc, SC, SC2, mx, eq, km, sel, prio, NE)
                            loc.tick(nc.vector.tensor_tensor(both[:], sel[:, 0], sel[:, 1], ALU.add))
                            loc.link(nc.vector.tensor_tensor(dm[:], mx[:, 1], mx[:, 0], ALU.subtract))
                            dve.sem_inc(s_both, 1)
                            dve.sem_inc(s_dm, 1)
                            dve.wait_ge(s_ex, 1)
                            loc.link(nc.vector.tensor_scalar(probs[:, 0], dm[:], 1.0, None, ALU.add))
                            loc.link(nc.vector.reciprocal(probs[:, 0], probs[:, 0]))
                            loc.tick(nc.vector.tensor_tensor(probs[:, 1], dm[:], probs[:, 0], ALU.mult))
                            dve.wait_ge(s_cum, 1)
                            loc.link(nc.vector.tensor_copy(tot[:], pB[:, 0:NT * NE].rearrange("p (t e) -> p e t", e=NE)))
                            for e in range(NE):
                                loc.tick(nc.vector.tensor_tensor_scan(inc[:, e], ones[:, 0:NT], tot[:, e], 0.0,
                                                                      ALU.mult, ALU.add))
                            loc.settle()
                            loc.link(nc.vector.tensor_scalar(cnt[:], inc[:, :, NT - 1], float(z.TOK - 1), None, ALU.add))
                            loc.link(nc.vector.tensor_copy(cnt_i[:], cnt[:]))
                            loc.link(nc.vector.tensor_single_scalar(cnt_i[:], cnt_i[:], z.TOK.bit_length() - 1,
                                                                    op=ALU.arith_shift_right))
                            loc.link(nc.vector.tensor_copy(tiles[:], cnt_i[:]))
                            loc.link(nc.vector.tensor_tensor_scan(tend[:], ones[:, 0:NE], tiles[:], 0.0,
                                                                  ALU.mult, ALU.add))
                            loc.link(nc.vector.tensor_tensor(tbeg[:], tend[:], tiles[:], ALU.subtract))
                            loc.tick(nc.vector.tensor_tensor(ucmp[:], tbeg[0:1].unsqueeze(1).to_broadcast([1, z.ET, NE]),
                                                             ui[:].unsqueeze(2).to_broadcast([1, z.ET, NE]), ALU.is_le))
                            loc.link(nc.vector.tensor_tensor(inc[:], inc[:], tot[:], ALU.subtract))
                            loc.link(nc.vector.tensor_tensor(
                                row[:], inc[:].rearrange("p e t -> p t e"),
                                pA[:, 0:NT * NE].rearrange("p (t e) -> p t e", e=NE), ALU.add))
                            loc.link(nc.vector.scalar_tensor_tensor(out=row[:], in0=over_t(tbeg[:]), scalar=float(z.TOK),
                                                                    in1=row[:], op0=ALU.mult, op1=ALU.add))
                            loc.link(nc.vector.tensor_reduce(ui[:], ucmp[:], AX_X, ALU.add))
                            loc.tick(nc.vector.tensor_scalar(eid[:], ui[:], -1.0, None, ALU.add))
                            for c in range(2):
                                loc.link(nc.vector.tensor_tensor(eq[:], sel[:, c], row[:], ALU.mult))
                                loc.link(nc.vector.tensor_reduce(pos_f[:, :, c], eq[:], AX_X, ALU.add))
                            loc.link(nc.vector.tensor_copy(pos[:], pos_f[:]))

            SLOTS = 7
            assert NT % SLOTS == 0
            with ExitStack() as ctx:
                sb, ps, sem = make(ctx)
                stage = sb("stage", [P, SLOTS, D])
                sidx = sb("sidx", [P, SLOTS, 2], I32)
                s_staged = [sem(f"s_staged{k}") for k in range(SLOTS)]
                s_seen = sem("s_seen5")
                s_held = sem("s_held5")
                with nc.Block() as block:
                    @block.scalar
                    def _(act):
                        def one_round(i, first):
                            for k in range(SLOTS):
                                t = bass.ds(i * SLOTS + k, 1)
                                if not first:
                                    act.wait_ge(s_sent[k], i * 32)
                                    act.sem_inc(s_held, 1)
                                nc.scalar.activation(stage[:, k].unsqueeze(1), ACC[:, t, 0:D], ACT.Copy)\
                                    .then_inc(s_staged[k], 1)
                                nc.scalar.activation(sidx[:, k].unsqueeze(1), pos_f[:, t, :], ACT.Copy)\
                                    .then_inc(s_staged[k], 1)

                        one_round(0, True)
                        with act.Fori(1, NT // SLOTS) as i:
                            one_round(i, False)

                    @block.gpsimd
                    def _(pool):
                        with pool.Fori(0, NT // SLOTS) as i:
                            for k in range(SLOTS):
                                pool.wait_ge(s_staged[k], i * 2 + 2)
                                pool.sem_inc(s_seen, 1)
                                for c in range(2):
                                    pool.indirect_dma_start(
                                        out=xd_rows, in_=stage[:, k, :], in_offset=None,
                                        out_offset=bass.IndirectOffsetOnAxis(ap=sidx[:, k, c:c + 1], axis=0),
                                    ).then_inc(s_sent[k], 16)
                        for k in range(SLOTS):
                            pool.wait_ge(s_sent[k], 32 * (NT // SLOTS))

            clear_spent()
            HALVES = z.TOK // P
            with ExitStack() as ctx:
                sb, ps, sem = make(ctx)
                w1s = sb("w1s", [P, 2, KD, z.HID])
                w2s = sb("w2s", [P, 2, KH, D])
                b1s = sb("b1s", [P, 2, KH])
                b2s = sb("b2s", [1, 2, D])
                XE = sb("XE", [P, 2, HALVES, D])
                XT = sb("XT", [P, 2, KD, z.TOK])
                HE = sb("HE", [P, KH, z.TOK])
                YE = sb("YE", [P, 2, HALVES, D])
                pX = ps("pX6", [P, KD, z.TOK])
                pH = [ps(f"pH6{i}", [P, 512]) for i in range(3)]
                pY = [ps(f"pY6{i}", [P, 512]) for i in range(2)]
                s_load = [sem(f"s_load6{k}") for k in range(2)]
                s_tile = sem("s_tile6")
                s_turned = sem("s_turned6")
                s_xt = sem("s_xt6")
                s_hmm = sem("s_hmm6")
                s_relu = sem("s_relu6")
                s_ymm = sem("s_ymm6")
                s_ycp = sem("s_ycp6")
                s_store = [sem(f"s_store6{k}") for k in range(2)]
                U = z.ET
                assert U % 2 == 0
                with nc.Block() as block:
                    @block.sync
                    def _(sp):
                        with sp.Fori(0, U // 2) as i:
                            for k in range(2):
                                u = i * 2 + k
                                e = sp.value_load(eid[0:1, bass.ds(u, 1)], min_val=0, max_val=NE - 1)
                                sp.wait_ge(s_ymm, u + 1)
                                sp.dma_start(XE[:, k], xd_rows[bass.ds(u * z.TOK, z.TOK), :]
                                             .rearrange("(a p) d -> p a d", p=P)).then_inc(s_load[k], 16)
                                sp.dma_start(w1s[:, k], a["W1"][bass.ds(e, 1)].rearrange("a p (k h) -> p (a k) h", k=KD))\
                                    .then_inc(s_load[k], 16)
                                sp.dma_start(w2s[:, k], a["W2"][bass.ds(e, 1)].rearrange("a p (k d) -> p (a k) d", k=KH))\
                                    .then_inc(s_load[k], 16)
                                sp.dma_start(b1s[:, k], a["b1"][bass.ds(e, 1)].rearrange("a p k -> p (a k)"))\
                                    .then_inc(s_load[k], 16)
                                sp.dma_start(b2s[:, k], a["b2"][bass.ds(e, 1)]).then_inc(s_load[k], 16)

                    @block.tensor
                    def _(pe):
                        pe.sem_inc(s_ymm, 2)
                        pe.sem_inc(s_xt, 1)
                        pe.sem_inc(s_relu, 3)
                        with pe.Fori(0, U // 2) as i:
                            for k in range(2):
                                u = i * 2 + k
                                pe.wait_ge(s_load[k], i * 80 + 80)
                                pe.wait_ge(s_xt, u + 1)
                                for h in range(HALVES):
                                    for m in range(KD):
                                        tr = nc.tensor.transpose(pX[:, m, h * P:(h + 1) * P],
                                                                 XE[:, k, h, m * P:(m + 1) * P], ident[:])
                                tr.then_inc(s_turned, 1)
                                pe.wait_ge(s_xt, u + 2)
                                for b in range(KH):
                                    pe.wait_ge(s_relu, u * KH + b + 1)
                                    for m in range(KD):
                                        mm = nc.tensor.matmul(pH[b % 3][:, 0:z.TOK],
                                                              w1s[:, k, m, b * P:(b + 1) * P], XT[:, k, m, :],
                                                              start=(m == 0), stop=(m == KD - 1))
                                    mm.then_inc(s_hmm, 1)
                                pe.wait_ge(s_ycp, 2 * u + 1)
                                for h in range(HALVES):
                                    for b in range(KH):
                                        if h == 0:
                                            pe.wait_ge(s_relu, u * KH + b + 4)
                                        nc.tensor.matmul(pY[h][:, 0:D], HE[:, b, h * P:(h + 1) * P], w2s[:, k, b, :],
                                                         start=(b == 0), stop=False)
                                    mm = nc.tensor.matmul(pY[h][:, 0:D], ones[0:1, :], b2s[:, k], start=False, stop=True)
                                mm.then_inc(s_ymm, 1)

                    @block.scalar
                    def _(act):
                        act.sem_inc(s_ycp, 2)
                        with act.Fori(0, U // 2) as i:
                            for k in range(2):
                                u = i * 2 + k
                                for b in range(KH):
                                    act.wait_ge(s_hmm, u * KH + b + 1)
                                    if b == 0:
                                        act.wait_ge(s_ymm, u + 2)
                                    nc.scalar.activation(HE[:, b, :], pH[b % 3][:, 0:z.TOK], ACT.Relu,
                                                         bias=b1s[:, k, b:b + 1]).then_inc(s_relu, 1)
                                act.wait_ge(s_ycp, 2 * u + 4)
                                act.dma_start(yd_rows[bass.ds(u * z.TOK, z.TOK), :].rearrange("(a p) d -> p a d", p=P),
                                              YE[:, k]).then_inc(s_store[k], 16)
                        for k in range(2):
                            act.wait_ge(s_store[k], 16 * (U // 2))

                    @block.vector
                    def _(dve):
                        def turn(i, first):
                            for k in range(2):
                                u = i * 2 + k
                                dve.wait_ge(s_turned, u + 1)
                                nc.vector.tensor_copy(XT[:, k], pX[:]).then_inc(s_xt, 1)
                                if not first:
                                    dve.wait_ge(s_store[k], i * 16)
                                dve.wait_ge(s_ymm, u + 3)
                                for h in range(HALVES):
                                    nc.vector.tensor_copy(YE[:, k, h, :], pY[h][:, 0:D]).then_inc(s_ycp, 1)
                        turn(0, True)
                        with dve.Fori(1, U // 2) as i:
                            turn(i, False)

            with ExitStack() as ctx:
                sb, ps, sem = make(ctx)
                Y = sb("Y7", [P, SLOTS, 2, D])
                gidx = sb("gidx", [P, SLOTS, 2], I32)
                s_idx = [sem(f"s_idx7{k}") for k in range(SLOTS)]
                s_added = sem("s_added7")
                s_seen = sem("s_seen7")
                with nc.Block() as block:
                    @block.scalar
                    def _(act):
                        act.sem_inc(s_added, 2 * SLOTS)
                        with act.Fori(0, NT // SLOTS) as i:
                            for k in range(SLOTS):
                                t = bass.ds(i * SLOTS + k, 1)
                                act.wait_ge(s_added, (i * SLOTS + k) * 2 + 2)
                                act.sem_inc(s_seen, 1)
                                nc.scalar.activation(gidx[:, k].unsqueeze(1), pos_f[:, t, :], ACT.Copy)\
                                    .then_inc(s_idx[k], 1)

                    @block.gpsimd
                    def _(pool):
                        with pool.Fori(0, NT // SLOTS) as i:
                            for k in range(SLOTS):
                                pool.wait_ge(s_idx[k], i + 1)
                                pool.sem_inc(s_seen, 1)
                                for c in range(2):
                                    pool.indirect_dma_start(
                                        out=Y[:, k, c, :], out_offset=None, in_=yd_rows,
                                        in_offset=bass.IndirectOffsetOnAxis(ap=gidx[:, k, c:c + 1], axis=0),
                                    ).then_inc(s_got[k], 16)

                    @block.vector
                    def _(dve):
                        with dve.Fori(0, NT // SLOTS) as i:
                            for k in range(SLOTS):
                                t = bass.ds(i * SLOTS + k, 1)
                                dve.wait_ge(s_got[k], i * 32 + 32)
                                for c in range(2):
                                    if c:
                                        dve.wait_ge(s_added, (i * SLOTS + k) * 2 + 2 * SLOTS + 1)
                                    nc.vector.scalar_tensor_tensor(
                                        out=X[:, t, :], in0=Y[:, k, c].unsqueeze(1), scalar=probs[:, c, t],
                                        in1=X[:, t, :], op0=ALU.mult, op1=ALU.add).then_inc(s_added, 1)
        if stop == 7:
            return dump(X)

        clear_spent()
        HW = HC + 1
        GR = HEADS * HW
        late = ExitStack()
        with late:
            sb, ps, sem = make(late)
            ADST = sb("ADST", [P, NT, HEADS])
            with ExitStack() as ctx:
                sb, ps, sem = make(ctx)
                Wrow = sb("Wrow", [P, KD, GR])
                Wd = sb("Wd", [P, KD, HEADS])
                WpT = sb("WpT", [P, KD, D])
                att = sb("att", [P, KD, 2])
                head_of = sb("head_of", [P, KD], I32)
                head_f = sb("head_f", [P, KD])
                hh = sb("hh", [P, HEADS])
                A = sb("A8", [P, KD, 2, HEADS])
                IN = sb("IN8", [P, 2, D])
                HT = sb("HT8", [P, 2, D])
                OUT = sb("OUT8", [P, 2, GR])
                pT = [ps(f"pT8{i}", [P, 512]) for i in range(2)]
                pO = [ps(f"pO8{i}", [P, 512]) for i in range(2)]
                pW = ps("pW8", [P, 512])
                s_w = sem("s_w8")
                s_iota = sem("s_iota8")
                s_A = sem("s_A8")
                s_wmm = sem("s_wmm8")
                s_wcp = sem("s_wcp8")
                s_stat = sem("s_stat8")
                s_var = sem("s_var8")
                s_root = sem("s_root8")
                s_in = sem("s_in8")
                s_turned = sem("s_turned8")
                s_ht = sem("s_ht8")
                s_mm = sem("s_mm8")
                s_cp = sem("s_cp8")
                s_held = sem("s_held8")
                s_store = [sem(f"s_store8{k}") for k in range(2)]
                s_dve = sem("s_dve8")
                with nc.Block() as block:
                    @block.sync
                    def _(sp):
                        sp.dma_start(WpT[:], a["WpT"].rearrange("(k p) n -> p k n", p=P)).then_inc(s_w, 16)
                        sp.dma_start(att[:], a["att"].rearrange("(k p) n -> p k n", p=P)).then_inc(s_w, 16)
                        for m in range(KD):
                            sp.dma_start(Wrow[:, m, :].rearrange("p (h c) -> p h c", c=HW)[:, :, 0:HC],
                                         a["Wp"][m * P:(m + 1) * P, :].rearrange("p (h c) -> p h c", c=HC))\
                                .then_inc(s_w, 16)

                        def store(t, k):
                            sp.wait_ge(s_cp, 2 * t + 6)
                            sp.dma_start(g_rows[bass.ds(t * P, P), :], OUT[:, k]).then_inc(s_store[k], 16)
                        each_tile(sp, store)
                        sp.wait_ge(s_store[0], 16 * ((NT + 1) // 2))
                        sp.wait_ge(s_store[1], 16 * (NT // 2))

                    @block.gpsimd
                    def _(pool):
                        nc.gpsimd.iota(head_of[:], pattern=[[P, KD]], base=0, channel_multiplier=1).then_inc(s_iota, 1)
                        nc.gpsimd.iota(hh[:], pattern=[[1, HEADS]], base=0, channel_multiplier=0,
                                       allow_small_or_imprecise_dtypes=True).then_inc(s_iota, 1)

                    @block.vector
                    def _(dve):
                        loc = Local(dve, s_dve)
                        with dve.Fori(0, NT) as t:
                            nc.vector.bn_stats(stats[:, bass.ds(t, 1), :], X[:, bass.ds(t, 1), :]).then_inc(s_stat, 1)
                        dve.wait_ge(s_iota, 2)
                        loc.link(nc.vector.tensor_single_scalar(head_of[:], head_of[:], HC.bit_length() - 1,
                                                                op=ALU.arith_shift_right))
                        loc.link(nc.vector.tensor_copy(head_f[:], head_of[:]))
                        dve.wait_ge(s_w, 16 * (2 + KD))
                        for m in range(KD):
                            for c in range(2):
                                loc.tick(nc.vector.tensor_scalar(A[:, m, c], hh[:], head_f[:, m:m + 1],
                                                                 att[:, m, c:c + 1], ALU.is_equal, ALU.mult))
                        loc.settle()
                        dve.sem_inc(s_A, 1)
                        dve.wait_ge(s_wmm, 1)
                        pw = pW[:, 0:KD * 2 * HEADS].rearrange("p (k c h) -> p k c h", k=KD, c=2)
                        wr = Wrow[:].rearrange("p k (h c) -> p k h c", c=HW)
                        nc.vector.tensor_copy(wr[:, :, :, HC], pw[:, :, 0, :]).then_inc(s_wcp, 1)
                        nc.vector.tensor_copy(Wd[:], pw[:, :, 1, :]).then_inc(s_wcp, 1)
                        dve.wait_ge(s_stat, NT)
                        ln_moments(loc, s_var)
                        ln_rstd(loc, s_root)
                        dve.sem_inc(s_turned, 2)
                        loc.restart()

                        def tile_in(t, k):
                            dve.wait_ge(s_turned, t + 1)
                            ln_apply(IN[:, k].unsqueeze(1), X[:, bass.ds(t, 1), :], bass.ds(t, 1)).then_inc(s_in, 1)
                        each_tile(dve, tile_in)

                    @block.scalar
                    def _(act):
                        ln_root(act, s_var, s_root)
                        act.sem_inc(s_ht, 2)
                        act.sem_inc(s_cp, 4)
                        act.sem_inc(s_mm, 2)

                        def turned_in(t, k):
                            act.wait_ge(s_turned, t + 3)
                            act.wait_ge(s_mm, t + 1)
                            nc.scalar.activation(HT[:, k], pT[k][:, 0:D], ACT.Copy).then_inc(s_ht, 1)

                        def tile_out(t, k, first=False):
                            act.wait_ge(s_mm, t + 3)
                            if not first:
                                act.wait_ge(s_store[k], (t - k) * 8)
                            nc.scalar.activation(OUT[:, k], pO[k][:, 0:GR], ACT.Copy).then_inc(s_cp, 1)
                            act.sem_inc(s_held, 1)
                            nc.scalar.activation(ADST[:, bass.ds(t, 1), :], pO[k][:, GR:GR + HEADS].unsqueeze(1),
                                                 ACT.Copy).then_inc(s_cp, 1)
                        turned_in(0, 0)
                        for k in range(2):
                            turned_in(k + 1, 1 - k)
                            tile_out(k, k, True)
                        with act.Fori(1, NT // 2) as i:
                            for k in range(2):
                                turned_in(i * 2 + k + 1, 1 - k)
                                tile_out(i * 2 + k, k)
                        tile_out(NT - 1, 0)

                    @block.tensor
                    def _(pe):
                        pe.wait_ge(s_A, 1)
                        for m in range(KD):
                            for j in range(KD):
                                mm = nc.tensor.matmul(pW[:, m * 2 * HEADS:(m + 1) * 2 * HEADS],
                                                      WpT[:, j, m * P:(m + 1) * P],
                                                      A[:, j].rearrange("p c h -> p (c h)"), start=(j == 0), stop=(j == KD - 1))
                        mm.then_inc(s_wmm, 1)
                        pe.wait_ge(s_wcp, 2)

                        def turn(t, k):
                            pe.wait_ge(s_in, t + 1)
                            pe.wait_ge(s_ht, t + 1)
                            for m in range(KD):
                                tr = nc.tensor.transpose(pT[k][:, m * P:(m + 1) * P], IN[:, k, m * P:(m + 1) * P], ident[:])
                            tr.then_inc(s_turned, 1)

                        def proj(t, k):
                            pe.wait_ge(s_ht, t + 3)
                            pe.wait_ge(s_cp, 2 * t + 2)
                            for m in range(KD):
                                nc.tensor.matmul(pO[k][:, 0:GR], HT[:, k, m * P:(m + 1) * P], Wrow[:, m, :],
                                                 start=(m == 0), stop=(m == KD - 1))
                            for m in range(KD):
                                mm = nc.tensor.matmul(pO[k][:, GR:GR + HEADS], HT[:, k, m * P:(m + 1) * P], Wd[:, m, :],
                                                      start=(m == 0), stop=(m == KD - 1))
                            mm.then_inc(s_mm, 1)
                        skewed(pe, turn, proj)

            BC = z.BS * Q
            BR = z.BS * HEADS
            RB = R // z.BS
            FAR = 1e28
            NR = GR + HEADS + 1
            with ExitStack() as ctx:
                sb, ps, sem = make(ctx)
                G = sb("G1", [P, R * Q, GW])
                O = sb("O1", [P, 2, Q, P])
                slot_idx = sb("slot_idx1", [P, R * Q], I32)
                MR = sb("MR", [P, NT, HEADS])
                both = sb("both9", [P, 2, 2, HEADS])
                DR = sb("DR", [BR, z.SE], I32)
                DB = sb("DB", [BR, z.SE])
                FL = sb("FL", [BR, z.SE + 1])
                M1 = sb("M1", [BR, z.SE])
                M2 = sb("M2", [BR, z.SE])
                SCO = sb("SCO", [P, Q, z.BS, HEADS])
                EX = sb("EX", [P, Q, z.BS, HEADS])
                gone = sb("gone", [P, 2])
                df = sb("df", [P, 2, 2, HEADS])
                fac = sb("fac", [P, 2, 2, HEADS])
                TM = sb("TM", [P, 2, GR])
                BANK, BANKS = 512, 4
                pS = ps("pS9", [P, BANKS * BANK])
                pA = ps("pA9", [P, Q * P])
                pM = ps("pM9", [P, 512])
                s_gath = s_gath_l1
                s_pool_idx = [sem(f"s_pidx9{k}") for k in range(R)]
                s_item = sem("s_item9")
                s_oh = sem("s_oh9")
                s_merged = sem("s_merged9")
                s_seen = sem("s_seen9")
                s_dr = sem("s_dr9")
                s_db = sem("s_db9")
                s_fl = sem("s_fl9")
                s_at = sem("s_at9")
                s_sco = sem("s_sco9")
                s_max = sem("s_max9")
                s_mt = sem("s_mt9")
                s_sub = sem("s_sub9")
                s_exp = sem("s_exp9")
                s_prep = sem("s_prep9")
                s_diff = sem("s_diff9")
                s_fac = sem("s_fac9")
                s_dve = sem("s_dve9")

                def batches(eng, body, items):
                    body(0, 0, 0, lambda: None)
                    with eng.Fori(0, z.NB // RB) as i:
                        for k in range(RB):
                            b = i * RB + k + 1
                            body(b, (k + 1) % RB, i + (k + 1) // RB, lambda: items(b - 1))
                    items(z.NB - 1)

                def pairs(eng, b, item):
                    lo = eng.value_load(pair_end[0:1, bass.ds(b, 1)], min_val=0, max_val=z.ITEMS // 2)
                    hi = eng.value_load(pair_end[0:1, bass.ds(b + 1, 1)], min_val=1, max_val=z.ITEMS // 2)
                    with eng.Fori(lo, hi) as i:
                        for k in range(2):
                            item(i * 2 + k, k)

                with nc.Block() as block:
                    @block.gpsimd
                    def _(pool):
                        gather_supers(pool, g_rows, G, GR, slot_idx, s_gath, s_item, s_pool_idx, s_seen)

                    @block.sync
                    def _(sp):
                        def load(b):
                            v = dst_sorted[bass.ds(b * (BC * P), BC * P)].rearrange("(s e) -> s e", s=z.BS)
                            sp.dma_start(DR[:], v.unsqueeze(1).to_broadcast([z.BS, HEADS, z.SE])).then_inc(s_dr, 16)
                        load(0)
                        with sp.Fori(1, z.NB) as b:
                            sp.wait_ge(s_db, b + 0)
                            load(b)

                    @block.tensor
                    def _(pe):
                        def item(w, k):
                            s = load_item(pe, w, 0)
                            pe.wait_ge(s_merged, w + 1)
                            pe.wait_ge(s_oh, w + 1)
                            for q in range(Q):
                                mm = nc.tensor.matmul(pS[:, bass.ds((w % BANKS) * BANK, NR)], O[:, k, q, :],
                                                      G[:, bass.ds((s % R) * Q + q, 1), 0:NR].rearrange("p a d -> p (a d)"),
                                                      start=(q == 0), stop=(q == Q - 1))
                            mm.then_inc(s_item, 1)

                        def items(b):
                            pairs(pe, b, item)

                        def batch(b, k, i, items_before):
                            pe.wait_ge(s_sco, b + 1)
                            for q in range(Q):
                                tr = nc.tensor.transpose(pA[0:BR, q * P:(q + 1) * P],
                                                         SCO[:, q].rearrange("p s h -> p (s h)"), ident[:])
                            tr.then_inc(s_at, 1)
                            pe.wait_ge(s_prep, b + 1)
                            pe.sem_inc(s_seen, 1)
                            items_before()
                            pe.wait_ge(s_max, b + 1)
                            pe.sem_inc(s_seen, 1)
                            for q in range(Q):
                                tr = nc.tensor.transpose(pM[:, q * BR:(q + 1) * BR], M2[:, q * P:(q + 1) * P],
                                                         ident[0:BR, 0:BR])
                            tr.then_inc(s_mt, 1)
                        pe.sem_inc(s_prep, 1)

                        def last_items(b):
                            if isinstance(b, int):
                                pe.wait_ge(s_prep, b + 2)
                            items(b)
                        batches(pe, batch, last_items)

                    @block.scalar
                    def _(act):
                        def item(w, k):
                            act.wait_ge(s_diff, w + 1)
                            nc.scalar.activation(fac[:, k], df[:, k], ACT.Exp).then_inc(s_fac, 1)

                        def batch(b, k, i, items_before):
                            gate = G[:, k * BC:(k + 1) * BC, 0:GR].rearrange("p (s q) (h c) -> p q s h c", q=Q, c=HW)
                            for s in range(z.BS):
                                act.wait_ge(s_gath[k * z.BS + s], i * (16 * Q) + 16 * Q)
                            nc.scalar.activation(SCO[:], gate[:, :, :, :, HC], ACT.Copy).then_inc(s_sco, 1)
                            act.wait_ge(s_dr, b * 16 + 16)
                            act.wait_ge(s_fl, b + 1)
                            nc.scalar.activation(DB[:], DR[:], ACT.Copy, scale=FAR).then_inc(s_db, 1)
                            items_before()
                            act.wait_ge(s_sub, b + 1)
                            nc.scalar.activation(gate[:, :, :, :, HC], EX[:], ACT.Exp).then_inc(s_exp, 1)
                        batches(act, batch, lambda b: pairs(act, b, item))

                    @block.vector
                    def _(dve):
                        loc = Local(dve, s_dve)
                        loc.tick(nc.vector.memset(ACC[:], 0.0))
                        loc.tick(nc.vector.memset(MR[:], -BIG))
                        loc.tick(nc.vector.memset(FL[:, 0:1], -FAR))
                        loc.link(nc.vector.memset(FL[:, z.SE:z.SE + 1], -FAR))
                        dve.sem_inc(s_fl, 1)
                        dve.sem_inc(s_item, 2)
                        dve.sem_inc(s_merged, BANKS)
                        one_hots(dve, O, 0, 0).then_inc(s_oh, 1)
                        one_hots(dve, O, 1, 1).then_inc(s_oh, 1)
                        loc.restart()

                        def pair(w0):
                            J, S = [], []
                            done = {}

                            def step(name, ins):
                                loc.tick(ins)
                                done[name] = loc.n

                            def after(name):
                                dve.wait_ge(s_dve, done[name])

                            def start(k):
                                dve.wait_ge(s_item, w0 + k + 3)
                                step(f"gone{k}", nc.vector.tensor_scalar(gone[:, k:k + 1], S[k][:, GR + HEADS:NR], BIG, -BIG,
                                                                         ALU.mult, ALU.add))

                            def keep(k):
                                step(f"kept{k}", nc.vector.tensor_scalar(both[:, k, 0].unsqueeze(1), MR[:, J[k]], 0.0, None,
                                                                         ALU.add))

                            def item_max(k):
                                after(f"gone{k}")
                                step(f"of_item{k}", nc.vector.scalar_tensor_tensor(
                                    out=both[:, k, 1].unsqueeze(1), in0=S[k][:, GR:GR + HEADS].unsqueeze(1),
                                    scalar=gone[:, k:k + 1], in1=ADST[:, J[k], :], op0=ALU.add, op1=ALU.add))

                            def new_max(k):
                                after(f"kept{k}")
                                after(f"of_item{k}")
                                step(f"max{k}", nc.vector.tensor_tensor(MR[:, J[k]], both[:, k, 1].unsqueeze(1),
                                                                        both[:, k, 0].unsqueeze(1), ALU.max))

                            def differ(k):
                                after(f"max{k}")
                                nc.vector.tensor_tensor(df[:, k], both[:, k], MR[:, J[k]].to_broadcast([P, 2, HEADS]),
                                                        ALU.subtract).then_inc(s_diff, 1)

                            def scale_new(k):
                                dve.wait_ge(s_fac, w0 + k + 1)
                                step(f"new{k}", nc.vector.tensor_tensor(
                                    TM[:, k].rearrange("p (h c) -> p h c", c=HW),
                                    S[k][:, 0:GR].rearrange("p (h c) -> p h c", c=HW),
                                    fac[:, k, 1].unsqueeze(2).to_broadcast([P, HEADS, HW]), ALU.mult))

                            def scale_old(k):
                                acc = ACC[:, J[k], 0:GR].rearrange("p a (h c) -> p (a h) c", c=HW)
                                step(f"old{k}", nc.vector.tensor_tensor(
                                    acc, acc, fac[:, k, 0].unsqueeze(2).to_broadcast([P, HEADS, HW]), ALU.mult))

                            def merge(k):
                                after(f"new{k}")
                                dve.sem_inc(s_merged, 1)
                                after(f"old{k}")
                                acc = ACC[:, J[k], 0:GR]
                                step(f"merged{k}", nc.vector.tensor_tensor(acc, acc, TM[:, k].unsqueeze(1), ALU.add))

                            def blocks(k):
                                one_hots(dve, O, w0 + k + 2, k).then_inc(s_oh, 1)

                            for k in range(2):
                                J.append(bass.ds(load_item(dve, w0 + k, 1), 1))
                                S.append(pS[:, bass.ds(((w0 + k) % BANKS) * BANK, BANK)])
                            start(0)
                            keep(0)
                            blocks(0)
                            item_max(0)
                            start(1)
                            new_max(0)
                            item_max(1)
                            differ(0)
                            keep(1)
                            blocks(1)
                            new_max(1)
                            scale_new(0)
                            differ(1)
                            scale_old(0)
                            merge(0)
                            scale_new(1)
                            after("merged0")
                            scale_old(1)
                            merge(1)
                            loc.restart()

                        def items(b):
                            lo = dve.value_load(pair_end[0:1, bass.ds(b, 1)], min_val=0, max_val=z.ITEMS // 2)
                            hi = dve.value_load(pair_end[0:1, bass.ds(b + 1, 1)], min_val=1, max_val=z.ITEMS // 2)
                            with dve.Fori(lo, hi) as i:
                                pair(i * 2)

                        def batch(b, k, i, items_before):
                            dve.wait_ge(s_db, b + 1)
                            loc.link(nc.vector.tensor_tensor(FL[:, 1:z.SE], DB[:, 0:z.SE - 1], DB[:, 1:z.SE],
                                                             ALU.subtract))
                            dve.sem_inc(s_fl, 1)
                            dve.wait_ge(s_at, b + 1)
                            loc.link(nc.vector.tensor_tensor_scan(M1[:], FL[:, 0:z.SE], pA[0:BR, :], -BIG, ALU.add, ALU.max))
                            loc.link(nc.vector.tensor_tensor_scan(M2[:, ::-1], FL[:, 1:z.SE + 1][:, ::-1], M1[:, ::-1], -BIG,
                                                                  ALU.add, ALU.max))
                            dve.sem_inc(s_max, 1)
                            loc.restart()
                            items_before()
                            dve.wait_ge(s_mt, b + 1)
                            rows = G[:, k * BC:(k + 1) * BC, :]
                            pm = pM[:, 0:Q * BR].rearrange("p (q s h) -> p q s h", q=Q, h=HEADS)
                            last = lastT[:, bass.ds(b * BC, BC)]
                            loc.link(nc.vector.tensor_tensor(EX[:], SCO[:], pm, ALU.subtract))
                            dve.sem_inc(s_sub, 1)
                            by_chunk = "p (s q) h -> p s q h"
                            loc.tick(nc.vector.tensor_tensor(
                                rows[:, :, GR:GR + HEADS].rearrange(by_chunk, q=Q),
                                pM[:, 0:Q * BR].rearrange("p (q s h) -> p s q h", q=Q, h=HEADS),
                                last.unsqueeze(2).to_broadcast([P, BC, HEADS]).rearrange(by_chunk, q=Q), ALU.mult))
                            loc.tick(nc.vector.tensor_scalar(rows[:, :, GR + HEADS], last, 0.0, None, ALU.add))
                            dve.wait_ge(s_exp, b + 1)
                            for s in range(z.BS):
                                c = rows[:, s * Q:(s + 1) * Q, 0:GR].rearrange("p q (h c) -> p q h c", c=HW)
                                loc.tick(nc.vector.tensor_tensor(
                                    c[:, :, :, 0:HC], c[:, :, :, 0:HC],
                                    c[:, :, :, HC:HW].to_broadcast([P, Q, HEADS, HC]), ALU.mult))
                            loc.settle()
                            dve.sem_inc(s_prep, 1)
                            loc.restart()
                        batches(dve, batch, items)

            FE = a["eb3"].shape[0]
            H1, H2, HS = a["eb1"].shape[0], a["eb2"].shape[0], a["sb1"].shape[1]
            G4 = late.enter_context(nc.sbuf_tensor("G4", [P, NT, FE], F32))
            with ExitStack() as ctx:
                sb, ps, sem = make(ctx)
                gW = sb("gW", [P, KD, FE])
                gb = sb("gb", [1, FE])
                RS = sb("RS", [P, NT, HEADS])
                T1 = sb("T1", [P, 2, D])
                IN = sb("IN10", [P, 2, D])
                HT = sb("HT10", [P, 2, D])
                SC = sb("SC10", [P, NT, FE])
                SC2 = sb("SC210", [P, NT, FE])
                eq = sb("eq10", [P, NT, FE])
                km = sb("km10", [P, NT])
                mx = sb("mx10", [P, 2, NT])
                sel = sb("sel10", [P, 2, NT, FE])
                pr = sb("pr10", [P, 2, NT])
                prio = sb("prio10", [P, FE])
                pT = [ps(f"pT10{i}", [P, 512]) for i in range(2)]
                pG = [ps(f"pG10{i}", [P, 512]) for i in range(2)]
                s_w = sem("s_w10")
                s_const = sem("s_const10")
                s_t1 = sem("s_t110")
                s_x3 = sem("s_x310")
                s_stat = sem("s_stat10")
                s_var = sem("s_var10")
                s_root = sem("s_root10")
                s_in = sem("s_in10")
                s_turned = sem("s_turned10")
                s_ht = sem("s_ht10")
                s_kept = sem("s_kept10")
                s_sc = sem("s_sc10")
                s_sccp = sem("s_sccp10")
                s_held = sem("s_held10")
                s_e = sem("s_e10")
                s_ed = sem("s_ed10")
                s_dve = sem("s_dve10")
                with nc.Block() as block:
                    @block.sync
                    def _(sp):
                        sp.dma_start(gW[:], a["gW"].rearrange("(k p) n -> p k n", p=P)).then_inc(s_w, 16)
                        sp.dma_start(gb[:], a["gb"].unsqueeze(0)).then_inc(s_w, 16)

                    @block.gpsimd
                    def _(pool):
                        nc.gpsimd.iota(prio[:], pattern=[[-1, FE]], base=FE, channel_multiplier=0,
                                       allow_small_or_imprecise_dtypes=True).then_inc(s_const, 1)

                    @block.vector
                    def _(dve):
                        loc = Local(dve, s_dve)
                        sums = ACC[:, :, 0:GR].rearrange("p t (h c) -> p t h c", c=HW)
                        loc.link(nc.vector.tensor_scalar(RS[:], sums[:, :, :, HC], 1e-16, None, ALU.add))
                        loc.link(nc.vector.reciprocal(RS[:], RS[:]))
                        dve.sem_inc(s_x3, 2)
                        loc.restart()

                        def add_tile(t, k):
                            one = bass.ds(t, 1)
                            dve.wait_ge(s_x3, t + 1)
                            acc = ACC[:, one, 0:GR].rearrange("p a (h c) -> p (a h) c", c=HW)[:, :, 0:HC]
                            nc.vector.tensor_tensor(T1[:, k].rearrange("p (h c) -> p h c", c=HC), acc,
                                                    RS[:, one, :].rearrange("p a h -> p (a h)").unsqueeze(2)
                                                    .to_broadcast([P, HEADS, HC]), ALU.mult).then_inc(s_t1, 1)
                            dve.wait_ge(s_t1, t + 1)
                            nc.vector.tensor_tensor(X[:, one, :], X[:, one, :], T1[:, k].unsqueeze(1), ALU.add)\
                                .then_inc(s_x3, 1)
                        each_tile(dve, add_tile)
                        dve.wait_ge(s_x3, NT + 2)
                        with dve.Fori(0, NT) as t:
                            nc.vector.bn_stats(stats[:, bass.ds(t, 1), :], X[:, bass.ds(t, 1), :]).then_inc(s_stat, 1)
                        dve.wait_ge(s_stat, NT)
                        ln_moments(loc, s_var)
                        ln_rstd(loc, s_root)
                        dve.sem_inc(s_turned, 2)
                        loc.restart()

                        def tile_in(t, k):
                            dve.wait_ge(s_turned, t + 1)
                            ln_apply(IN[:, k].unsqueeze(1), X[:, bass.ds(t, 1), :], bass.ds(t, 1)).then_inc(s_in, 1)
                        each_tile(dve, tile_in)
                        wide = lambda v: v.unsqueeze(2).to_broadcast([P, NT, FE])
                        dve.wait_ge(s_sccp, NT + 2)
                        dve.wait_ge(s_const, 1)
                        loc.link(nc.vector.tensor_reduce(km[:], SC[:], AX_X, ALU.max))
                        loc.link(nc.vector.tensor_tensor(SC[:], SC[:], wide(km[:]), ALU.subtract))
                        dve.sem_inc(s_e, 1)
                        dve.wait_ge(s_ed, 1)
                        loc.link(nc.vector.tensor_reduce(km[:], SC[:], AX_X, ALU.add))
                        loc.link(nc.vector.reciprocal(km[:], km[:]))
                        loc.link(nc.vector.tensor_tensor(SC[:], SC[:], wide(km[:]), ALU.mult))
                        top_two(loc, SC, SC2, mx, eq, km, sel, prio, FE)
                        loc.link(nc.vector.tensor_tensor(pr[:, 1], mx[:, 1], mx[:, 0], ALU.subtract))
                        dve.sem_inc(s_e, 1)
                        dve.wait_ge(s_ed, 2)
                        loc.link(nc.vector.tensor_scalar(pr[:, 0], pr[:, 1], 1.0, None, ALU.add))
                        loc.link(nc.vector.reciprocal(pr[:, 0], pr[:, 0]))
                        loc.link(nc.vector.tensor_tensor(pr[:, 1], pr[:, 1], pr[:, 0], ALU.mult))
                        loc.tick(nc.vector.tensor_tensor(G4[:], sel[:, 0], wide(pr[:, 0]), ALU.mult))
                        loc.link(nc.vector.tensor_tensor(eq[:], sel[:, 1], wide(pr[:, 1]), ALU.mult))
                        loc.link(nc.vector.tensor_tensor(G4[:], G4[:], eq[:], ALU.add))

                    @block.scalar
                    def _(act):
                        ln_root(act, s_var, s_root)
                        act.sem_inc(s_ht, 2)
                        act.sem_inc(s_kept, 2)
                        act.sem_inc(s_sc, 2)
                        act.sem_inc(s_sccp, 2)

                        def turned_in(t, k):
                            act.wait_ge(s_turned, t + 3)
                            act.wait_ge(s_sc, t + 1)
                            nc.scalar.activation(HT[:, k], pT[k][:, 0:D], ACT.Copy).then_inc(s_ht, 1)
                            act.sem_inc(s_held, 1)
                            nc.scalar.activation(ACC[:, bass.ds(t, 1), 0:D], pT[k][:, 0:D].unsqueeze(1), ACT.Copy)\
                                .then_inc(s_kept, 1)

                        def tile_out(t, k):
                            act.wait_ge(s_sc, t + 3)
                            act.sem_inc(s_held, 1)
                            nc.scalar.activation(SC[:, bass.ds(t, 1), :], pG[k][:, 0:FE].unsqueeze(1), ACT.Copy)\
                                .then_inc(s_sccp, 1)
                        skewed(act, turned_in, tile_out)
                        act.wait_ge(s_e, 1)
                        nc.scalar.activation(SC[:], SC[:], ACT.Exp).then_inc(s_ed, 1)
                        act.wait_ge(s_e, 2)
                        nc.scalar.activation(pr[:, 1], pr[:, 1], ACT.Exp).then_inc(s_ed, 1)

                    @block.tensor
                    def _(pe):
                        pe.wait_ge(s_w, 32)
                        pe.wait_ge(s_in, 1)

                        def turn(t, k):
                            pe.wait_ge(s_in, t + 1)
                            pe.wait_ge(s_kept, t + 1)
                            for m in range(KD):
                                tr = nc.tensor.transpose(pT[k][:, m * P:(m + 1) * P], IN[:, k, m * P:(m + 1) * P], ident[:])
                            tr.then_inc(s_turned, 1)

                        def gate(t, k):
                            pe.wait_ge(s_ht, t + 3)
                            pe.wait_ge(s_sccp, t + 1)
                            for m in range(KD):
                                nc.tensor.matmul(pG[k][:, 0:FE], HT[:, k, m * P:(m + 1) * P], gW[:, m, :],
                                                 start=(m == 0), stop=False)
                            nc.tensor.matmul(pG[k][:, 0:FE], ones[0:1, :], gb[:], start=False, stop=True)\
                                .then_inc(s_sc, 1)
                        skewed(pe, turn, gate)
            if stop == 10:
                return dump(X)

            with ExitStack() as ctx:
                sb, ps, sem = make(ctx)
                NH, NE1 = HS, FE
                sW1 = sb("sW1", [P, KD, HS * P])
                sW2 = sb("sW2", [P, HS, P])
                sW3 = sb("sW3", [P, D])
                eW1 = sb("eW1", [P, KD, FE * H1])
                eW2 = sb("eW2", [P, FE, H2])
                eW3 = sb("eW3", [H2, FE, D])
                sb1 = sb("sb1", [P, HS])
                sb2 = sb("sb2", [P, 1])
                sb3 = sb("sb3", [1, D])
                eb1 = sb("eb1", [P, FE])
                eb2 = sb("eb2", [H2, FE])
                eb3 = sb("eb3", [1, FE, D])
                S1 = sb("S1", [P, HS, P])
                E1 = sb("E1", [P, FE, P])
                S2 = sb("S2", [P, P])
                E2 = sb("E2", [H2, FE, P])
                pS1 = ps("pS111", [P, HS, P])
                pE1 = ps("pE111", [P, FE, P])
                pS2 = ps("pS211", [P, 512])
                pE2 = ps("pE211", [P, FE, P])
                pSo = ps("pSo11", [P, 512])
                pEo = [ps(f"pEo11{i}", [P, 2, D]) for i in range(2)]
                s_w = sem("s_w11")
                s_l1 = sem("s_l111")
                s_r1 = sem("s_r111")
                s_l2 = sem("s_l211")
                s_r2 = sem("s_r211")
                s_l3 = sem("s_l311")
                s_add = sem("s_add11")
                s_store = sem("s_store11")
                assert H1 == P and FE == 4
                with nc.Block() as block:
                    @block.sync
                    def _(sp):
                        loads = [(sW1[:], a["sW1"].rearrange("(k p) n -> p k n", p=P)),
                                 (sW2[:], a["sW2"].rearrange("(k p) n -> p k n", p=P)), (sW3[:], a["sW3"]),
                                 (eW1[:], a["eW1"].rearrange("(k p) n -> p k n", p=P)),
                                 (eW2[:], a["eW2"].rearrange("p (e n) -> p e n", e=FE)),
                                 (eW3[:], a["eW3"].rearrange("p (e n) -> p e n", e=FE)),
                                 (sb1[:], a["sb1"]), (sb2[:], a["sb2"]), (sb3[:], a["sb3"].unsqueeze(0)),
                                 (eb1[:], a["eb1"]), (eb2[:], a["eb2"]), (eb3[:], a["eb3"].unsqueeze(0))]
                        for o_, i_ in loads:
                            sp.dma_start(o_, i_).then_inc(s_w, 16)
                        with sp.Fori(0, FULL) as t:
                            sp.wait_ge(s_add, (t + 1) * (FE + 1) + 1)
                            sp.dma_start(out[bass.ds(t * P, P), :], X[:, bass.ds(t, 1), :].rearrange("p a d -> p (a d)"))\
                                .then_inc(s_store, 16)
                        sp.wait_ge(s_add, NT * (FE + 1) + 1)
                        sp.dma_start(out[FULL * P:N, :], X[0:REST, FULL, :]).then_inc(s_store, 16)
                        sp.wait_ge(s_store, 16 * NT)

                    @block.tensor
                    def _(pe):
                        pe.wait_ge(s_w, 16 * 12)

                        def tile(t):
                            h = lambda m: ACC[:, bass.ds(t, 1), m * P:(m + 1) * P].rearrange("p a d -> p (a d)")
                            pe.wait_ge(s_r1, t * (HS + FE) + 1)
                            for b in range(HS):
                                for m in range(KD):
                                    mm = nc.tensor.matmul(pS1[:, b, :], sW1[:, m, b * P:(b + 1) * P], h(m),
                                                          start=(m == 0), stop=(m == KD - 1))
                                mm.then_inc(s_l1, 1)
                            for e in range(FE):
                                for m in range(KD):
                                    mm = nc.tensor.matmul(pE1[:, e, :], eW1[:, m, e * P:(e + 1) * P], h(m),
                                                          start=(m == 0), stop=(m == KD - 1))
                                mm.then_inc(s_l1, 1)
                            pe.wait_ge(s_r2, t * (1 + FE) + 1)
                            pe.wait_ge(s_r1, t * (HS + FE) + 1 + HS)
                            for b in range(HS):
                                mm = nc.tensor.matmul(pS2[:, 0:P], sW2[:, b, :], S1[:, b, :],
                                                      start=(b == 0), stop=(b == HS - 1))
                            mm.then_inc(s_l2, 1)
                            for e in range(FE):
                                pe.wait_ge(s_r1, t * (HS + FE) + 1 + HS + e + 1)
                                nc.tensor.matmul(pE2[0:H2, e, :], eW2[:, e, :], E1[:, e, :], start=True, stop=True)\
                                    .then_inc(s_l2, 1)
                            pe.wait_ge(s_add, t * (FE + 1) + 1)
                            pe.wait_ge(s_r2, t * (1 + FE) + 2)
                            nc.tensor.matmul(pSo[:, 0:D], S2[:], sW3[:], start=True, stop=False)
                            nc.tensor.matmul(pSo[:, 0:D], ones[0:1, :], sb3[:], start=False, stop=True).then_inc(s_l3, 1)
                            for e in range(FE):
                                pe.wait_ge(s_r2, t * (1 + FE) + 3 + e)
                                nc.tensor.matmul(pEo[e // 2][:, e % 2, :], E2[:, e, :], eW3[:, e, :], start=True, stop=False)
                                nc.tensor.matmul(pEo[e // 2][:, e % 2, :], ones[0:1, :], eb3[:, e, :], start=False, stop=True)\
                                    .then_inc(s_l3, 1)
                        with pe.Fori(0, NT) as t:
                            tile(t)

                    @block.scalar
                    def _(act):
                        act.sem_inc(s_r1, 1)
                        act.sem_inc(s_r2, 1)
                        act.wait_ge(s_w, 16 * 12)
                        with act.Fori(0, NT) as t:
                            for b in range(HS + FE):
                                if b in (0, HS):
                                    act.wait_ge(s_l1, t * (HS + FE) + (HS if b == 0 else HS + FE))
                                o_, i_, bi = ((S1[:, b], pS1[:, b], sb1[:, b:b + 1]) if b < HS else
                                              (E1[:, b - HS], pE1[:, b - HS], eb1[:, b - HS:b - HS + 1]))
                                nc.scalar.activation(o_, i_, ACT.Relu, bias=bi).then_inc(s_r1, 1)
                            for e in range(-1, FE):
                                if e < 1:
                                    act.wait_ge(s_l2, t * (1 + FE) + (1 if e < 0 else 1 + FE))
                                o_, i_, bi = ((S2[:], pS2[:, 0:P], sb2[:, 0:1]) if e < 0 else
                                              (E2[:, e], pE2[0:H2, e], eb2[:, e:e + 1]))
                                nc.scalar.activation(o_, i_, ACT.Relu, bias=bi).then_inc(s_r2, 1)

                    @block.vector
                    def _(dve):
                        dve.sem_inc(s_add, 1)
                        with dve.Fori(0, NT) as t:
                            one = bass.ds(t, 1)
                            dve.wait_ge(s_l3, t * (FE + 1) + 1)
                            nc.vector.tensor_tensor(X[:, one, :], X[:, one, :], pSo[:, 0:D].unsqueeze(1), ALU.add)\
                                .then_inc(s_add, 1)
                            for e in range(FE):
                                if e % 2 == 0:
                                    dve.wait_ge(s_l3, t * (FE + 1) + 3 + e)
                                dve.wait_ge(s_add, t * (FE + 1) + 2 + e)
                                nc.vector.scalar_tensor_tensor(
                                    out=X[:, one, :], in0=pEo[e // 2][:, e % 2, :].unsqueeze(1), scalar=G4[:, one, e],
                                    in1=X[:, one, :], op0=ALU.mult, op1=ALU.add).then_inc(s_add, 1)


def kernel(**inputs):
    import numpy as _np
    import concourse.bacc as _bacc
    from concourse import mybir as _mybir
    from concourse.bass_utils import run_bass_kernel_spmd as _run

    nc = _bacc.Bacc("TRN2", target_bir_lowering=False, num_devices=1)
    a = {k: _np.asarray(v) for k, v in inputs.items()}
    ne, hid, d = a["L0_ffn_W1"].shape
    heads, hc = a["L1_gnn_a_src"].shape
    z = Sizes(a["x"].shape[0], a["x"].shape[1], a["src"].shape[0], ne, hid, heads)
    t_ = lambda v, *axes: _np.transpose(v, axes)
    blocks = lambda v: t_(v.reshape(ne, -1, P, v.shape[-1]), 0, 2, 1, 3).reshape(ne, P, -1)
    laid = {
        "x": a["x"], "src": a["src"], "dst": a["dst"],
        "W0": a["L0_gnn_W"], "b0": a["L0_gnn_b"],
        "WgT": a["L0_ffn_Wg"].T, "bg": a["L0_ffn_bg"],
        "W1": blocks(t_(a["L0_ffn_W1"], 0, 2, 1)),
        "b1": t_(a["L0_ffn_b1"].reshape(ne, hid // P, P), 0, 2, 1),
        "W2": blocks(t_(a["L0_ffn_W2"], 0, 2, 1)),
        "b2": a["L0_ffn_b2"],
        "Wp": a["L1_gnn_W"], "WpT": a["L1_gnn_W"].T,
        "att": _np.stack([a["L1_gnn_a_src"].reshape(-1), a["L1_gnn_a_dst"].reshape(-1)], 1),
        "sW1": a["L1_ffn_sW1"], "sb1": a["L1_ffn_sb1"].reshape(-1, P).T,
        "sW2": a["L1_ffn_sW2"], "sb2": a["L1_ffn_sb2"].reshape(-1, P).T,
        "sW3": a["L1_ffn_sW3"], "sb3": a["L1_ffn_sb3"],
        "eW1": t_(a["L1_ffn_eW1"], 1, 0, 2).reshape(d, -1), "eb1": a["L1_ffn_eb1"].T,
        "eW2": t_(a["L1_ffn_eW2"], 1, 0, 2).reshape(P, -1), "eb2": a["L1_ffn_eb2"].T,
        "eW3": t_(a["L1_ffn_eW3"], 1, 0, 2).reshape(a["L1_ffn_eW3"].shape[1], -1), "eb3": a["L1_ffn_eb3"],
        "gW": a["L1_ffn_gW"], "gb": a["L1_ffn_gb"],
    }
    arrays, aps = {}, {}
    for name, v in laid.items():
        v = _np.ascontiguousarray(v)
        arrays[f"in_{name}_dram"] = v
        aps[name] = nc.dram_tensor(f"in_{name}_dram", v.shape, _mybir.dt.from_np(v.dtype), kind="ExternalInput").ap()
    out = nc.dram_tensor("out_0_dram", a["x"].shape, F32, kind="ExternalOutput").ap()
    build(nc, STOP, z, aps, out)
    r = _run(nc, [arrays], core_ids=[0])
    return r.results[0]["out_0_dram"]
```

```python
from contextlib import ExitStack

import concourse.bass as bass
from concourse import mybir

P = 128
ALU = mybir.AluOpType
ACT = mybir.ActivationFunctionType
AX_X = mybir.AxisListType.X
F32 = mybir.dt.float32
I32 = mybir.dt.int32

LN_EPS = 1e-5
NORM_EPS = 1e-12
BIG = 1e30
UNROLL = 7
DEEP = 4
FAR = 1e28
STOP = 99


class Sizes:

    def __init__(self, n_nodes, d, n_edges, n_exp, hid, heads):
        self.N, self.D, self.E = n_nodes, d, n_edges
        self.NT = -(-n_nodes // P)
        self.NPAD = self.NT * P
        self.KD = d // P
        self.Q = 8
        self.SE = self.Q * P
        self.NS = -(-n_edges // self.SE)
        self.RG = -(-self.NS * self.Q // P)
        self.EPAD = (self.RG * P + 1) * P
        self.R = 8
        self.ITEMS = self.NS + self.NT - 1
        self.TABW = self.ITEMS + 4
        self.SRANGE = self.NS + 4
        self.BS = 2
        self.NB = self.NS // self.BS
        self.NE, self.HID = n_exp, hid
        self.KH = hid // P
        self.HEADS = heads
        self.TOK = 256
        self.ET = (2 * self.NPAD + n_exp * (self.TOK - 1)) // self.TOK
        self.LEAST = n_nodes * 2 // (8 * self.TOK) * 8
        self.NEVER = 8191
        assert self.ITEMS % 2 == 0 and self.NS % self.BS == 0 and self.R == 4 * self.BS and self.NB > 4 and self.NT % 2 and self.NEVER >= self.NPAD


class Local:

    def __init__(self, eng, sem):
        self.eng, self.sem, self.n = eng, sem, 0

    def tick(self, ins):
        ins.then_inc(self.sem, 1)
        self.n += 1

    def settle(self):
        self.eng.wait_ge(self.sem, self.n)

    def link(self, ins):
        self.tick(ins)
        self.settle()

    def restart(self):
        if self.n:
            self.settle()
            self.eng.sem_clear(self.sem)
            self.n = 0


def build(nc, stop, z, a, out):
    N, D, NT, KD, Q, NS, R = z.N, z.D, z.NT, z.KD, z.Q, z.NS, z.R
    FULL = N // P
    REST = N - FULL * P
    HEADS, HC = z.HEADS, z.D // z.HEADS
    GW = D + 2 * HEADS + 2

    def scratch(name, shape, dt):
        return nc.dram_tensor(name, shape, dt).ap()

    src_sorted = scratch("src_sorted", (z.EPAD,), I32)
    dst_sorted = scratch("dst_sorted", (z.EPAD,), I32)
    seg_gaps = scratch("seg_gaps", (z.RG * P * P,), F32)
    node_count = scratch("node_count", (z.NEVER + 1, 1), F32)
    node_start = scratch("node_start", (z.NEVER + 1, 1), F32)
    h0_rows = scratch("h0_rows", (z.NPAD, D), F32)
    xd_rows = scratch("xd_rows", ((z.ET + 4) * z.TOK, D), F32)
    yd_rows = scratch("yd_rows", (z.ET * z.TOK, D), F32)
    g_rows = scratch("g_rows", (z.NPAD, D + HEADS), F32)

    spent = []

    def clear_spent():
        nums = sorted(set(spent))
        firsts = [n for n in nums if n - 1 not in nums]
        lasts = [n for n in nums if n + 1 not in nums]
        with nc.Block() as block:
            @block.sync
            def _(sp):
                for lo, hi in zip(firsts, lasts):
                    sp.sem_clear(range(lo, hi + 1))
        spent.clear()

    top = ExitStack()

    def make(ctx):
        def sb(name, shape, dt=F32):
            return ctx.enter_context(nc.sbuf_tensor(name, shape, dt))

        def ps(name, shape, dt=F32):
            return ctx.enter_context(nc.psum_tensor(name, shape, dt))

        def sem(name):
            one = ctx.enter_context(nc.semaphore(name))
            spent.append(one.num)
            return one

        return sb, ps, sem

    with top:
        sb, _, sem = make(top)
        s_gath_l0 = [sem(f"s_gath_l0_{k}") for k in range(R)]
        s_gath_l1 = [sem(f"s_gath_l1_{k}") for k in range(R)]
        s_sent = [sem(f"s_sent{k}") for k in range(7)]
        s_got = [sem(f"s_got{k}") for k in range(7)]
        s_sort = [sem(f"s_sort{k}") for k in range(4)]
        spent.clear()
        X = sb("X", [P, NT, D])
        ACC = sb("ACC", [P, NT, D + HEADS])
        ident = sb("ident", [P, P])
        ones = sb("ones", [P, P])
        iota_n = sb("iota_n", [P, P])
        srcT = sb("srcT", [P, z.RG * P], I32)
        dstT = sb("dstT", [P, z.RG * P])
        lastT = sb("lastT", [P, z.RG * P])
        tab = sb("tab", [1, z.TABW, 2], I32)
        packed = sb("packed", [1, z.ITEMS // 2], I32)
        free_at = sb("free_at", [1, NS], I32)
        tile_base = sb("tile_base", [P, z.TABW])
        pair_end = sb("pair_end", [1, z.NB + 1], I32)

        stats = sb("stats", [P, NT, 6])
        mean = sb("mean", [P, NT])
        rstd = sb("rstd", [P, NT])
        lnt = sb("lnt", [P, 3, NT])

        def ln_moments(loc, s_var):
            me, vo = stats[:, :, 1], stats[:, :, 5]
            mo, ve = stats[:, :, 4], stats[:, :, 2]
            loc.tick(nc.vector.tensor_tensor(lnt[:, 0], me, mo, ALU.add))
            loc.tick(nc.vector.tensor_tensor(lnt[:, 1], me, mo, ALU.subtract))
            loc.link(nc.vector.tensor_tensor(lnt[:, 2], ve, vo, ALU.add))
            loc.tick(nc.vector.tensor_scalar(mean[:], lnt[:, 0], 0.5, None, ALU.mult))
            loc.link(nc.vector.scalar_tensor_tensor(out=lnt[:, 1], in0=lnt[:, 1], scalar=0.25, in1=lnt[:, 1],
                                                    op0=ALU.mult, op1=ALU.mult))
            loc.link(nc.vector.scalar_tensor_tensor(out=lnt[:, 1], in0=lnt[:, 2], scalar=1.0 / D, in1=lnt[:, 1],
                                                    op0=ALU.mult, op1=ALU.add))
            loc.tick(nc.vector.tensor_scalar(lnt[:, 0], lnt[:, 1], LN_EPS, None, ALU.add))
            loc.settle()
            nc.vector.sem_inc(s_var, 1)

        def ln_root(act, s_var, s_root):
            act.wait_ge(s_var, 1)
            nc.scalar.activation(lnt[:, 2], lnt[:, 0], ACT.Sqrt).then_inc(s_root, 1)

        def ln_rstd(loc, s_root):
            loc.eng.wait_ge(s_root, 1)
            loc.link(nc.vector.reciprocal(rstd[:], lnt[:, 2]))

        def ln_apply(out_ap, in_ap, t):
            return nc.vector.tensor_scalar(out_ap, in_ap, mean[:, t], rstd[:, t], ALU.subtract, ALU.mult)

        def each_tile(eng, body, depth=2):
            with eng.Fori(0, NT // depth) as i:
                for k in range(depth):
                    body(i * depth + k, k)
            for t in range(NT // depth * depth, NT):
                body(t, t % depth)

        def all_stats(dve, s_stat):
            each_tile(dve, lambda t, k: nc.vector.bn_stats(
                stats[:, bass.ds(t, 1), :], X[:, bass.ds(t, 1), :]).then_inc(s_stat, 1), UNROLL)

        LISTS = ((src_sorted, 0), (dst_sorted, 0), (dst_sorted, 1))
        LLEN = z.RG * P * P
        NTURN = len(LISTS) * z.RG
        edge = ExitStack()
        with edge:
            sb, ps, sem = make(edge)
            rows_i = sb("rows_i", [P, 3, z.RG, P], I32)
            rows_f = sb("rows_f", [P, 3, z.RG, P])
            gaps = sb("gaps", [P, z.RG, P])
            q_last = sb("q_last", [P, 1])
            viol = sb("viol", [P, 1])
            unsorted = sb("unsorted", [1, 1], I32)
            pT = [ps(f"pT{i}", [P, 4 * P]) for i in range(2)]

            def load_lists(sp, s_rows):
                for n, (lst, off) in enumerate(LISTS):
                    sp.dma_start(rows_i[:, n, :, :], lst[off:off + LLEN].rearrange("(g p e) -> p g e", p=P, e=P))\
                        .then_inc(s_rows, 16)

            def rows_ready(loc, s_rows, s_rowsf):
                loc.eng.wait_ge(s_rows, 16 * len(LISTS))
                loc.link(nc.vector.tensor_copy(rows_f[:], rows_i[:]))
                loc.link(nc.vector.tensor_tensor(rows_i[:, 0], rows_f[:, 1], rows_f[:, 2], ALU.is_gt))
                loc.link(nc.vector.tensor_reduce(viol[:], rows_i[:, 0].rearrange("p g e -> p (g e)"), AX_X, ALU.max))
                loc.link(nc.vector.tensor_tensor(rows_f[:, 2], rows_f[:, 1], rows_f[:, 2], ALU.not_equal))
                loc.link(nc.vector.tensor_scalar(rows_f[:, 2, :, P - 1:P], rows_f[:, 2, :, P - 1:P], q_last[:, 0:1],
                                                 None, ALU.max))
                loc.link(nc.vector.tensor_scalar(gaps[:], rows_f[:, 2], -FAR, None, ALU.mult))
                loc.eng.sem_inc(s_rowsf, 1)

            def store_gaps(sp, s_rowsf, s_gaps):
                sp.wait_ge(s_rowsf, 1)
                sp.dma_start(seg_gaps.rearrange("(g p e) -> p g e", p=P, e=P), gaps[:]).then_inc(s_gaps, 16)
                sp.wait_ge(s_gaps, 16)

            def turn_lists(pe, s_rowsf, s_turned, s_copied):
                pe.wait_ge(s_rowsf, 1)
                for t in range(NTURN):
                    n, g = divmod(t, z.RG)
                    if t >= 2:
                        pe.wait_ge(s_copied, t - 1)
                    nc.tensor.transpose(pT[t % 2][:, 0:P], rows_f[:, n, g, :], ident[:]).then_inc(s_turned, 1)

            def copy_lists(dve, s_turned, s_copied):
                for t in range(NTURN):
                    n, g = divmod(t, z.RG)
                    dve.wait_ge(s_turned, t + 1)
                    nc.vector.tensor_copy((srcT, dstT, lastT)[n][:, g * P:(g + 1) * P], pT[t % 2][:, 0:P])\
                        .then_inc(s_copied, 1)
                dve.wait_ge(s_copied, NTURN)

            with ExitStack() as ctx:
                sb, ps, sem = make(ctx)
                pads = sb("pads", [16, 2, (z.EPAD - z.E) // 16], I32)
                q_last_i = sb("q_last_i", [P, 1], I32)
                pV = ps("pV", [P, 512])
                s_x = sem("s_x")
                s_pads = sem("s_pads")
                s_lists = sem("s_lists")
                s_rows = sem("s_rows")
                s_const = sem("s_const")
                s_rowsf = sem("s_rowsf")
                s_gaps = sem("s_gaps")
                s_turned = sem("s_turned")
                s_copied = sem("s_copied")
                s_viol = sem("s_viol")
                s_stat = sem("s_stat")
                s_var = sem("s_var")
                s_root = sem("s_root")
                s_h0 = sem("s_h0")
                s_h0st = sem("s_h0st")
                s_dve = sem("s_dve")
                s_pool = sem("s_pool")
                with nc.Block() as block:
                    @block.sync
                    def _(sp):
                        for lst, name in ((src_sorted, "src"), (dst_sorted, "dst")):
                            sp.dma_start(lst[0:z.E].rearrange("(a b) -> a b", a=16),
                                         a[name].rearrange("(a b) -> a b", a=16)).then_inc(s_lists, 16)
                        sp.dma_start(X[:, 0:FULL, :], a["x"][0:FULL * P, :].rearrange("(t p) d -> p t d", p=P))\
                            .then_inc(s_x, 16)
                        sp.wait_ge(s_const, 1)
                        sp.dma_start(X[0:REST, FULL, :], a["x"][FULL * P:N, :]).then_inc(s_x, 16)
                        sp.wait_ge(s_pads, 2)
                        for n, lst in enumerate((src_sorted, dst_sorted)):
                            sp.dma_start(lst[z.E:z.EPAD].rearrange("(a b) -> a b", a=16), pads[:, n, :])\
                                .then_inc(s_lists, 16)
                        sp.wait_ge(s_lists, 64)
                        load_lists(sp, s_rows)
                        assert NT % UNROLL == 0
                        for t in range(0, NT, UNROLL):
                            sp.wait_ge(s_h0, t + UNROLL)
                            sp.dma_start(h0_rows[t * P:(t + UNROLL) * P, :].rearrange("(t p) d -> p t d", p=P),
                                         ACC[:, t:t + UNROLL, 0:D]).then_inc(s_h0st, 16)
                        store_gaps(sp, s_rowsf, s_gaps)
                        sp.wait_ge(s_h0st, 16 * (NT // UNROLL))

                    @block.gpsimd
                    def _(pool):
                        loc = Local(pool, s_pool)
                        nc.gpsimd.memset(X[:, FULL, :], 0.0).then_inc(s_const, 1)
                        nc.gpsimd.memset(pads[:, 0, :], 0).then_inc(s_pads, 1)
                        nc.gpsimd.memset(pads[:, 1, :], z.NEVER).then_inc(s_pads, 1)
                        loc.link(nc.gpsimd.memset(ident[:], 0.0))
                        nc.gpsimd.affine_select(out=ident[:], in_=ident[:], compare_op=ALU.not_equal, fill=1.0,
                                                base=0, pattern=[[-1, P]], channel_multiplier=1)\
                            .then_inc(s_const, 1)
                        nc.gpsimd.memset(ones[:], 1.0).then_inc(s_const, 1)
                        nc.gpsimd.iota(iota_n[:], pattern=[[1, P]], base=0, channel_multiplier=0,
                                       allow_small_or_imprecise_dtypes=True).then_inc(s_const, 1)
                        nc.gpsimd.iota(q_last_i[:], pattern=[[1, 1]], base=0, channel_multiplier=1)\
                            .then_inc(s_const, 1)

                    @block.scalar
                    def _(act):
                        ln_root(act, s_var, s_root)

                    @block.vector
                    def _(dve):
                        loc = Local(dve, s_dve)
                        dve.wait_ge(s_const, 5)
                        loc.link(nc.vector.tensor_single_scalar(q_last_i[:], q_last_i[:], Q - 1, op=ALU.bitwise_and))
                        loc.link(nc.vector.tensor_single_scalar(q_last[:], q_last_i[:], Q - 1, op=ALU.is_equal))
                        dve.wait_ge(s_x, 32)
                        all_stats(dve, s_stat)
                        dve.wait_ge(s_stat, NT)
                        ln_moments(loc, s_var)
                        ln_rstd(loc, s_root)
                        each_tile(dve, lambda t, k: ln_apply(ACC[:, bass.ds(t, 1), 0:D], X[:, bass.ds(t, 1), :],
                                                             bass.ds(t, 1)).then_inc(s_h0, 1), UNROLL)
                        rows_ready(loc, s_rows, s_rowsf)
                        copy_lists(dve, s_turned, s_copied)
                        dve.wait_ge(s_viol, 1)
                        loc.link(nc.vector.tensor_scalar(unsorted[:], pV[0:1, 0:1], 1.0, None, ALU.min))

                    @block.tensor
                    def _(pe):
                        pe.wait_ge(s_const, 3)
                        turn_lists(pe, s_rowsf, s_turned, s_copied)
                        nc.tensor.matmul(pV[:, 0:1], ones[:], viol[:], start=True, stop=True).then_inc(s_viol, 1)

            CHUNKS = -(-z.E // P)
            NODES = z.NEVER + 1
            PER = NODES // P
            with ExitStack() as ctx:
                sb, ps, sem = make(ctx)
                rank = sb("rank", [P, CHUNKS])
                lower = sb("lower", [P, P])
                below = sb("below1", [P, P])
                col = sb("col", [P, 1])
                diag = sb("diag", [P, P])
                same = sb("same", [P, P])
                r_in = sb("r_in", [P, 1])
                n_in = sb("n_in", [P, 1])
                got = sb("got", [P, 1])
                put = sb("put", [P, 1])
                cidx = sb("cidx", [P, 1], I32)
                pidx = sb("pidx", [P, 1], I32)
                fidx = sb("fidx", [P, 1])
                pay = sb("pay", [P, 2], I32)
                counts = sb("counts", [P, PER])
                starts = sb("starts", [P, PER])
                off = sb("off", [P, 1])
                pB = ps("pB1", [P, 512])
                pP = ps("pP1", [P, 512])
                s_ones = sem("s_ones1")
                s_cz = sem("s_cz")
                s_set = sem("s_set1")
                s_a = sem("s_a1")
                s_b = sem("s_b1")
                s_cur = s_sort[0]
                s_put = s_sort[1]
                s_start = s_sort[2]
                s_move = s_sort[3]
                s_c = sem("s_c1")
                s_done = sem("s_done1")
                s_seen = sem("s_seen1")
                s_cl = sem("s_cl1")
                s_tot = sem("s_tot1")
                s_off = sem("s_off1")
                s_st = sem("s_st1")
                s_stw = sem("s_stw1")
                s_p = sem("s_p1")
                s_q = sem("s_q1")
                s_moved = sem("s_moved1")
                s_rows = sem("s_rows1")
                s_rowsf = sem("s_rowsf1")
                s_gaps = sem("s_gaps1")
                s_turned = sem("s_turned1")
                s_copied = sem("s_copied1")
                s_dve = sem("s_dve1")
                s_pool = sem("s_pool1")
                flag = lambda eng: eng.value_load(unsorted[0:1, 0:1], min_val=0, max_val=1)
                with nc.Block() as block:
                    @block.sync
                    def _(sp):
                        with sp.If(flag(sp)):
                            sp.wait_ge(s_set, 1)
                            sp.dma_start(node_count.rearrange("(p c) a -> p (c a)", p=P), counts[:]).then_inc(s_cz, 16)
                            sp.wait_ge(s_done, CHUNKS + 1)
                            sp.dma_start(counts[:], node_count.rearrange("(p c) a -> p (c a)", p=P)).then_inc(s_cl, 16)
                            sp.wait_ge(s_st, 1)
                            sp.dma_start(node_start.rearrange("(p c) a -> p (c a)", p=P), starts[:]).then_inc(s_stw, 16)
                            sp.wait_ge(s_stw, 16)
                            sp.wait_ge(s_moved, CHUNKS + 1)
                            load_lists(sp, s_rows)
                            store_gaps(sp, s_rowsf, s_gaps)

                    @block.gpsimd
                    def _(pool):
                        with pool.If(flag(pool)):
                            loc = Local(pool, s_pool)
                            nc.gpsimd.affine_select(out=lower[:], in_=ones[:], compare_op=ALU.is_ge, fill=0.0,
                                                    base=-1, pattern=[[-1, P]], channel_multiplier=1).then_inc(s_ones, 1)
                            nc.gpsimd.affine_select(out=below[:], in_=ones[:], compare_op=ALU.is_ge, fill=0.0,
                                                    base=-1, pattern=[[1, P]], channel_multiplier=-1).then_inc(s_ones, 1)
                            pool.wait_ge(s_cz, 16)
                            pool.sem_inc(s_done, 1)
                            with pool.Fori(0, CHUNKS) as c:
                                pool.wait_ge(s_a, c + 1)
                                pool.sem_inc(s_seen, 1)
                                pool.indirect_dma_start(
                                    out=got[:], out_offset=None, in_=node_count,
                                    in_offset=bass.IndirectOffsetOnAxis(ap=cidx[:, 0:1], axis=0)).then_inc(s_cur, 16)
                                pool.wait_ge(s_c, c + 1)
                                pool.sem_inc(s_seen, 1)
                                pool.indirect_dma_start(
                                    out=node_count, in_=put[:], in_offset=None,
                                    out_offset=bass.IndirectOffsetOnAxis(ap=pidx[:, 0:1], axis=0),
                                    bounds_check=NODES - 1, oob_is_err=False).then_inc(s_put, 16)
                                pool.wait_ge(s_put, c * 16 + 16)
                                pool.sem_inc(s_done, 1)
                            pool.wait_ge(s_stw, 16)
                            pool.sem_inc(s_moved, 1)
                            with pool.Fori(0, CHUNKS) as c:
                                pool.wait_ge(s_p, c + 1)
                                pool.sem_inc(s_seen, 1)
                                pool.indirect_dma_start(
                                    out=got[:], out_offset=None, in_=node_start,
                                    in_offset=bass.IndirectOffsetOnAxis(ap=cidx[:, 0:1], axis=0)).then_inc(s_start, 16)
                                pool.wait_ge(s_q, c + 1)
                                pool.sem_inc(s_seen, 1)
                                for n, lst in enumerate((src_sorted, dst_sorted)):
                                    pool.indirect_dma_start(
                                        out=lst.unsqueeze(1), in_=pay[:, n:n + 1], in_offset=None,
                                        out_offset=bass.IndirectOffsetOnAxis(ap=pidx[:, 0:1], axis=0)).then_inc(s_move, 16)
                                pool.wait_ge(s_move, c * 32 + 32)
                                pool.sem_inc(s_moved, 1)

                    @block.tensor
                    def _(pe):
                        with pe.If(flag(pe)):
                            with pe.Fori(0, CHUNKS) as c:
                                pe.wait_ge(s_a, c + 1)
                                nc.tensor.matmul(pB[:, 0:P], ones[:], diag[:], start=True, stop=True).then_inc(s_b, 1)
                            pe.wait_ge(s_ones, 2)
                            pe.wait_ge(s_tot, 1)
                            nc.tensor.matmul(pP[:, 0:1], below[:], off[:], start=True, stop=True).then_inc(s_off, 1)
                            turn_lists(pe, s_rowsf, s_turned, s_copied)

                    @block.vector
                    def _(dve):
                        with dve.If(flag(dve)):
                            loc = Local(dve, s_dve)
                            loc.link(nc.vector.memset(counts[:], 0.0))
                            dve.sem_inc(s_set, 1)
                            dve.wait_ge(s_ones, 2)
                            loc.restart()
                            with dve.Fori(0, CHUNKS) as c:
                                dve.wait_ge(s_done, c + 1)
                                loc.link(nc.vector.tensor_scalar(col[:], dstT[:, bass.ds(c, 1)], 0.0, None, ALU.add))
                                loc.tick(nc.vector.tensor_copy(cidx[:], col[:]))
                                loc.link(nc.vector.tensor_scalar(diag[:], ident[:], col[:, 0:1], None, ALU.mult))
                                dve.sem_inc(s_a, 1)
                                dve.wait_ge(s_b, c + 1)
                                loc.link(nc.vector.tensor_scalar(same[:], pB[:, 0:P], col[:, 0:1], None, ALU.is_equal))
                                loc.tick(nc.vector.tensor_reduce(n_in[:], same[:], AX_X, ALU.add))
                                loc.link(nc.vector.tensor_tensor(diag[:], same[:], lower[:], ALU.mult))
                                loc.link(nc.vector.tensor_reduce(r_in[:], diag[:], AX_X, ALU.add))
                                loc.link(nc.vector.tensor_tensor(fidx[:], n_in[:], r_in[:], ALU.subtract))
                                loc.link(nc.vector.tensor_scalar(fidx[:], fidx[:], -1.0, float(2 * NODES), ALU.add, ALU.mult))
                                loc.link(nc.vector.tensor_tensor(pidx[:], fidx[:], col[:], ALU.add))
                                dve.wait_ge(s_cur, c * 16 + 16)
                                loc.tick(nc.vector.tensor_tensor(rank[:, bass.ds(c, 1)], got[:], r_in[:], ALU.add))
                                loc.link(nc.vector.tensor_tensor(put[:], got[:], n_in[:], ALU.add))
                                dve.sem_inc(s_c, 1)
                                loc.restart()
                            dve.wait_ge(s_cl, 16)
                            loc.link(nc.vector.tensor_tensor_scan(starts[:], ones[:, 0:PER], counts[:], 0.0,
                                                                  ALU.mult, ALU.add))
                            loc.link(nc.vector.tensor_copy(off[:], starts[:, PER - 1:PER]))
                            dve.sem_inc(s_tot, 1)
                            loc.link(nc.vector.tensor_tensor(starts[:], starts[:], counts[:], ALU.subtract))
                            dve.wait_ge(s_off, 1)
                            loc.link(nc.vector.tensor_scalar(starts[:], starts[:], pP[:, 0:1], None, ALU.add))
                            dve.sem_inc(s_st, 1)
                            loc.restart()
                            with dve.Fori(0, CHUNKS) as c:
                                dve.wait_ge(s_moved, c + 1)
                                loc.tick(nc.vector.tensor_scalar(cidx[:], dstT[:, bass.ds(c, 1)], 0.0, None, ALU.add))
                                loc.tick(nc.vector.tensor_scalar(pay[:, 1:2], dstT[:, bass.ds(c, 1)], 0.0, None, ALU.add))
                                loc.link(nc.vector.tensor_scalar(pay[:, 0:1], srcT[:, bass.ds(c, 1)], 0.0, None, ALU.add))
                                dve.sem_inc(s_p, 1)
                                dve.wait_ge(s_start, c * 16 + 16)
                                loc.link(nc.vector.tensor_tensor(pidx[:], got[:], rank[:, bass.ds(c, 1)], ALU.add))
                                dve.sem_inc(s_q, 1)
                                loc.restart()
                            rows_ready(loc, s_rows, s_rowsf)
                            copy_lists(dve, s_turned, s_copied)

        with ExitStack() as ctx:
            sb, ps, sem = make(ctx)
            J = NT - 1
            thr = sb("thr", [P, 1])
            wi = sb("wi", [P, z.TABW])
            cmp1 = sb("cmp1", [P, NS])
            cmpw = sb("cmpw", [P, z.TABW])
            cmps = sb("cmps", [P, NS])
            cmpb = sb("cmpb", [P, z.NB + 1])
            e_end = sb("e_end", [P, 1])
            w_start = sb("w_start", [P, 1])
            tmp1 = sb("tmp1", [P, z.TABW])
            js = sb("js", [1, 2, z.TABW])
            pk = sb("pk", [1, z.ITEMS // 2])
            pD = ps("pD", [P, 512])
            pJ = ps("pJ", [P, 512])
            pF = ps("pF", [P, 512])
            pB = ps("pB", [P, 512])
            s_const = sem("s_const1c")
            s_d1 = sem("s_d1")
            s_cmp = sem("s_cmp")
            s_tabs = sem("s_tabs")
            s_dve = sem("s_dve1c")
            with nc.Block() as block:
                @block.gpsimd
                def _(pool):
                    nc.gpsimd.iota(wi[:], pattern=[[1, z.TABW]], base=0, channel_multiplier=0,
                                   allow_small_or_imprecise_dtypes=True).then_inc(s_const, 1)
                    nc.gpsimd.iota(thr[:], pattern=[[1, 1]], base=P, channel_multiplier=P,
                                   allow_small_or_imprecise_dtypes=True).then_inc(s_const, 1)

                @block.tensor
                def _(pe):
                    nc.tensor.matmul(pD[0:J, 0:NS - 1], ones[0:1, 0:J], dstT[0:1, Q:Q * NS:Q], start=True, stop=True)\
                        .then_inc(s_d1, 1)
                    pe.wait_ge(s_cmp, 3)
                    nc.tensor.matmul(pJ[:, 0:z.TABW], ones[0:J, :], cmpw[0:J, :], start=True, stop=True)
                    nc.tensor.matmul(pB[:, 0:z.NB + 1], ones[0:J, :], cmpb[0:J, :], start=True, stop=True)
                    nc.tensor.matmul(pF[:, 0:NS], ones[0:J, :], cmps[0:J, :], start=True, stop=True)\
                        .then_inc(s_tabs, 1)

                @block.vector
                def _(dve):
                    loc = Local(dve, s_dve)
                    dve.wait_ge(s_const, 2)
                    dve.wait_ge(s_d1, 1)
                    loc.link(nc.vector.tensor_scalar(cmp1[0:J, 0:NS - 1], pD[0:J, 0:NS - 1], thr[0:J, 0:1], None,
                                                     ALU.is_lt))
                    loc.link(nc.vector.tensor_reduce(e_end[0:J], cmp1[0:J, 0:NS - 1], AX_X, ALU.add))
                    loc.link(nc.vector.scalar_tensor_tensor(out=w_start[0:J], in0=thr[0:J], scalar=1.0 / P,
                                                            in1=e_end[0:J], op0=ALU.mult, op1=ALU.add))
                    loc.tick(nc.vector.tensor_scalar(cmpw[0:J], wi[0:J], w_start[0:J, 0:1], None, ALU.is_ge))
                    loc.tick(nc.vector.tensor_scalar(cmps[0:J], wi[0:J, 0:NS], float(1 - R), e_end[0:J, 0:1], ALU.add,
                                                     ALU.is_gt))
                    loc.link(nc.vector.tensor_scalar(cmpb[0:J], wi[0:J, 0:z.NB + 1], float(z.BS), e_end[0:J, 0:1],
                                                     ALU.mult, ALU.is_gt))
                    dve.sem_inc(s_cmp, 3)
                    dve.wait_ge(s_tabs, 1)
                    loc.tick(nc.vector.tensor_tensor(tab[0:1, :, 0], wi[0:1], pJ[0:1, 0:z.TABW], ALU.subtract))
                    loc.tick(nc.vector.tensor_copy(tab[0:1, :, 1], pJ[0:1, 0:z.TABW]))
                    loc.tick(nc.vector.tensor_scalar(tile_base[:], pJ[:, 0:z.TABW], float(P), None, ALU.mult))
                    loc.link(nc.vector.tensor_scalar(tmp1[0:1, 0:NS], wi[0:1, 0:NS], float(1 - R), 0.0, ALU.add,
                                                     ALU.max))
                    loc.link(nc.vector.scalar_tensor_tensor(out=free_at[:], in0=tmp1[0:1, 0:NS], scalar=2.0,
                                                            in1=pF[0:1, 0:NS], op0=ALU.add, op1=ALU.add))
                    loc.tick(nc.vector.tensor_copy(js[:, 0], pJ[0:1, 0:z.TABW]))
                    loc.link(nc.vector.tensor_tensor(js[:, 1], wi[0:1], pJ[0:1, 0:z.TABW], ALU.subtract))
                    even = lambda what, first: js[:, what, first:first + z.ITEMS - 1:2]
                    loc.link(nc.vector.tensor_tensor(pk[:], even(1, 3), even(1, 2), ALU.subtract))
                    for radix, digit in ((z.SRANGE, even(1, 2)), (NT, even(0, 1)), (NT, even(0, 0))):
                        loc.link(nc.vector.scalar_tensor_tensor(out=pk[:], in0=pk[:], scalar=float(radix), in1=digit,
                                                                op0=ALU.mult, op1=ALU.add))
                    loc.tick(nc.vector.tensor_copy(packed[:], pk[:]))
                    loc.link(nc.vector.scalar_tensor_tensor(out=pair_end[:], in0=wi[0:1, 0:z.NB + 1], scalar=float(z.BS),
                                                            in1=pB[0:1, 0:z.NB + 1], op0=ALU.mult, op1=ALU.add))
                    loc.link(nc.vector.tensor_single_scalar(pair_end[:], pair_end[:], 1, op=ALU.arith_shift_right))

        def gather_supers(pool, rows, G, width, slot_idx, s_gath, s_item, s_pool_idx, s_seen):
            def one(s, k, n):
                need = pool.value_load(free_at[0:1, bass.ds(s, 1)], min_val=2, max_val=z.ITEMS + 2)
                pool.wait_ge(s_item, need)
                pool.sem_inc(s_seen, 1)
                nc.gpsimd.tensor_copy(slot_idx[:, k * Q:(k + 1) * Q], srcT[:, bass.ds(s * Q, Q)])\
                    .then_inc(s_pool_idx[k], 1)
                pool.wait_ge(s_pool_idx[k], 1)
                pool.sem_clear(s_pool_idx[k])
                for q in range(Q):
                    pool.indirect_dma_start(
                        out=G[:, k * Q + q, 0:width], out_offset=None, in_=rows,
                        in_offset=bass.IndirectOffsetOnAxis(ap=slot_idx[:, k * Q + q:k * Q + q + 1], axis=0),
                    ).then_inc(s_gath[k], 16)
            rounds = NS // R
            with pool.Fori(0, rounds) as i:
                for k in range(R):
                    one(i * R + k, k, i)
            for s in range(rounds * R, NS):
                one(s, s % R, rounds)

        def load_item(eng, w, what):
            hi = (NS + 3, NT - 1)[what]
            return eng.value_load(tab[0:1, bass.ds(w, 1), what], min_val=0, max_val=hi)

        def one_hots(dve, O, w, k):
            s = load_item(dve, w, 0)
            base = tile_base[:, bass.ds(w, 1)]
            return nc.vector.scalar_tensor_tensor(
                out=O[:, k], in0=iota_n[:].unsqueeze(1).to_broadcast([P, Q, P]), scalar=base,
                in1=dstT[:, bass.ds(s * Q, Q)].unsqueeze(2).to_broadcast([P, Q, P]), op0=ALU.add, op1=ALU.is_equal)

        clear_spent()
        with ExitStack() as ctx:
            sb, ps, sem = make(ctx)
            G = sb("G0", [P, R * Q, D + 1])
            O = sb("O0", [P, 2, Q, P])
            slot_idx = sb("slot_idx0", [P, R * Q], I32)
            pS = [ps(f"pS{i}", [P, 512]) for i in range(2)]
            s_gath = s_gath_l0
            s_pool_idx = [sem(f"s_pidx{k}") for k in range(R)]
            s_landed = sem("s_landed")
            s_item = sem("s_item")
            s_oh = sem("s_oh")
            s_merged = sem("s_merged")
            s_ready = sem("s_ready")
            s_seen = sem("s_seen")
            s_dve = sem("s_dve0")
            W = D + 1
            with nc.Block() as block:
                @block.gpsimd
                def _(pool):
                    pool.wait_ge(s_ready, 1)
                    gather_supers(pool, h0_rows, G, D, slot_idx, s_gath, s_item, s_pool_idx, s_seen)

                @block.sync
                def _(sp):
                    rounds = NS // R
                    with sp.Fori(0, rounds) as i:
                        for k in range(R):
                            sp.wait_ge(s_gath[k], i * (16 * Q) + 16 * Q)
                            sp.sem_inc(s_landed, 1)
                    for s in range(rounds * R, NS):
                        sp.wait_ge(s_gath[s % R], 16 * Q * (rounds + 1))
                        sp.sem_inc(s_landed, 1)

                @block.tensor
                def _(pe):
                    with pe.Fori(0, z.ITEMS // 2) as i:
                        for k in range(2):
                            w = i * 2 + k
                            s = load_item(pe, w, 0)
                            pe.wait_ge(s_landed, s + 1)
                            pe.wait_ge(s_merged, w + 1)
                            pe.wait_ge(s_oh, w + 1)
                            for q in range(Q):
                                mm = nc.tensor.matmul(pS[k][:, 0:W], O[:, k, q, :],
                                                      G[:, bass.ds((s % R) * Q + q, 1), :].rearrange("p a d -> p (a d)"),
                                                      start=(q == 0), stop=(q == Q - 1))
                            mm.then_inc(s_item, 1)

                @block.vector
                def _(dve):
                    loc = Local(dve, s_dve)
                    loc.tick(nc.vector.memset(ACC[:], 0.0))
                    loc.link(nc.vector.memset(G[:, :, D:D + 1], 1.0))
                    dve.sem_inc(s_ready, 1)
                    dve.sem_inc(s_item, 2)
                    dve.sem_inc(s_merged, 2)
                    one_hots(dve, O, 0, 0).then_inc(s_oh, 1)
                    loc.restart()
                    with dve.Fori(0, z.ITEMS // 2) as i:
                        for k in range(2):
                            w = i * 2 + k
                            dve.wait_ge(s_item, w + 2)
                            one_hots(dve, O, w + 1, 1 - k).then_inc(s_oh, 1)
                            j = load_item(dve, w, 1)
                            dve.wait_ge(s_item, w + 3)
                            dve.wait_ge(s_merged, w + 2)
                            nc.vector.tensor_tensor(ACC[:, bass.ds(j, 1), 0:W], ACC[:, bass.ds(j, 1), 0:W],
                                                    pS[k][:, 0:W].unsqueeze(1), ALU.add).then_inc(s_merged, 1)
        def dump(view):
            with ExitStack() as ctx:
                sb, ps, sem = make(ctx)
                s_out = sem("s_outdbg")
                with nc.Block() as block:
                    @block.sync
                    def _(sp):
                        sp.dma_start(out[0:FULL * P, :].rearrange("(t p) d -> p t d", p=P), view[:, 0:FULL, 0:D]).then_inc(s_out, 16)
                        sp.dma_start(out[FULL * P:N, :], view[0:REST, FULL, 0:D]).then_inc(s_out, 16)
                        sp.wait_ge(s_out, 32)

        if stop == 2:
            return dump(ACC)

        def top_two(loc, scores, rest, mx, eq, km, sel, prio, n):
            cur = scores
            for c in range(2):
                wide = lambda v: v.unsqueeze(2).to_broadcast([P, NT, n])
                loc.link(nc.vector.tensor_reduce(mx[:, c], cur[:], AX_X, ALU.max))
                loc.link(nc.vector.tensor_tensor(eq[:], cur[:], wide(mx[:, c]), ALU.is_equal))
                loc.link(nc.vector.tensor_tensor(eq[:], eq[:], prio[:].unsqueeze(1).to_broadcast([P, NT, n]), ALU.mult))
                loc.link(nc.vector.tensor_reduce(km[:], eq[:], AX_X, ALU.max))
                loc.link(nc.vector.tensor_tensor(sel[:, c], eq[:], wide(km[:]), ALU.is_equal))
                if c == 0:
                    loc.link(nc.vector.scalar_tensor_tensor(out=rest[:], in0=sel[:, 0], scalar=-BIG, in1=scores[:],
                                                            op0=ALU.mult, op1=ALU.add))
                    cur = rest

        clear_spent()
        def skewed(eng, lead, main, depth=2):
            assert (NT - 1) % depth == 0
            lead(0, 0)
            with eng.Fori(0, (NT - 1) // depth) as i:
                for k in range(depth):
                    lead(i * depth + k + 1, (k + 1) % depth)
                    main(i * depth + k, k)
            main(NT - 1, 0)

        NE, KH = z.NE, z.KH
        route = ExitStack()
        with route:
            sb, ps, sem = make(route)
            probs = sb("probs", [P, 2, NT])
            pos_f = sb("pos_f", [P, NT, 2])
            pos = sb("pos", [P, NT, 2], I32)
            eid = sb("eid", [1, z.ET], I32)
            fresh = sb("fresh", [1, z.ET], I32)
            n_pairs = sb("n_pairs", [1, 1], I32)
            with ExitStack() as ctx:
                sb, ps, sem = make(ctx)
                W0 = sb("W0", [P, 2 * KD, D])
                b0 = sb("b0", [1, D])
                Wg = sb("Wg", [P, KD, NE])
                bg = sb("bg", [P, NE])
                IN = sb("IN", [P, 2, 2 * D])
                HT = sb("HT", [P, 2, 2 * D])
                rdeg = sb("rdeg", [P, NT])
                ssq = sb("ssq", [P, NT])
                rnorm = sb("rnorm", [P, NT])
                sq = sb("sq", [P, 2, D])
                SC = sb("SC", [P, NT, NE])
                zero_rows = sb("zero_rows", [P, 2048])
                pT = [ps(f"pT3{i}", [P, 512]) for i in range(2)]
                pO = [ps(f"pO3{i}", [P, 512]) for i in range(2)]
                pG = [ps(f"pG3{i}", [P, 512]) for i in range(2)]
                s_w = sem("s_w3")
                s_zero = sem("s_zero3")
                s_zst = sem("s_zst3")
                s_in = sem("s_in3")
                s_turned = sem("s_turned3")
                s_ht = sem("s_ht3")
                s_out3 = sem("s_out3")
                s_relu = sem("s_relu3")
                s_held = sem("s_held3")
                s_rdeg = sem("s_rdeg3")
                s_root0 = sem("s_root03")
                s_x1 = sem("s_x13")
                s_stat = sem("s_stat3")
                s_var = sem("s_var3")
                s_root = sem("s_root3")
                s_in1 = sem("s_in13")
                s_turned1 = sem("s_turned13")
                s_ht1 = sem("s_ht13")
                s_sc = sem("s_sc3")
                s_sccp = sem("s_sccp3")
                s_kept = sem("s_kept3")
                s_dve = sem("s_dve3")
                s_act = sem("s_act3")
                IN4 = IN[:].rearrange("p k (m d) -> p (k m) d", d=D)
                HT4 = HT[:].rearrange("p k (m d) -> p (k m) d", d=D)
                pT4 = pT + pO
                with nc.Block() as block:
                    @block.sync
                    def _(sp):
                        sp.dma_start(W0[:], a["W0"].rearrange("(k p) n -> p k n", p=P)).then_inc(s_w, 16)
                        sp.dma_start(b0[:], a["b0"].unsqueeze(0)).then_inc(s_w, 16)
                        sp.dma_start(Wg[:], a["WgT"].rearrange("(k p) n -> p k n", p=P)).then_inc(s_w, 16)
                        sp.dma_start(bg[:], a["bg"].unsqueeze(0).to_broadcast([P, NE])).then_inc(s_w, 16)
                        sp.wait_ge(s_zero, 1)
                        flat = xd_rows.rearrange("(c p r) d -> c p (r d)", p=P, r=2048 // D)
                        chunks = (z.ET + 4) * z.TOK * D // (P * 2048)
                        for c in range(chunks):
                            sp.dma_start(flat[c], zero_rows[:]).then_inc(s_zst, 16)
                        tail = yd_rows[z.LEAST * z.TOK:, :].rearrange("(c p r) d -> c p (r d)", p=P, r=2048 // D)
                        tails = (z.ET - z.LEAST) * z.TOK * D // (P * 2048)
                        for c in range(tails):
                            sp.dma_start(tail[c], zero_rows[:]).then_inc(s_zst, 16)
                        sp.wait_ge(s_zst, 16 * (chunks + tails))

                    @block.gpsimd
                    def _(pool):
                        nc.gpsimd.memset(zero_rows[:], 0.0).then_inc(s_zero, 1)

                    @block.vector
                    def _(dve):
                        loc = Local(dve, s_dve)
                        loc.link(nc.vector.tensor_scalar(rdeg[:], ACC[:, :, D], 1.0, None, ALU.max))
                        loc.link(nc.vector.reciprocal(rdeg[:], rdeg[:]))
                        dve.sem_inc(s_rdeg, 1)
                        dve.sem_inc(s_turned, 2)
                        loc.restart()

                        def tile_in(t, k):
                            dve.wait_ge(s_turned, t + 1)
                            ln_apply(IN[:, k, 0:D].unsqueeze(1), X[:, bass.ds(t, 1), :], bass.ds(t, 1))\
                                .then_inc(s_in, 1)
                            nc.vector.tensor_scalar(IN[:, k, D:2 * D].unsqueeze(1), ACC[:, bass.ds(t, 1), 0:D],
                                                    rdeg[:, bass.ds(t, 1)], None, ALU.mult).then_inc(s_in, 1)
                        each_tile(dve, tile_in)
                        dve.wait_ge(s_root0, 1)
                        loc.link(nc.vector.tensor_scalar(rnorm[:], rnorm[:], NORM_EPS, None, ALU.max))
                        loc.link(nc.vector.reciprocal(rnorm[:], rnorm[:]))
                        loc.restart()

                        def x1(t, k):
                            one = bass.ds(t, 1)
                            nc.vector.scalar_tensor_tensor(
                                out=X[:, one, :], in0=ACC[:, one, 0:D], scalar=rnorm[:, one], in1=X[:, one, :],
                                op0=ALU.mult, op1=ALU.add).then_inc(s_x1, 1)
                        each_tile(dve, x1, UNROLL)
                        dve.wait_ge(s_x1, NT)
                        all_stats(dve, s_stat)
                        dve.wait_ge(s_stat, NT)
                        ln_moments(loc, s_var)
                        ln_rstd(loc, s_root)
                        dve.sem_inc(s_turned1, DEEP)
                        dve.sem_inc(s_kept, DEEP)

                        def tile_h1(t, k):
                            dve.wait_ge(s_turned1, t + 1)
                            dve.wait_ge(s_kept, t + 1)
                            ln_apply(IN4[:, k].unsqueeze(1), X[:, bass.ds(t, 1), :], bass.ds(t, 1))\
                                .then_inc(s_in1, 1)
                        each_tile(dve, tile_h1, DEEP)
                        dve.wait_ge(s_w, 64)
                        dve.wait_ge(s_sccp, NT + 2)
                        loc.link(nc.vector.tensor_tensor(SC[:], SC[:], bg[:].unsqueeze(1).to_broadcast([P, NT, NE]), ALU.add))

                    @block.scalar
                    def _(act):
                        loc = Local(act, s_act)
                        act.wait_ge(s_rdeg, 1)
                        act.sem_inc(s_ht, 2)
                        act.sem_inc(s_relu, 2)

                        def turned_in(t, k):
                            act.wait_ge(s_turned, t + 3)
                            act.wait_ge(s_out3, t + 1)
                            nc.scalar.activation(HT[:, k, :], pT[k][:], ACT.Copy).then_inc(s_ht, 1)

                        def relu_out(t, k):
                            act.wait_ge(s_out3, t + 3)
                            act.sem_inc(s_held, 1)
                            nc.scalar.activation(ACC[:, bass.ds(t, 1), 0:D], pO[k][:, 0:D].unsqueeze(1), ACT.Relu)\
                                .then_inc(s_relu, 1)
                            act.wait_ge(s_relu, t + 3)
                            act.sem_inc(s_held, 1)
                            loc.link(nc.scalar.activation(sq[:, k].unsqueeze(1), ACC[:, bass.ds(t, 1), 0:D],
                                                          ACT.Square, accum_out=ssq[:, bass.ds(t, 1)]))
                            loc.restart()

                        act.sem_inc(s_out3, 2)
                        loc.restart()

                        skewed(act, turned_in, relu_out)
                        nc.scalar.activation(rnorm[:], ssq[:], ACT.Sqrt).then_inc(s_root0, 1)
                        ln_root(act, s_var, s_root)
                        act.sem_inc(s_sc, DEEP)

                        def turned_h1(t, k):
                            act.wait_ge(s_turned1, t + 1 + DEEP)
                            act.wait_ge(s_sc, t + 1)
                            nc.scalar.activation(HT4[:, k], pT4[k][:, 0:D], ACT.Copy).then_inc(s_ht1, 1)
                            act.sem_inc(s_held, 1)
                            nc.scalar.activation(ACC[:, bass.ds(t, 1), 0:D], IN4[:, k].unsqueeze(1), ACT.Copy)\
                                .then_inc(s_kept, 1)

                        def scores(t, k):
                            act.wait_ge(s_sc, t + 1 + DEEP)
                            act.sem_inc(s_held, 1)
                            nc.scalar.activation(SC[:, bass.ds(t, 1), :], pG[k % 2][:, 0:NE].unsqueeze(1), ACT.Copy)\
                                .then_inc(s_sccp, 1)
                        skewed(act, turned_h1, scores, DEEP)

                    @block.tensor
                    def _(pe):
                        pe.wait_ge(s_w, 64)
                        pe.wait_ge(s_rdeg, 1)

                        def turn(t, k):
                            pe.wait_ge(s_in, 2 * t + 2)
                            pe.wait_ge(s_ht, t + 1)
                            for m in range(2 * KD):
                                tr = nc.tensor.transpose(pT[k][:, m * P:(m + 1) * P], IN[:, k, m * P:(m + 1) * P], ident[:])
                            tr.then_inc(s_turned, 1)

                        def dense(t, k):
                            pe.wait_ge(s_ht, t + 3)
                            pe.wait_ge(s_relu, t + 1)
                            for m in range(2 * KD):
                                nc.tensor.matmul(pO[k][:, 0:D], HT[:, k, m * P:(m + 1) * P], W0[:, m, :],
                                                 start=(m == 0), stop=False)
                            nc.tensor.matmul(pO[k][:, 0:D], ones[0:1, :], b0[:], start=False, stop=True)\
                                .then_inc(s_out3, 1)
                        skewed(pe, turn, dense)
                        pe.sem_inc(s_ht1, DEEP)
                        pe.sem_inc(s_sccp, 2)

                        def turn_h1(t, k):
                            pe.wait_ge(s_in1, t + 1)
                            pe.wait_ge(s_ht1, t + 1)
                            for m in range(KD):
                                tr = nc.tensor.transpose(pT4[k][:, m * P:(m + 1) * P], IN4[:, k, m * P:(m + 1) * P],
                                                         ident[:])
                            tr.then_inc(s_turned1, 1)

                        def gate(t, k):
                            pe.wait_ge(s_ht1, t + 1 + DEEP)
                            pe.wait_ge(s_sccp, t + 1)
                            for m in range(KD):
                                mm = nc.tensor.matmul(pG[k % 2][:, 0:NE], HT4[:, k, m * P:(m + 1) * P], Wg[:, m, :],
                                                 start=(m == 0), stop=(m == KD - 1))
                            mm.then_inc(s_sc, 1)
                        skewed(pe, turn_h1, gate, DEEP)

                with ExitStack() as ctx4:
                    sb, ps, sem = make(ctx4)
                    prio = sb("prio", [P, NE])
                    mx = sb("mx", [P, 2, NT])
                    eq = sb("eq", [P, NT, NE])
                    km = sb("km", [P, NT])
                    sel = sb("sel", [P, 2, NT, NE])
                    SC2 = sb("SC2", [P, NT, NE])
                    both = sb("both", [P, NT, NE])
                    below = sb("below", [P, P])
                    tot = sb("tot", [P, NE, NT])
                    inc = sb("inc", [P, NE, NT])
                    cnt = sb("cnt", [P, NE])
                    cnt_i = sb("cnt_i", [P, NE], I32)
                    tiles = sb("tiles", [P, NE])
                    tend = sb("tend", [P, NE])
                    tbeg = sb("tbeg", [P, NE])
                    row = sb("row", [P, NT, NE])
                    ui = sb("ui", [1, z.ET])
                    ucmp = sb("ucmp", [1, z.ET, NE])
                    dm = sb("dm", [P, NT])
                    pA = ps("pA4", [P, 512])
                    pB = ps("pB4", [P, 512])
                    s_const = sem("s_const4")
                    s_both = sem("s_both4")
                    s_cum = sem("s_cum4")
                    s_dm = sem("s_dm4")
                    s_ex = sem("s_ex4")
                    s_dve = sem("s_dve4")
                    s_pool = sem("s_pool4")
                    with nc.Block() as block:
                        @block.gpsimd
                        def _(pool):
                            loc = Local(pool, s_pool)
                            nc.gpsimd.iota(prio[:], pattern=[[-1, NE]], base=NE, channel_multiplier=0,
                                           allow_small_or_imprecise_dtypes=True).then_inc(s_const, 1)
                            nc.gpsimd.iota(ui[:], pattern=[[1, z.ET]], base=0, channel_multiplier=0,
                                           allow_small_or_imprecise_dtypes=True).then_inc(s_const, 1)
                            nc.gpsimd.affine_select(out=below[:], in_=ones[:], compare_op=ALU.is_ge, fill=0.0,
                                                    base=-1, pattern=[[1, P]], channel_multiplier=-1)\
                                .then_inc(s_const, 1)

                        @block.scalar
                        def _(act):
                            act.wait_ge(s_dm, 1)
                            nc.scalar.activation(dm[:], dm[:], ACT.Exp).then_inc(s_ex, 1)

                        @block.tensor
                        def _(pe):
                            pe.wait_ge(s_const, 3)
                            pe.wait_ge(s_both, 1)
                            flat = both[:].rearrange("p t e -> p (t e)")
                            nc.tensor.matmul(pA[:, 0:NT * NE], below[:], flat, start=True, stop=True)
                            nc.tensor.matmul(pB[:, 0:NT * NE], ones[:], flat, start=True, stop=True).then_inc(s_cum, 1)

                        @block.vector
                        def _(dve):
                            loc = Local(dve, s_dve)
                            over_t = lambda v: v.unsqueeze(1).to_broadcast([P, NT, NE])
                            dve.wait_ge(s_const, 3)
                            top_two(loc, SC, SC2, mx, eq, km, sel, prio, NE)
                            loc.tick(nc.vector.tensor_tensor(both[:], sel[:, 0], sel[:, 1], ALU.add))
                            loc.link(nc.vector.tensor_tensor(dm[:], mx[:, 1], mx[:, 0], ALU.subtract))
                            dve.sem_inc(s_both, 1)
                            dve.sem_inc(s_dm, 1)
                            dve.wait_ge(s_ex, 1)
                            loc.link(nc.vector.tensor_scalar(probs[:, 0], dm[:], 1.0, None, ALU.add))
                            loc.link(nc.vector.reciprocal(probs[:, 0], probs[:, 0]))
                            loc.tick(nc.vector.tensor_tensor(probs[:, 1], dm[:], probs[:, 0], ALU.mult))
                            dve.wait_ge(s_cum, 1)
                            loc.link(nc.vector.tensor_copy(tot[:], pB[:, 0:NT * NE].rearrange("p (t e) -> p e t", e=NE)))
                            for e in range(NE):
                                loc.tick(nc.vector.tensor_tensor_scan(inc[:, e], ones[:, 0:NT], tot[:, e], 0.0,
                                                                      ALU.mult, ALU.add))
                            loc.settle()
                            loc.link(nc.vector.tensor_scalar(cnt[:], inc[:, :, NT - 1], float(z.TOK - 1), None, ALU.add))
                            loc.link(nc.vector.tensor_copy(cnt_i[:], cnt[:]))
                            loc.link(nc.vector.tensor_single_scalar(cnt_i[:], cnt_i[:], z.TOK.bit_length() - 1,
                                                                    op=ALU.arith_shift_right))
                            loc.link(nc.vector.tensor_copy(tiles[:], cnt_i[:]))
                            loc.link(nc.vector.tensor_tensor_scan(tend[:], ones[:, 0:NE], tiles[:], 0.0,
                                                                  ALU.mult, ALU.add))
                            loc.link(nc.vector.tensor_tensor(tbeg[:], tend[:], tiles[:], ALU.subtract))
                            loc.tick(nc.vector.tensor_tensor(ucmp[:], tbeg[0:1].unsqueeze(1).to_broadcast([1, z.ET, NE]),
                                                             ui[:].unsqueeze(2).to_broadcast([1, z.ET, NE]), ALU.is_le))
                            loc.link(nc.vector.tensor_tensor(inc[:], inc[:], tot[:], ALU.subtract))
                            loc.link(nc.vector.tensor_tensor(
                                row[:], inc[:].rearrange("p e t -> p t e"),
                                pA[:, 0:NT * NE].rearrange("p (t e) -> p t e", e=NE), ALU.add))
                            loc.link(nc.vector.scalar_tensor_tensor(out=row[:], in0=over_t(tbeg[:]), scalar=float(z.TOK),
                                                                    in1=row[:], op0=ALU.mult, op1=ALU.add))
                            loc.link(nc.vector.tensor_reduce(ui[:], ucmp[:], AX_X, ALU.add))
                            loc.tick(nc.vector.tensor_scalar(eid[:], ui[:], -1.0, None, ALU.add))
                            loc.tick(nc.vector.memset(fresh[:, 0:2], 1))
                            loc.tick(nc.vector.tensor_tensor(fresh[:, 2:z.ET], ui[:, 2:z.ET], ui[:, 0:z.ET - 2],
                                                             ALU.not_equal))
                            loc.link(nc.vector.tensor_scalar(cnt[0:1, 0:1], tend[0:1, NE - 1:NE], 1.0, None, ALU.add))
                            loc.link(nc.vector.tensor_copy(n_pairs[:], cnt[0:1, 0:1]))
                            loc.link(nc.vector.tensor_single_scalar(n_pairs[:], n_pairs[:], 1,
                                                                    op=ALU.arith_shift_right))
                            for c in range(2):
                                loc.link(nc.vector.tensor_tensor(eq[:], sel[:, c], row[:], ALU.mult))
                                loc.link(nc.vector.tensor_reduce(pos_f[:, :, c], eq[:], AX_X, ALU.add))
                            loc.link(nc.vector.tensor_copy(pos[:], pos_f[:]))

            SLOTS = 7
            assert NT % SLOTS == 0
            with ExitStack() as ctx:
                sb, ps, sem = make(ctx)
                stage = sb("stage", [P, SLOTS, D])
                sidx = sb("sidx", [P, SLOTS, 2], I32)
                s_staged = [sem(f"s_staged{k}") for k in range(SLOTS)]
                s_seen = sem("s_seen5")
                s_held = sem("s_held5")
                with nc.Block() as block:
                    @block.scalar
                    def _(act):
                        def one_round(i, first):
                            for k in range(SLOTS):
                                t = bass.ds(i * SLOTS + k, 1)
                                if not first:
                                    act.wait_ge(s_sent[k], i * 32)
                                    act.sem_inc(s_held, 1)
                                nc.scalar.activation(stage[:, k].unsqueeze(1), ACC[:, t, 0:D], ACT.Copy)\
                                    .then_inc(s_staged[k], 1)
                                nc.scalar.activation(sidx[:, k].unsqueeze(1), pos_f[:, t, :], ACT.Copy)\
                                    .then_inc(s_staged[k], 1)

                        one_round(0, True)
                        with act.Fori(1, NT // SLOTS) as i:
                            one_round(i, False)

                    @block.gpsimd
                    def _(pool):
                        with pool.Fori(0, NT // SLOTS) as i:
                            for k in range(SLOTS):
                                pool.wait_ge(s_staged[k], i * 2 + 2)
                                pool.sem_inc(s_seen, 1)
                                for c in range(2):
                                    pool.indirect_dma_start(
                                        out=xd_rows, in_=stage[:, k, :], in_offset=None,
                                        out_offset=bass.IndirectOffsetOnAxis(ap=sidx[:, k, c:c + 1], axis=0),
                                    ).then_inc(s_sent[k], 16)
                        for k in range(SLOTS):
                            pool.wait_ge(s_sent[k], 32 * (NT // SLOTS))

            clear_spent()
            HALVES = z.TOK // P
            with ExitStack() as ctx:
                sb, ps, sem = make(ctx)
                w1s = sb("w1s", [P, 2, KD, z.HID])
                w2s = sb("w2s", [P, 2, KH, D])
                b1s = sb("b1s", [P, 2, KH])
                b2s = sb("b2s", [P, 2, D])
                XE = sb("XE", [P, 2, HALVES, D])
                XT = sb("XT", [P, 2, KD, z.TOK])
                HE = sb("HE", [P, KH, z.TOK])
                YE = sb("YE", [P, 2, HALVES, D])
                pX = ps("pX6", [P, KD, z.TOK])
                pH = [ps(f"pH6{i}", [P, 512]) for i in range(3)]
                pY = [ps(f"pY6{i}", [P, 512]) for i in range(2)]
                s_load = [sem(f"s_load6{k}") for k in range(2)]
                s_xload = [sem(f"s_xload6{k}") for k in range(2)]
                s_weights = sem("s_weights6")
                s_seen = sem("s_seen6")
                s_turned = sem("s_turned6")
                s_xt = sem("s_xt6")
                s_hmm = sem("s_hmm6")
                s_relu = sem("s_relu6")
                s_ymm = sem("s_ymm6")
                s_ycp = sem("s_ycp6")
                s_store = [sem(f"s_store6{k}") for k in range(2)]
                assert z.ET % 2 == 0

                def pairs_used(eng):
                    return eng.value_load(n_pairs[:], min_val=z.LEAST // 2, max_val=z.ET // 2)

                with nc.Block() as block:
                    @block.sync
                    def _(sp):
                        def load_tokens(u, k):
                            sp.wait_ge(s_turned, u + 1)
                            sp.dma_start(XE[:, k], xd_rows[bass.ds(u * z.TOK, z.TOK), :]
                                         .rearrange("(a p) d -> p a d", p=P)).then_inc(s_xload[k], 16)

                        n = pairs_used(sp)
                        load_tokens(0, 0)
                        with sp.Fori(0, n) as i:
                            for k in range(2):
                                u = i * 2 + k
                                load_tokens(u + 1, 1 - k)
                                e = sp.value_load(eid[0:1, bass.ds(u, 1)], min_val=0, max_val=NE - 1)
                                new = sp.value_load(fresh[0:1, bass.ds(u, 1)], min_val=0, max_val=1)
                                sp.wait_ge(s_ymm, u + 1)
                                sp.wait_ge(s_ycp, u * 2 + 1)
                                sp.sem_inc(s_seen, 1)
                                with sp.If(new):
                                    sp.dma_start(w1s[:, k], a["W1"][bass.ds(e, 1)].rearrange("a p (k h) -> p (a k) h", k=KD))\
                                        .then_inc(s_load[k], 16)
                                    sp.dma_start(w2s[:, k], a["W2"][bass.ds(e, 1)].rearrange("a p (k d) -> p (a k) d", k=KH))\
                                        .then_inc(s_load[k], 16)
                                    sp.dma_start(b1s[:, k], a["b1"][bass.ds(e, 1)].rearrange("a p k -> p (a k)"))\
                                        .then_inc(s_load[k], 16)
                                    sp.dma_start(b2s[:, k], a["b2"][bass.ds(e, 1)].to_broadcast([P, D])).then_inc(s_load[k], 16)
                                    sp.wait_ge(s_load[k], 64)
                                    sp.sem_clear(s_load[k])
                                sp.sem_inc(s_weights, 1)

                    @block.tensor
                    def _(pe):
                        pe.sem_inc(s_ymm, 2)
                        pe.sem_inc(s_turned, 2)
                        pe.sem_inc(s_xt, 1)
                        pe.sem_inc(s_relu, 3)

                        def turn(u, k, i):
                            pe.wait_ge(s_xload[k], i * 16 + 16)
                            pe.wait_ge(s_xt, u + 1)
                            pe.sem_inc(s_seen, 1)
                            for h in range(HALVES):
                                for m in range(KD):
                                    tr = nc.tensor.transpose(pX[:, m, h * P:(h + 1) * P],
                                                             XE[:, k, h, m * P:(m + 1) * P], ident[:])
                            tr.then_inc(s_turned, 1)

                        n = pairs_used(pe)
                        turn(0, 0, 0)
                        with pe.Fori(0, n) as i:
                            for k in range(2):
                                u = i * 2 + k
                                pe.wait_ge(s_weights, u + 1)
                                pe.wait_ge(s_xt, u + 2)
                                for b in range(KH):
                                    pe.wait_ge(s_relu, u * KH + b + 1)
                                    for m in range(KD):
                                        mm = nc.tensor.matmul(pH[b % 3][:, 0:z.TOK],
                                                              w1s[:, k, m, b * P:(b + 1) * P], XT[:, k, m, :],
                                                              start=(m == 0), stop=(m == KD - 1))
                                    mm.then_inc(s_hmm, 1)
                                turn(u + 1, 1 - k, i + k)
                                pe.wait_ge(s_ycp, 2 * u + 3)
                                for h in range(HALVES):
                                    for b in range(KH):
                                        if h == 0:
                                            pe.wait_ge(s_relu, u * KH + b + 4)
                                        mm = nc.tensor.matmul(pY[h][:, 0:D], HE[:, b, h * P:(h + 1) * P], w2s[:, k, b, :],
                                                              start=(b == 0), stop=(b == KH - 1))
                                mm.then_inc(s_ymm, 1)

                    @block.scalar
                    def _(act):
                        act.sem_inc(s_ycp, 3)
                        n = pairs_used(act)
                        with act.Fori(0, n) as i:
                            for k in range(2):
                                u = i * 2 + k
                                for b in range(KH):
                                    act.wait_ge(s_hmm, u * KH + b + 1)
                                    if b == 0:
                                        act.wait_ge(s_ymm, u + 2)
                                    nc.scalar.activation(HE[:, b, :], pH[b % 3][:, 0:z.TOK], ACT.Relu,
                                                         bias=b1s[:, k, b:b + 1]).then_inc(s_relu, 1)
                                act.wait_ge(s_ycp, 2 * u + 5)
                                act.dma_start(yd_rows[bass.ds(u * z.TOK, z.TOK), :].rearrange("(a p) d -> p a d", p=P),
                                              YE[:, k]).then_inc(s_store[k], 16)
                        for k in range(2):
                            act.wait_ge(s_store[k], n * 16)
                            act.sem_inc(s_seen, 1)

                    @block.vector
                    def _(dve):
                        def copy_turned(u, k):
                            dve.wait_ge(s_turned, u + 3)
                            nc.vector.tensor_copy(XT[:, k], pX[:]).then_inc(s_xt, 1)

                        def turn(i, first):
                            for k in range(2):
                                u = i * 2 + k
                                copy_turned(u + 1, 1 - k)
                                if not first:
                                    dve.wait_ge(s_store[k], i * 16)
                                dve.wait_ge(s_ymm, u + 3)
                                for h in range(HALVES):
                                    nc.vector.tensor_tensor(YE[:, k, h, :], pY[h][:, 0:D], b2s[:, k], ALU.add)\
                                        .then_inc(s_ycp, 1)
                        n = pairs_used(dve)
                        copy_turned(0, 0)
                        turn(0, True)
                        with dve.Fori(1, n) as i:
                            turn(i, False)

            with ExitStack() as ctx:
                sb, ps, sem = make(ctx)
                Y = sb("Y7", [P, SLOTS, 2, D])
                gidx = sb("gidx", [P, SLOTS, 2], I32)
                s_idx = [sem(f"s_idx7{k}") for k in range(SLOTS)]
                s_added = sem("s_added7")
                s_seen = sem("s_seen7")
                with nc.Block() as block:
                    @block.scalar
                    def _(act):
                        act.sem_inc(s_added, 2 * SLOTS)
                        with act.Fori(0, NT // SLOTS) as i:
                            for k in range(SLOTS):
                                t = bass.ds(i * SLOTS + k, 1)
                                act.wait_ge(s_added, (i * SLOTS + k) * 2 + 2)
                                act.sem_inc(s_seen, 1)
                                nc.scalar.activation(gidx[:, k].unsqueeze(1), pos_f[:, t, :], ACT.Copy)\
                                    .then_inc(s_idx[k], 1)

                    @block.gpsimd
                    def _(pool):
                        with pool.Fori(0, NT // SLOTS) as i:
                            for k in range(SLOTS):
                                pool.wait_ge(s_idx[k], i + 1)
                                pool.sem_inc(s_seen, 1)
                                for c in range(2):
                                    pool.indirect_dma_start(
                                        out=Y[:, k, c, :], out_offset=None, in_=yd_rows,
                                        in_offset=bass.IndirectOffsetOnAxis(ap=gidx[:, k, c:c + 1], axis=0),
                                    ).then_inc(s_got[k], 16)

                    @block.vector
                    def _(dve):
                        with dve.Fori(0, NT // SLOTS) as i:
                            for k in range(SLOTS):
                                t = bass.ds(i * SLOTS + k, 1)
                                dve.wait_ge(s_got[k], i * 32 + 32)
                                for c in range(2):
                                    if c:
                                        dve.wait_ge(s_added, (i * SLOTS + k) * 2 + 2 * SLOTS + 1)
                                    nc.vector.scalar_tensor_tensor(
                                        out=X[:, t, :], in0=Y[:, k, c].unsqueeze(1), scalar=probs[:, c, t],
                                        in1=X[:, t, :], op0=ALU.mult, op1=ALU.add).then_inc(s_added, 1)
        if stop == 7:
            return dump(X)

        clear_spent()
        HW = HC + 1
        GR = HEADS * HW
        late = ExitStack()
        with late:
            sb, ps, sem = make(late)
            ADST = sb("ADST", [P, NT, HEADS])
            with ExitStack() as ctx:
                sb, ps, sem = make(ctx)
                Wrow = sb("Wrow", [P, KD, GR])
                Wd = sb("Wd", [P, KD, HEADS])
                WpT = sb("WpT", [P, KD, D])
                att = sb("att", [P, KD, 2])
                head_of = sb("head_of", [P, KD], I32)
                head_f = sb("head_f", [P, KD])
                hh = sb("hh", [P, HEADS])
                A = sb("A8", [P, KD, 2, HEADS])
                IN = sb("IN8", [P, 2, D])
                HT = sb("HT8", [P, 2, D])
                OUT = sb("OUT8", [P, 2, GR])
                pT = [ps(f"pT8{i}", [P, 512]) for i in range(2)]
                pO = [ps(f"pO8{i}", [P, 512]) for i in range(2)]
                pW = ps("pW8", [P, 512])
                s_w = sem("s_w8")
                s_iota = sem("s_iota8")
                s_A = sem("s_A8")
                s_wmm = sem("s_wmm8")
                s_wcp = sem("s_wcp8")
                s_stat = sem("s_stat8")
                s_var = sem("s_var8")
                s_root = sem("s_root8")
                s_in = sem("s_in8")
                s_turned = sem("s_turned8")
                s_ht = sem("s_ht8")
                s_mm = sem("s_mm8")
                s_cp = sem("s_cp8")
                s_held = sem("s_held8")
                s_store = [sem(f"s_store8{k}") for k in range(2)]
                s_dve = sem("s_dve8")
                with nc.Block() as block:
                    @block.sync
                    def _(sp):
                        sp.dma_start(WpT[:], a["WpT"].rearrange("(k p) n -> p k n", p=P)).then_inc(s_w, 16)
                        sp.dma_start(att[:], a["att"].rearrange("(k p) n -> p k n", p=P)).then_inc(s_w, 16)
                        for m in range(KD):
                            sp.dma_start(Wrow[:, m, :].rearrange("p (h c) -> p h c", c=HW)[:, :, 0:HC],
                                         a["Wp"][m * P:(m + 1) * P, :].rearrange("p (h c) -> p h c", c=HC))\
                                .then_inc(s_w, 16)

                        def store(t, k):
                            sp.wait_ge(s_cp, 2 * t + 6)
                            sp.dma_start(g_rows[bass.ds(t * P, P), :], OUT[:, k]).then_inc(s_store[k], 16)
                        each_tile(sp, store)
                        sp.wait_ge(s_store[0], 16 * ((NT + 1) // 2))
                        sp.wait_ge(s_store[1], 16 * (NT // 2))

                    @block.gpsimd
                    def _(pool):
                        nc.gpsimd.iota(head_of[:], pattern=[[P, KD]], base=0, channel_multiplier=1).then_inc(s_iota, 1)
                        nc.gpsimd.iota(hh[:], pattern=[[1, HEADS]], base=0, channel_multiplier=0,
                                       allow_small_or_imprecise_dtypes=True).then_inc(s_iota, 1)

                    @block.vector
                    def _(dve):
                        loc = Local(dve, s_dve)
                        all_stats(dve, s_stat)
                        dve.wait_ge(s_iota, 2)
                        loc.link(nc.vector.tensor_single_scalar(head_of[:], head_of[:], HC.bit_length() - 1,
                                                                op=ALU.arith_shift_right))
                        loc.link(nc.vector.tensor_copy(head_f[:], head_of[:]))
                        dve.wait_ge(s_w, 16 * (2 + KD))
                        for m in range(KD):
                            for c in range(2):
                                loc.tick(nc.vector.tensor_scalar(A[:, m, c], hh[:], head_f[:, m:m + 1],
                                                                 att[:, m, c:c + 1], ALU.is_equal, ALU.mult))
                        loc.settle()
                        dve.sem_inc(s_A, 1)
                        dve.wait_ge(s_wmm, 1)
                        pw = pW[:, 0:KD * 2 * HEADS].rearrange("p (k c h) -> p k c h", k=KD, c=2)
                        wr = Wrow[:].rearrange("p k (h c) -> p k h c", c=HW)
                        nc.vector.tensor_copy(wr[:, :, :, HC], pw[:, :, 0, :]).then_inc(s_wcp, 1)
                        nc.vector.tensor_copy(Wd[:], pw[:, :, 1, :]).then_inc(s_wcp, 1)
                        dve.wait_ge(s_stat, NT)
                        ln_moments(loc, s_var)
                        ln_rstd(loc, s_root)
                        dve.sem_inc(s_turned, 2)
                        loc.restart()

                        def tile_in(t, k):
                            dve.wait_ge(s_turned, t + 1)
                            ln_apply(IN[:, k].unsqueeze(1), X[:, bass.ds(t, 1), :], bass.ds(t, 1)).then_inc(s_in, 1)
                        each_tile(dve, tile_in)

                    @block.scalar
                    def _(act):
                        ln_root(act, s_var, s_root)
                        act.sem_inc(s_ht, 2)
                        act.sem_inc(s_cp, 4)
                        act.sem_inc(s_mm, 2)

                        def turned_in(t, k):
                            act.wait_ge(s_turned, t + 3)
                            act.wait_ge(s_mm, t + 1)
                            nc.scalar.activation(HT[:, k], pT[k][:, 0:D], ACT.Copy).then_inc(s_ht, 1)

                        def tile_out(t, k, first=False):
                            act.wait_ge(s_mm, t + 3)
                            if not first:
                                act.wait_ge(s_store[k], (t - k) * 8)
                            nc.scalar.activation(OUT[:, k], pO[k][:, 0:GR], ACT.Copy).then_inc(s_cp, 1)
                            act.sem_inc(s_held, 1)
                            nc.scalar.activation(ADST[:, bass.ds(t, 1), :], pO[k][:, GR:GR + HEADS].unsqueeze(1),
                                                 ACT.Copy).then_inc(s_cp, 1)
                        turned_in(0, 0)
                        for k in range(2):
                            turned_in(k + 1, 1 - k)
                            tile_out(k, k, True)
                        with act.Fori(1, NT // 2) as i:
                            for k in range(2):
                                turned_in(i * 2 + k + 1, 1 - k)
                                tile_out(i * 2 + k, k)
                        tile_out(NT - 1, 0)

                    @block.tensor
                    def _(pe):
                        pe.wait_ge(s_A, 1)
                        for m in range(KD):
                            for j in range(KD):
                                mm = nc.tensor.matmul(pW[:, m * 2 * HEADS:(m + 1) * 2 * HEADS],
                                                      WpT[:, j, m * P:(m + 1) * P],
                                                      A[:, j].rearrange("p c h -> p (c h)"), start=(j == 0), stop=(j == KD - 1))
                        mm.then_inc(s_wmm, 1)
                        pe.wait_ge(s_wcp, 2)

                        def turn(t, k):
                            pe.wait_ge(s_in, t + 1)
                            pe.wait_ge(s_ht, t + 1)
                            for m in range(KD):
                                tr = nc.tensor.transpose(pT[k][:, m * P:(m + 1) * P], IN[:, k, m * P:(m + 1) * P], ident[:])
                            tr.then_inc(s_turned, 1)

                        def proj(t, k):
                            pe.wait_ge(s_ht, t + 3)
                            pe.wait_ge(s_cp, 2 * t + 2)
                            for m in range(KD):
                                nc.tensor.matmul(pO[k][:, 0:GR], HT[:, k, m * P:(m + 1) * P], Wrow[:, m, :],
                                                 start=(m == 0), stop=(m == KD - 1))
                            for m in range(KD):
                                mm = nc.tensor.matmul(pO[k][:, GR:GR + HEADS], HT[:, k, m * P:(m + 1) * P], Wd[:, m, :],
                                                      start=(m == 0), stop=(m == KD - 1))
                            mm.then_inc(s_mm, 1)
                        skewed(pe, turn, proj)

            BC = z.BS * Q
            BR = z.BS * HEADS
            RB = R // z.BS
            PAIR_STEPS = 14
            NR = GR + HEADS + 1
            with ExitStack() as ctx:
                sb, ps, sem = make(ctx)
                G = sb("G1", [P, R * Q, GW])
                O = sb("O1", [P, 2, Q, P])
                slot_idx = sb("slot_idx1", [P, R * Q], I32)
                MR = sb("MR", [P, NT, HEADS])
                both = sb("both9", [P, 2, 2, HEADS])
                FL = sb("FL", [BR, z.SE + 1])
                M2 = sb("M2", [BR, z.SE])
                SCO = sb("SCO", [P, 2, Q, z.BS, HEADS])
                EX = sb("EX", [P, Q, z.BS, HEADS])
                gone = sb("gone", [P, 2])
                df = sb("df", [P, 2, 2, HEADS])
                fac = sb("fac", [P, 2, 2, HEADS])
                TM = sb("TM", [P, GR])
                BANK, BANKS = 512, 4
                pS = ps("pS9", [P, BANKS * BANK])
                pA = ps("pA9", [P, Q * P])
                pM = ps("pM9", [P, 512])
                s_gath = s_gath_l1
                s_pool_idx = [sem(f"s_pidx9{k}") for k in range(R)]
                s_item = sem("s_item9")
                s_oh = sem("s_oh9")
                s_merged = sem("s_merged9")
                s_seen = sem("s_seen9")
                s_dr = sem("s_dr9")
                s_pair = sem("s_pair9")
                s_at = sem("s_at9")
                s_sco = sem("s_sco9")
                s_max = sem("s_max9")
                s_mt = sem("s_mt9")
                s_sub = sem("s_sub9")
                s_exp = sem("s_exp9")
                s_prep = sem("s_prep9")
                s_diff = sem("s_diff9")
                s_fac = sem("s_fac9")
                s_dve = sem("s_dve9")

                def batches(eng, first, body, last_items):
                    first()
                    body(0, 0, 0, False, True)
                    rounds = (z.NB - 2) // RB
                    with eng.Fori(0, rounds) as i:
                        for k in range(RB):
                            body(i * RB + k + 1, (k + 1) % RB, i + (k + 1) // RB, True, True)
                    for b in range(rounds * RB + 1, z.NB):
                        body(b, b % RB, b // RB, True, b + 1 < z.NB)
                    last_items(z.NB - 1)

                def span(eng, b):
                    lo = eng.value_load(pair_end[0:1, bass.ds(b, 1)], min_val=0, max_val=z.ITEMS // 2)
                    hi = eng.value_load(pair_end[0:1, bass.ds(b + 1, 1)], min_val=1, max_val=z.ITEMS // 2)
                    return lo, hi

                with nc.Block() as block:
                    @block.gpsimd
                    def _(pool):
                        gather_supers(pool, g_rows, G, GR, slot_idx, s_gath, s_item, s_pool_idx, s_seen)

                    @block.sync
                    def _(sp):
                        def load(b):
                            v = seg_gaps[bass.ds(b * (BC * P), BC * P)].rearrange("(s e) -> s e", s=z.BS)
                            sp.dma_start(FL[:, 1:z.SE + 1], v.unsqueeze(1).to_broadcast([z.BS, HEADS, z.SE]))\
                                .then_inc(s_dr, 16)
                        load(0)
                        with sp.Fori(1, z.NB) as b:
                            sp.wait_ge(s_max, b + 0)
                            load(b)

                    @block.tensor
                    def _(pe):
                        def items(pairs_of_batch, b):
                            with pe.Fori(*pairs_of_batch) as i:
                                for k in range(2):
                                    w = i * 2 + k
                                    s = load_item(pe, w, 0)
                                    pe.wait_ge(s_prep, b + 1)
                                    pe.wait_ge(s_merged, w + 1)
                                    pe.wait_ge(s_oh, w + 1)
                                    for q in range(Q):
                                        mm = nc.tensor.matmul(
                                            pS[:, bass.ds((w % BANKS) * BANK, NR)], O[:, k, q, :],
                                            G[:, bass.ds((s % R) * Q + q, 1), 0:NR].rearrange("p a d -> p (a d)"),
                                            start=(q == 0), stop=(q == Q - 1))
                                    mm.then_inc(s_item, 1)
                                    pe.sem_inc(s_seen, 1)

                        def turn_scores(b, k):
                            pe.wait_ge(s_sco, b + 1)
                            for q in range(Q):
                                tr = nc.tensor.transpose(pA[0:BR, q * P:(q + 1) * P],
                                                         SCO[:, k % 2, q].rearrange("p s h -> p (s h)"), ident[:])
                            tr.then_inc(s_at, 1)

                        def batch(b, k, i, before, ahead):
                            if before:
                                pairs_before = span(pe, b - 1)
                                pe.wait_ge(s_prep, b + 0)
                            pe.wait_ge(s_max, b + 1)
                            pe.sem_inc(s_seen, 1)
                            for q in range(Q):
                                tr = nc.tensor.transpose(pM[:, q * BR:(q + 1) * BR], M2[:, q * P:(q + 1) * P],
                                                         ident[0:BR, 0:BR])
                            tr.then_inc(s_mt, 1)
                            if ahead:
                                turn_scores(b + 1, k + 1)
                            pe.sem_inc(s_seen, 1)
                            if before:
                                items(pairs_before, b - 1)

                        batches(pe, lambda: turn_scores(0, 0), batch, lambda b: items(span(pe, b), b))

                    @block.scalar
                    def _(act):
                        def items(pairs_of_batch):
                            with act.Fori(*pairs_of_batch) as i:
                                for k in range(2):
                                    act.wait_ge(s_diff, i * 2 + k + 1)
                                    nc.scalar.activation(fac[:, k], df[:, k], ACT.Exp).then_inc(s_fac, 1)

                        def gates(k):
                            return G[:, k * BC:(k + 1) * BC, 0:GR].rearrange("p (s q) (h c) -> p q s h c", q=Q, c=HW)[
                                :, :, :, :, HC]

                        def scores(k, i):
                            for s in range(z.BS):
                                act.wait_ge(s_gath[k * z.BS + s], i * (16 * Q) + 16 * Q)
                            nc.scalar.activation(SCO[:, k % 2], gates(k), ACT.Copy).then_inc(s_sco, 1)

                        def batch(b, k, i, before, ahead):
                            if before:
                                pairs_before = span(act, b - 1)
                            if ahead:
                                scores((k + 1) % RB, i + (k + 1) // RB)
                            act.wait_ge(s_sub, b + 1)
                            nc.scalar.activation(gates(k), EX[:], ACT.Exp).then_inc(s_exp, 1)
                            if before:
                                items(pairs_before)
                        batches(act, lambda: scores(0, 0), batch, lambda b: items(span(act, b)))

                    @block.vector
                    def _(dve):
                        loc = Local(dve, s_dve)
                        loc.tick(nc.vector.memset(ACC[:], 0.0))
                        loc.tick(nc.vector.memset(MR[:], -BIG))
                        loc.link(nc.vector.memset(FL[:, 0:1], -FAR))
                        dve.sem_inc(s_pair, PAIR_STEPS)
                        dve.sem_inc(s_item, 2)
                        dve.sem_inc(s_merged, BANKS)
                        one_hots(dve, O, 0, 0).then_inc(s_oh, 1)
                        one_hots(dve, O, 1, 1).then_inc(s_oh, 1)
                        loc.restart()

                        def pair(i):
                            w0 = i * 2
                            J, S = [], []
                            done = {}

                            def step(name, ins):
                                ins.then_inc(s_pair, 1)
                                done[name] = len(done) + 1

                            def after(name):
                                dve.wait_ge(s_pair, done[name])

                            def start(k):
                                step(f"gone{k}", nc.vector.tensor_scalar(gone[:, k:k + 1], S[k][:, GR + HEADS:NR], BIG, -BIG,
                                                                         ALU.mult, ALU.add))

                            def keep(k):
                                step(f"kept{k}", nc.vector.tensor_scalar(both[:, k, 0].unsqueeze(1), MR[:, J[k]], 0.0, None,
                                                                         ALU.add))

                            def item_max(k):
                                after(f"gone{k}")
                                step(f"of_item{k}", nc.vector.scalar_tensor_tensor(
                                    out=both[:, k, 1].unsqueeze(1), in0=S[k][:, GR:GR + HEADS].unsqueeze(1),
                                    scalar=gone[:, k:k + 1], in1=ADST[:, J[k], :], op0=ALU.add, op1=ALU.add))

                            def new_max(k):
                                after(f"kept{k}")
                                after(f"of_item{k}")
                                step(f"max{k}", nc.vector.tensor_tensor(MR[:, J[k]], both[:, k, 1].unsqueeze(1),
                                                                        both[:, k, 0].unsqueeze(1), ALU.max))

                            def differ(k):
                                after(f"max{k}")
                                nc.vector.tensor_tensor(df[:, k], both[:, k], MR[:, J[k]].to_broadcast([P, 2, HEADS]),
                                                        ALU.subtract).then_inc(s_diff, 1)

                            def scale_new(k):
                                dve.wait_ge(s_fac, w0 + k + 1)
                                step(f"new{k}", nc.vector.tensor_tensor(
                                    TM[:].rearrange("p (h c) -> p h c", c=HW),
                                    S[k][:, 0:GR].rearrange("p (h c) -> p h c", c=HW),
                                    fac[:, k, 1].unsqueeze(2).to_broadcast([P, HEADS, HW]), ALU.mult))

                            def scale_old(k):
                                acc = ACC[:, J[k], 0:GR].rearrange("p a (h c) -> p (a h) c", c=HW)
                                step(f"old{k}", nc.vector.tensor_tensor(
                                    acc, acc, fac[:, k, 0].unsqueeze(2).to_broadcast([P, HEADS, HW]), ALU.mult))

                            def merge(k):
                                after(f"new{k}")
                                dve.sem_inc(s_merged, 1)
                                after(f"old{k}")
                                acc = ACC[:, J[k], 0:GR]
                                step(f"merged{k}", nc.vector.tensor_tensor(acc, acc, TM[:].unsqueeze(1), ALU.add))

                            def blocks(k):
                                dve.wait_ge(s_item, w0 + k + 3)
                                nc.vector.scalar_tensor_tensor(
                                    out=O[:, k], in0=iota_n[:].unsqueeze(1).to_broadcast([P, Q, P]),
                                    scalar=tile_base[:, bass.ds(w0 + k + 2, 1)],
                                    in1=dstT[:, bass.ds(supers[k] * Q, Q)].unsqueeze(2).to_broadcast([P, Q, P]),
                                    op0=ALU.add, op1=ALU.is_equal).then_inc(s_oh, 1)

                            all_of = 2 * z.SRANGE * NT * NT
                            v = dve.value_load(packed[0:1, bass.ds(i, 1)], min_val=0, max_val=all_of - 1)
                            first = v // (NT * NT) % z.SRANGE
                            supers = [first, first + v // (NT * NT * z.SRANGE)]
                            blocks(0)
                            dve.wait_ge(s_pair, PAIR_STEPS)
                            dve.sem_clear(s_pair)
                            for k, tile in enumerate((v % NT, v // NT % NT)):
                                J.append(bass.ds(dve.snap(tile, min_val=0, max_val=NT - 1), 1))
                                S.append(pS[:, bass.ds(((w0 + k) % BANKS) * BANK, BANK)])
                            start(0)
                            keep(0)
                            item_max(0)
                            new_max(0)
                            differ(0)
                            blocks(1)
                            start(1)
                            keep(1)
                            scale_new(0)
                            item_max(1)
                            scale_old(0)
                            new_max(1)
                            differ(1)
                            merge(0)
                            after("merged0")
                            scale_new(1)
                            scale_old(1)
                            merge(1)
                            assert len(done) == PAIR_STEPS

                        def items(pairs_of_batch):
                            with dve.Fori(*pairs_of_batch) as i:
                                pair(i)

                        def scans(b, meanwhile=lambda: None):
                            dve.wait_ge(s_dr, b * 16 + 16)
                            dve.wait_ge(s_at, b + 1)
                            loc.tick(nc.vector.tensor_tensor_scan(M2[:], FL[:, 0:z.SE], pA[0:BR, :], -BIG, ALU.add, ALU.max))
                            got = meanwhile()
                            loc.settle()
                            loc.link(nc.vector.tensor_tensor_scan(M2[:, ::-1], FL[:, 1:z.SE + 1][:, ::-1], M2[:, ::-1], -BIG,
                                                                  ALU.add, ALU.max))
                            dve.sem_inc(s_max, 1)
                            loc.restart()
                            return got

                        def batch(b, k, i, before, ahead):
                            dve.wait_ge(s_mt, b + 1)
                            rows = G[:, k * BC:(k + 1) * BC, :]
                            pm = pM[:, 0:Q * BR].rearrange("p (q s h) -> p q s h", q=Q, h=HEADS)
                            last = lastT[:, bass.ds(b * BC, BC)]
                            loc.link(nc.vector.tensor_tensor(EX[:], SCO[:, k % 2], pm, ALU.subtract))
                            dve.sem_inc(s_sub, 1)
                            by_chunk = "p (s q) h -> p s q h"
                            loc.tick(nc.vector.tensor_tensor(
                                rows[:, :, GR:GR + HEADS].rearrange(by_chunk, q=Q),
                                pM[:, 0:Q * BR].rearrange("p (q s h) -> p s q h", q=Q, h=HEADS),
                                last.unsqueeze(2).to_broadcast([P, BC, HEADS]).rearrange(by_chunk, q=Q), ALU.mult))
                            loc.tick(nc.vector.tensor_scalar(rows[:, :, GR + HEADS], last, 0.0, None, ALU.add))
                            dve.wait_ge(s_exp, b + 1)
                            for s in range(z.BS):
                                c = rows[:, s * Q:(s + 1) * Q, 0:GR].rearrange("p q (h c) -> p q h c", c=HW)
                                loc.tick(nc.vector.tensor_tensor(
                                    c[:, :, :, 0:HC], c[:, :, :, 0:HC],
                                    c[:, :, :, HC:HW].to_broadcast([P, Q, HEADS, HC]), ALU.mult))
                            loc.settle()
                            dve.sem_inc(s_prep, 1)
                            loc.restart()
                            pairs_of = (lambda: span(dve, b - 1)) if before else (lambda: None)
                            pairs_before = scans(b + 1, pairs_of) if ahead else pairs_of()
                            if before:
                                items(pairs_before)
                        batches(dve, lambda: scans(0), batch, lambda b: items(span(dve, b)))

            FE = a["eb3"].shape[0]
            H1, H2, HS = a["eb1"].shape[0], a["eb2"].shape[0], a["sb1"].shape[1]
            G4 = late.enter_context(nc.sbuf_tensor("G4", [P, NT, FE], F32))
            with ExitStack() as ctx:
                sb, ps, sem = make(ctx)
                gW = sb("gW", [P, KD, FE])
                gb = sb("gb", [P, FE])
                RS = sb("RS", [P, NT, HEADS])
                T1 = sb("T1", [P, DEEP, D])
                IN = sb("IN10", [P, DEEP, D])
                HT = sb("HT10", [P, DEEP, D])
                SC = sb("SC10", [P, NT, FE])
                SC2 = sb("SC210", [P, NT, FE])
                eq = sb("eq10", [P, NT, FE])
                km = sb("km10", [P, NT])
                mx = sb("mx10", [P, 2, NT])
                sel = sb("sel10", [P, 2, NT, FE])
                pr = sb("pr10", [P, 2, NT])
                prio = sb("prio10", [P, FE])
                pT = [ps(f"pT10{i}", [P, 512]) for i in range(DEEP)]
                pG = [ps(f"pG10{i}", [P, 512]) for i in range(2)]
                s_w = sem("s_w10")
                s_const = sem("s_const10")
                s_t1 = sem("s_t110")
                s_x3 = sem("s_x310")
                s_stat = sem("s_stat10")
                s_var = sem("s_var10")
                s_root = sem("s_root10")
                s_in = sem("s_in10")
                s_turned = sem("s_turned10")
                s_ht = sem("s_ht10")
                s_kept = sem("s_kept10")
                s_sc = sem("s_sc10")
                s_sccp = sem("s_sccp10")
                s_held = sem("s_held10")
                s_e = sem("s_e10")
                s_ed = sem("s_ed10")
                s_dve = sem("s_dve10")
                with nc.Block() as block:
                    @block.sync
                    def _(sp):
                        sp.dma_start(gW[:], a["gW"].rearrange("(k p) n -> p k n", p=P)).then_inc(s_w, 16)
                        sp.dma_start(gb[:], a["gb"].unsqueeze(0).to_broadcast([P, FE])).then_inc(s_w, 16)

                    @block.gpsimd
                    def _(pool):
                        nc.gpsimd.iota(prio[:], pattern=[[-1, FE]], base=FE, channel_multiplier=0,
                                       allow_small_or_imprecise_dtypes=True).then_inc(s_const, 1)

                    @block.vector
                    def _(dve):
                        loc = Local(dve, s_dve)
                        sums = ACC[:, :, 0:GR].rearrange("p t (h c) -> p t h c", c=HW)
                        loc.link(nc.vector.tensor_scalar(RS[:], sums[:, :, :, HC], 1e-16, None, ALU.add))
                        loc.link(nc.vector.reciprocal(RS[:], RS[:]))
                        dve.sem_inc(s_x3, DEEP)
                        loc.restart()

                        def scale_tile(t, k):
                            one = bass.ds(t, 1)
                            dve.wait_ge(s_x3, t + 1)
                            acc = ACC[:, one, 0:GR].rearrange("p a (h c) -> p (a h) c", c=HW)[:, :, 0:HC]
                            nc.vector.tensor_tensor(T1[:, k].rearrange("p (h c) -> p h c", c=HC), acc,
                                                    RS[:, one, :].rearrange("p a h -> p (a h)").unsqueeze(2)
                                                    .to_broadcast([P, HEADS, HC]), ALU.mult).then_inc(s_t1, 1)

                        def add_tile(t, k):
                            one = bass.ds(t, 1)
                            dve.wait_ge(s_t1, t + 1)
                            nc.vector.tensor_tensor(X[:, one, :], X[:, one, :], T1[:, k].unsqueeze(1), ALU.add)\
                                .then_inc(s_x3, 1)
                        skewed(dve, scale_tile, add_tile, DEEP)
                        dve.wait_ge(s_x3, NT + DEEP)
                        all_stats(dve, s_stat)
                        dve.wait_ge(s_stat, NT)
                        ln_moments(loc, s_var)
                        ln_rstd(loc, s_root)
                        dve.sem_inc(s_turned, DEEP)
                        loc.restart()

                        def tile_in(t, k):
                            dve.wait_ge(s_turned, t + 1)
                            ln_apply(IN[:, k].unsqueeze(1), X[:, bass.ds(t, 1), :], bass.ds(t, 1)).then_inc(s_in, 1)
                        each_tile(dve, tile_in, DEEP)
                        wide = lambda v: v.unsqueeze(2).to_broadcast([P, NT, FE])
                        dve.wait_ge(s_sccp, NT + 2)
                        dve.wait_ge(s_const, 1)
                        dve.wait_ge(s_w, 32)
                        loc.link(nc.vector.tensor_tensor(SC[:], SC[:], gb[:].unsqueeze(1).to_broadcast([P, NT, FE]), ALU.add))
                        loc.link(nc.vector.tensor_reduce(km[:], SC[:], AX_X, ALU.max))
                        loc.link(nc.vector.tensor_tensor(SC[:], SC[:], wide(km[:]), ALU.subtract))
                        dve.sem_inc(s_e, 1)
                        dve.wait_ge(s_ed, 1)
                        loc.link(nc.vector.tensor_reduce(km[:], SC[:], AX_X, ALU.add))
                        loc.link(nc.vector.reciprocal(km[:], km[:]))
                        loc.link(nc.vector.tensor_tensor(SC[:], SC[:], wide(km[:]), ALU.mult))
                        top_two(loc, SC, SC2, mx, eq, km, sel, prio, FE)
                        loc.link(nc.vector.tensor_tensor(pr[:, 1], mx[:, 1], mx[:, 0], ALU.subtract))
                        dve.sem_inc(s_e, 1)
                        dve.wait_ge(s_ed, 2)
                        loc.link(nc.vector.tensor_scalar(pr[:, 0], pr[:, 1], 1.0, None, ALU.add))
                        loc.link(nc.vector.reciprocal(pr[:, 0], pr[:, 0]))
                        loc.link(nc.vector.tensor_tensor(pr[:, 1], pr[:, 1], pr[:, 0], ALU.mult))
                        loc.tick(nc.vector.tensor_tensor(G4[:], sel[:, 0], wide(pr[:, 0]), ALU.mult))
                        loc.link(nc.vector.tensor_tensor(eq[:], sel[:, 1], wide(pr[:, 1]), ALU.mult))
                        loc.link(nc.vector.tensor_tensor(G4[:], G4[:], eq[:], ALU.add))

                    @block.scalar
                    def _(act):
                        ln_root(act, s_var, s_root)
                        act.sem_inc(s_ht, DEEP)
                        act.sem_inc(s_kept, DEEP)
                        act.sem_inc(s_sc, DEEP)
                        act.sem_inc(s_sccp, 2)

                        def turned_in(t, k):
                            act.wait_ge(s_turned, t + 1 + DEEP)
                            act.wait_ge(s_sc, t + 1)
                            nc.scalar.activation(HT[:, k], pT[k][:, 0:D], ACT.Copy).then_inc(s_ht, 1)
                            act.sem_inc(s_held, 1)
                            nc.scalar.activation(ACC[:, bass.ds(t, 1), 0:D], pT[k][:, 0:D].unsqueeze(1), ACT.Copy)\
                                .then_inc(s_kept, 1)

                        def tile_out(t, k):
                            act.wait_ge(s_sc, t + 1 + DEEP)
                            act.sem_inc(s_held, 1)
                            nc.scalar.activation(SC[:, bass.ds(t, 1), :], pG[k % 2][:, 0:FE].unsqueeze(1), ACT.Copy)\
                                .then_inc(s_sccp, 1)
                        skewed(act, turned_in, tile_out, DEEP)
                        act.wait_ge(s_e, 1)
                        nc.scalar.activation(SC[:], SC[:], ACT.Exp).then_inc(s_ed, 1)
                        act.wait_ge(s_e, 2)
                        nc.scalar.activation(pr[:, 1], pr[:, 1], ACT.Exp).then_inc(s_ed, 1)

                    @block.tensor
                    def _(pe):
                        pe.wait_ge(s_w, 32)
                        pe.wait_ge(s_in, 1)

                        def turn(t, k):
                            pe.wait_ge(s_in, t + 1)
                            pe.wait_ge(s_kept, t + 1)
                            for m in range(KD):
                                tr = nc.tensor.transpose(pT[k][:, m * P:(m + 1) * P], IN[:, k, m * P:(m + 1) * P], ident[:])
                            tr.then_inc(s_turned, 1)

                        def gate(t, k):
                            pe.wait_ge(s_ht, t + 1 + DEEP)
                            pe.wait_ge(s_sccp, t + 1)
                            for m in range(KD):
                                mm = nc.tensor.matmul(pG[k % 2][:, 0:FE], HT[:, k, m * P:(m + 1) * P], gW[:, m, :],
                                                      start=(m == 0), stop=(m == KD - 1))
                            mm.then_inc(s_sc, 1)
                        skewed(pe, turn, gate, DEEP)
            if stop == 10:
                return dump(X)

            with ExitStack() as ctx:
                sb, ps, sem = make(ctx)
                NH, NE1 = HS, FE
                sW1 = sb("sW1", [P, KD, HS * P])
                sW2 = sb("sW2", [P, HS, P])
                sW3 = sb("sW3", [P, D])
                eW1 = sb("eW1", [P, KD, FE * H1])
                eW2 = sb("eW2", [P, FE, H2])
                eW3 = sb("eW3", [H2 + 1, FE, D])
                sb1 = sb("sb1", [P, HS])
                sb2 = sb("sb2", [P, 1])
                sb3 = sb("sb3", [P, D])
                eb1 = sb("eb1", [P, FE])
                eb2 = sb("eb2", [H2, FE])
                S1 = sb("S1", [P, HS, P])
                E1 = sb("E1", [P, FE, P])
                S2 = sb("S2", [P, P])
                E2 = sb("E2", [H2 + 1, FE, P])
                pS1 = ps("pS111", [P, HS, P])
                pE1 = ps("pE111", [P, FE, P])
                pS2 = ps("pS211", [P, 512])
                pE2 = ps("pE211", [P, FE, P])
                pSo = ps("pSo11", [P, 512])
                pEo = [ps(f"pEo11{i}", [P, 2, D]) for i in range(2)]
                s_w = sem("s_w11")
                s_row = sem("s_row11")
                s_biased = sem("s_biased11")
                s_l1 = sem("s_l111")
                s_r1 = sem("s_r111")
                s_l2 = sem("s_l211")
                s_r2 = sem("s_r211")
                s_l3 = sem("s_l311")
                s_add = sem("s_add11")
                s_store = sem("s_store11")
                assert H1 == P and FE == 4
                with nc.Block() as block:
                    @block.sync
                    def _(sp):
                        loads = [(sW1[:], a["sW1"].rearrange("(k p) n -> p k n", p=P)),
                                 (sW2[:], a["sW2"].rearrange("(k p) n -> p k n", p=P)), (sW3[:], a["sW3"]),
                                 (eW1[:], a["eW1"].rearrange("(k p) n -> p k n", p=P)),
                                 (eW2[:], a["eW2"].rearrange("p (e n) -> p e n", e=FE)),
                                 (eW3[0:H2], a["eW3"].rearrange("p (e n) -> p e n", e=FE)),
                                 (sb1[:], a["sb1"]), (sb2[:], a["sb2"]), (sb3[:], a["sb3"].unsqueeze(0).to_broadcast([P, D])),
                                 (eb1[:], a["eb1"]), (eb2[:], a["eb2"]), (eW3[H2:H2 + 1], a["eb3"].unsqueeze(0))]
                        for o_, i_ in loads:
                            sp.dma_start(o_, i_).then_inc(s_w, 16)
                        with sp.Fori(0, FULL) as t:
                            sp.wait_ge(s_add, (t + 1) * (FE + 1) + 1)
                            sp.dma_start(out[bass.ds(t * P, P), :], X[:, bass.ds(t, 1), :].rearrange("p a d -> p (a d)"))\
                                .then_inc(s_store, 16)
                        sp.wait_ge(s_add, NT * (FE + 1) + 1)
                        sp.dma_start(out[FULL * P:N, :], X[0:REST, FULL, :]).then_inc(s_store, 16)
                        sp.wait_ge(s_store, 16 * NT)

                    @block.tensor
                    def _(pe):
                        pe.wait_ge(s_w, 16 * 12)
                        pe.wait_ge(s_row, 1)

                        def tile(t):
                            h = lambda m: ACC[:, bass.ds(t, 1), m * P:(m + 1) * P].rearrange("p a d -> p (a d)")
                            pe.wait_ge(s_r1, t * (HS + FE) + 1)
                            for b in range(HS):
                                for m in range(KD):
                                    mm = nc.tensor.matmul(pS1[:, b, :], sW1[:, m, b * P:(b + 1) * P], h(m),
                                                          start=(m == 0), stop=(m == KD - 1))
                                mm.then_inc(s_l1, 1)
                            for e in range(FE):
                                for m in range(KD):
                                    mm = nc.tensor.matmul(pE1[:, e, :], eW1[:, m, e * P:(e + 1) * P], h(m),
                                                          start=(m == 0), stop=(m == KD - 1))
                                mm.then_inc(s_l1, 1)
                            pe.wait_ge(s_r2, t * (1 + FE) + 1)
                            pe.wait_ge(s_r1, t * (HS + FE) + 1 + HS)
                            for b in range(HS):
                                mm = nc.tensor.matmul(pS2[:, 0:P], sW2[:, b, :], S1[:, b, :],
                                                      start=(b == 0), stop=(b == HS - 1))
                            mm.then_inc(s_l2, 1)
                            for e in range(FE):
                                pe.wait_ge(s_r1, t * (HS + FE) + 1 + HS + e + 1)
                                nc.tensor.matmul(pE2[0:H2, e, :], eW2[:, e, :], E1[:, e, :], start=True, stop=True)\
                                    .then_inc(s_l2, 1)
                            pe.wait_ge(s_add, t * (FE + 1) + 1)
                            pe.wait_ge(s_r2, t * (1 + FE) + 2)
                            nc.tensor.matmul(pSo[:, 0:D], S2[:], sW3[:], start=True, stop=True).then_inc(s_l3, 1)
                            for e in range(FE):
                                pe.wait_ge(s_r2, t * (1 + FE) + 3 + e)
                                nc.tensor.matmul(pEo[e // 2][:, e % 2, :], E2[:, e, :], eW3[:, e, :], start=True, stop=True)\
                                    .then_inc(s_l3, 1)
                        with pe.Fori(0, NT) as t:
                            tile(t)

                    @block.scalar
                    def _(act):
                        act.sem_inc(s_r1, 1)
                        act.sem_inc(s_r2, 1)
                        act.wait_ge(s_w, 16 * 12)
                        with act.Fori(0, NT) as t:
                            for b in range(HS + FE):
                                if b in (0, HS):
                                    act.wait_ge(s_l1, t * (HS + FE) + (HS if b == 0 else HS + FE))
                                o_, i_, bi = ((S1[:, b], pS1[:, b], sb1[:, b:b + 1]) if b < HS else
                                              (E1[:, b - HS], pE1[:, b - HS], eb1[:, b - HS:b - HS + 1]))
                                nc.scalar.activation(o_, i_, ACT.Relu, bias=bi).then_inc(s_r1, 1)
                            for e in range(-1, FE):
                                if e < 1:
                                    act.wait_ge(s_l2, t * (1 + FE) + (1 if e < 0 else 1 + FE))
                                o_, i_, bi = ((S2[:], pS2[:, 0:P], sb2[:, 0:1]) if e < 0 else
                                              (E2[0:H2, e], pE2[0:H2, e], eb2[:, e:e + 1]))
                                nc.scalar.activation(o_, i_, ACT.Relu, bias=bi).then_inc(s_r2, 1)

                    @block.vector
                    def _(dve):
                        nc.vector.memset(E2[H2:H2 + 1], 1.0).then_inc(s_row, 1)
                        dve.sem_inc(s_add, 1)
                        dve.wait_ge(s_w, 16 * 12)
                        with dve.Fori(0, NT) as t:
                            one = bass.ds(t, 1)
                            nc.vector.tensor_tensor(X[:, one, :], X[:, one, :], sb3[:].unsqueeze(1), ALU.add)\
                                .then_inc(s_biased, 1)
                            dve.wait_ge(s_biased, t + 1)
                            dve.wait_ge(s_l3, t * (FE + 1) + 1)
                            nc.vector.tensor_tensor(X[:, one, :], X[:, one, :], pSo[:, 0:D].unsqueeze(1), ALU.add)\
                                .then_inc(s_add, 1)
                            for e in range(FE):
                                if e % 2 == 0:
                                    dve.wait_ge(s_l3, t * (FE + 1) + 3 + e)
                                dve.wait_ge(s_add, t * (FE + 1) + 2 + e)
                                nc.vector.scalar_tensor_tensor(
                                    out=X[:, one, :], in0=pEo[e // 2][:, e % 2, :].unsqueeze(1), scalar=G4[:, one, e],
                                    in1=X[:, one, :], op0=ALU.mult, op1=ALU.add).then_inc(s_add, 1)


def kernel(**inputs):
    import numpy as _np
    import concourse.bacc as _bacc
    from concourse import mybir as _mybir
    from concourse.bass_utils import run_bass_kernel_spmd as _run

    nc = _bacc.Bacc("TRN2", target_bir_lowering=False, num_devices=1)
    a = {k: _np.asarray(v) for k, v in inputs.items()}
    ne, hid, d = a["L0_ffn_W1"].shape
    heads, hc = a["L1_gnn_a_src"].shape
    z = Sizes(a["x"].shape[0], a["x"].shape[1], a["src"].shape[0], ne, hid, heads)
    t_ = lambda v, *axes: _np.transpose(v, axes)
    blocks = lambda v: t_(v.reshape(ne, -1, P, v.shape[-1]), 0, 2, 1, 3).reshape(ne, P, -1)
    laid = {
        "x": a["x"], "src": a["src"], "dst": a["dst"],
        "W0": a["L0_gnn_W"], "b0": a["L0_gnn_b"],
        "WgT": a["L0_ffn_Wg"].T, "bg": a["L0_ffn_bg"],
        "W1": blocks(t_(a["L0_ffn_W1"], 0, 2, 1)),
        "b1": t_(a["L0_ffn_b1"].reshape(ne, hid // P, P), 0, 2, 1),
        "W2": blocks(t_(a["L0_ffn_W2"], 0, 2, 1)),
        "b2": a["L0_ffn_b2"],
        "Wp": a["L1_gnn_W"], "WpT": a["L1_gnn_W"].T,
        "att": _np.stack([a["L1_gnn_a_src"].reshape(-1), a["L1_gnn_a_dst"].reshape(-1)], 1),
        "sW1": a["L1_ffn_sW1"], "sb1": a["L1_ffn_sb1"].reshape(-1, P).T,
        "sW2": a["L1_ffn_sW2"], "sb2": a["L1_ffn_sb2"].reshape(-1, P).T,
        "sW3": a["L1_ffn_sW3"], "sb3": a["L1_ffn_sb3"],
        "eW1": t_(a["L1_ffn_eW1"], 1, 0, 2).reshape(d, -1), "eb1": a["L1_ffn_eb1"].T,
        "eW2": t_(a["L1_ffn_eW2"], 1, 0, 2).reshape(P, -1), "eb2": a["L1_ffn_eb2"].T,
        "eW3": t_(a["L1_ffn_eW3"], 1, 0, 2).reshape(a["L1_ffn_eW3"].shape[1], -1), "eb3": a["L1_ffn_eb3"],
        "gW": a["L1_ffn_gW"], "gb": a["L1_ffn_gb"],
    }
    arrays, aps = {}, {}
    for name, v in laid.items():
        v = _np.ascontiguousarray(v)
        arrays[f"in_{name}_dram"] = v
        aps[name] = nc.dram_tensor(f"in_{name}_dram", v.shape, _mybir.dt.from_np(v.dtype), kind="ExternalInput").ap()
    out = nc.dram_tensor("out_0_dram", a["x"].shape, F32, kind="ExternalOutput").ap()
    build(nc, STOP, z, aps, out)
    r = _run(nc, [arrays], core_ids=[0])
    return r.results[0]["out_0_dram"]
```
